# Optimizing a Trainium2 kernel written in Bass

```python
import numpy as np
import jax
import jax.numpy as jnp

def _softmax(x, axis=-1):
    return jax.nn.softmax(x, axis=axis)

def _gelu(x):
    return jax.nn.gelu(x, approximate=True)

def _silu(x):
    return jax.nn.silu(x)

def _sigmoid(x):
    return jax.nn.sigmoid(x)

def _layernorm(x, axis=-1, eps=1e-05):
    m = jnp.mean(x, axis=axis, keepdims=True)
    v = jnp.var(x, axis=axis, keepdims=True)
    return (x - m) / jnp.sqrt(v + eps)

def _scatter_add(tgt, idx, src, axis=0):
    return tgt.at[idx].add(src)

def _segment_sum(src, seg, n):
    return jax.ops.segment_sum(src, seg, n)
kernel_name = 'mk_recurrent_d2_jaxref_r8_6fe09d'

def setup_inputs(seed: int=0):
    np.random.seed(seed)
    _w = jnp.asarray

    def _L0_attn_setup():
        import jax, jax.numpy as jnp
        import numpy as np
        N_EMBD = 256
        EXPAND = 2
        D_INNER = N_EMBD * EXPAND
        D_STATE = 128
        N_HEADS = D_INNER // D_STATE
        HEAD_DIM = D_INNER // N_HEADS
        N_GROUPS = 1
        D_CONV = 4
        CHUNK = 64
        N_LAYERS = 48
        GS = N_GROUPS * D_STATE
        PROJ = 2 * D_INNER + N_HEADS + 2 * GS
        RMS_EPS = 1e-06

        def _ssd_scan(A, B, C, dt, x, chunk_size=CHUNK):
            batch, seq_len, n_heads, P = x.shape
            G, N = (B.shape[2], B.shape[3])
            Hg = n_heads // G
            Q = chunk_size
            pad_len = -seq_len % Q
            if pad_len:
                A = jnp.pad(A, ((0, 0), (0, pad_len), (0, 0)))
                B = jnp.pad(B, ((0, 0), (0, pad_len), (0, 0), (0, 0)))
                C = jnp.pad(C, ((0, 0), (0, pad_len), (0, 0), (0, 0)))
                dt = jnp.pad(dt, ((0, 0), (0, pad_len), (0, 0)))
                x = jnp.pad(x, ((0, 0), (0, pad_len), (0, 0), (0, 0)))
            T_pad = seq_len + pad_len
            n_chunks = T_pad // Q
            A_c = A.reshape(batch, n_chunks, Q, n_heads)
            B_c = B.reshape(batch, n_chunks, Q, G, N)
            C_c = C.reshape(batch, n_chunks, Q, G, N)
            dt_c = dt.reshape(batch, n_chunks, Q, n_heads)
            x_c = x.reshape(batch, n_chunks, Q, n_heads, P)
            log_a = A_c * dt_c
            cum_log_a = jnp.cumsum(log_a, axis=2)
            chunk_log_decay = cum_log_a[:, :, -1, :]
            log_diff = cum_log_a[:, :, :, None, :] - cum_log_a[:, :, None, :, :]
            causal = jnp.tril(jnp.ones((Q, Q), dtype=jnp.bool_))[None, None, :, :, None]
            L = jnp.exp(jnp.where(causal, log_diff, -jnp.inf))
            CB = jnp.einsum('bcign,bcjgn->bcijg', C_c, B_c)
            L_rs = L.reshape(batch, n_chunks, Q, Q, G, Hg)
            dt_rs = dt_c.reshape(batch, n_chunks, Q, G, Hg)
            x_rs = x_c.reshape(batch, n_chunks, Q, G, Hg, P)
            y_intra = jnp.einsum('bcijGH,bcijG,bcjGH,bcjGHp->bciGHp', L_rs, CB, dt_rs, x_rs)
            decay_to_end = jnp.exp(chunk_log_decay[:, :, None, :] - cum_log_a)
            decay_to_end_rs = decay_to_end.reshape(batch, n_chunks, Q, G, Hg)
            state_local = jnp.einsum('bcjGH,bcjGH,bcjGn,bcjGHp->bcGHnp', decay_to_end_rs, dt_rs, B_c, x_rs)
            chunk_decay = jnp.exp(chunk_log_decay).reshape(batch, n_chunks, G, Hg)

            def scan_op(left, right):
                d_l, s_l = left
                d_r, s_r = right
                return (d_l * d_r, d_r[..., None, None] * s_l + s_r)
            _, state_at_end = jax.lax.associative_scan(scan_op, (chunk_decay, state_local), axis=1)
            state_at_start = jnp.concatenate([jnp.zeros_like(state_at_end[:, :1]), state_at_end[:, :-1]], axis=1)
            decay_from_start = jnp.exp(cum_log_a).reshape(batch, n_chunks, Q, G, Hg)
            y_inter = jnp.einsum('bciGH,bciGn,bcGHnp->bciGHp', decay_from_start, C_c, state_at_start)
            y = (y_intra + y_inter).reshape(batch, T_pad, n_heads, P)
            if pad_len:
                y = y[:, :seq_len]
            return y
        key = jax.random.key(seed)
        ks = jax.random.split(key, 6)
        Bsz, T = (2, 256)
        x = jax.random.normal(ks[0], (Bsz, T, N_EMBD), jnp.float32)
        norm_scale = jnp.ones((N_EMBD,), jnp.float32)
        in_proj_w = 0.02 * jax.random.normal(ks[1], (N_EMBD, PROJ), jnp.float32)
        conv_weight = 0.02 * jax.random.normal(ks[2], (D_CONV, D_INNER), jnp.float32)
        conv_bias = jnp.zeros((D_INNER,), jnp.float32)
        A_log = jnp.log(jnp.arange(1, N_HEADS + 1, dtype=jnp.float32))
        dt_bias = 0.1 * jax.random.normal(ks[3], (N_HEADS,), jnp.float32)
        D = jnp.ones((D_INNER,), jnp.float32)
        out_proj_w = 0.02 / np.sqrt(2 * N_LAYERS) * jax.random.normal(ks[4], (D_INNER, N_EMBD), jnp.float32)
        return dict(x=x, norm_scale=norm_scale, in_proj_w=in_proj_w, conv_weight=conv_weight, conv_bias=conv_bias, A_log=A_log, dt_bias=dt_bias, D=D, out_proj_w=out_proj_w)
    _L0_attn_in = _L0_attn_setup()

    def _L0_ffn_setup():
        import jax, jax.numpy as jnp
        import numpy as np
        B, T, C = (2, 256, 256)
        E = 8
        K = 2
        I = 704
        key = jax.random.key(seed)
        ks = jax.random.split(key, 5)
        s_in = 1.0 / np.sqrt(C)
        s_mid = 1.0 / np.sqrt(I)
        return {'x': jax.random.normal(ks[0], (B, T, C), dtype=jnp.float32), 'gate_w': jax.random.normal(ks[1], (E, C), dtype=jnp.float32) * s_in, 'fc1_w': jax.random.normal(ks[2], (E, I, C), dtype=jnp.float32) * s_in, 'fc2_w': jax.random.normal(ks[3], (E, I, C), dtype=jnp.float32) * s_in, 'proj_w': jax.random.normal(ks[4], (E, C, I), dtype=jnp.float32) * s_mid}
    _L0_ffn_in = _L0_ffn_setup()

    def _L1_attn_setup():
        import jax, jax.numpy as jnp
        import numpy as np
        B, S, HID = (1, 256, 256)
        H, KVH, HD = (32, 8, 64)
        THETA = 10000.0

        def _rotate_half(x):
            x1, x2 = jnp.split(x, 2, axis=-1)
            return jnp.concatenate([-x2, x1], axis=-1)

        def _rope_cos_sin(seq_len, head_dim, theta, dtype):
            inv_freq = 1.0 / theta ** (jnp.arange(0, head_dim, 2, dtype=jnp.float32) / head_dim)
            pos = jnp.arange(seq_len, dtype=jnp.float32)
            freqs = pos[:, None] * inv_freq[None, :]
            emb = jnp.concatenate([freqs, freqs], axis=-1)
            return (jnp.cos(emb).astype(dtype), jnp.sin(emb).astype(dtype))
        key = jax.random.key(seed)
        k0, k1, k2, k3, k4 = jax.random.split(key, 5)
        w = lambda k, shape: jax.random.normal(k, shape, dtype=jnp.float32) * 0.02
        return {'hidden_states': jax.random.normal(k0, (B, S, HID), dtype=jnp.float32), 'Wq': w(k1, (H * HD, HID)), 'Wk': w(k2, (KVH * HD, HID)), 'Wv': w(k3, (KVH * HD, HID)), 'Wo': w(k4, (HID, H * HD))}
    _L1_attn_in = _L1_attn_setup()

    def _L1_ffn_setup():
        import jax, jax.numpy as jnp
        import numpy as np
        D_IN = 256
        D_OUT = 256
        LN_EPS = 1e-05
        key = jax.random.key(seed)
        kx, kw, kb = jax.random.split(key, 3)
        x = jax.random.normal(kx, (8, 256, D_IN), dtype=jnp.float32)
        gamma = jnp.ones((D_IN,), dtype=jnp.float32)
        beta = jnp.zeros((D_IN,), dtype=jnp.float32)
        weight = jax.random.uniform(kw, (D_OUT, D_IN), dtype=jnp.float32) * 0.001
        bias = jax.random.uniform(kb, (D_OUT,), dtype=jnp.float32) * 0.001
        alpha = jnp.ones((D_OUT,), dtype=jnp.float32)
        return {'x': x, 'gamma': gamma, 'beta': beta, 'weight': weight, 'bias': bias, 'alpha': alpha}
    _L1_ffn_in = _L1_ffn_setup()
    _d = {'L0_attn_x': _L0_attn_in['x'], 'L0_attn_norm_scale': _L0_attn_in['norm_scale'], 'L0_attn_in_proj_w': _L0_attn_in['in_proj_w'], 'L0_attn_conv_weight': _L0_attn_in['conv_weight'], 'L0_attn_conv_bias': _L0_attn_in['conv_bias'], 'L0_attn_A_log': _L0_attn_in['A_log'], 'L0_attn_dt_bias': _L0_attn_in['dt_bias'], 'L0_attn_D': _L0_attn_in['D'], 'L0_attn_out_proj_w': _L0_attn_in['out_proj_w'], 'L0_ffn_gate_w': _L0_ffn_in['gate_w'], 'L0_ffn_fc1_w': _L0_ffn_in['fc1_w'], 'L0_ffn_fc2_w': _L0_ffn_in['fc2_w'], 'L0_ffn_proj_w': _L0_ffn_in['proj_w'], 'L1_attn_Wq': _L1_attn_in['Wq'], 'L1_attn_Wk': _L1_attn_in['Wk'], 'L1_attn_Wv': _L1_attn_in['Wv'], 'L1_attn_Wo': _L1_attn_in['Wo'], 'L1_ffn_gamma': _L1_ffn_in['gamma'], 'L1_ffn_beta': _L1_ffn_in['beta'], 'L1_ffn_weight': _L1_ffn_in['weight'], 'L1_ffn_bias': _L1_ffn_in['bias'], 'L1_ffn_alpha': _L1_ffn_in['alpha']}
    _x0 = _d['L0_attn_x']
    _d['L0_attn_x'] = jax.random.normal(jax.random.fold_in(jax.random.key(seed), 1), (2, 512, 256), dtype=_x0.dtype)
    del _x0
    return _d

def reference(L0_attn_x, L0_attn_norm_scale, L0_attn_in_proj_w, L0_attn_conv_weight, L0_attn_conv_bias, L0_attn_A_log, L0_attn_dt_bias, L0_attn_D, L0_attn_out_proj_w, L0_ffn_gate_w, L0_ffn_fc1_w, L0_ffn_fc2_w, L0_ffn_proj_w, L1_attn_Wq, L1_attn_Wk, L1_attn_Wv, L1_attn_Wo, L1_ffn_gamma, L1_ffn_beta, L1_ffn_weight, L1_ffn_bias, L1_ffn_alpha):

    def _L0_attn_ref(x, norm_scale, in_proj_w, conv_weight, conv_bias, A_log, dt_bias, D, out_proj_w):
        import jax, jax.numpy as jnp
        import numpy as np
        N_EMBD = 256
        EXPAND = 2
        D_INNER = N_EMBD * EXPAND
        D_STATE = 128
        N_HEADS = D_INNER // D_STATE
        HEAD_DIM = D_INNER // N_HEADS
        N_GROUPS = 1
        D_CONV = 4
        CHUNK = 64
        N_LAYERS = 48
        GS = N_GROUPS * D_STATE
        PROJ = 2 * D_INNER + N_HEADS + 2 * GS
        RMS_EPS = 1e-06

        def _ssd_scan(A, B, C, dt, x, chunk_size=CHUNK):
            batch, seq_len, n_heads, P = x.shape
            G, N = (B.shape[2], B.shape[3])
            Hg = n_heads // G
            Q = chunk_size
            pad_len = -seq_len % Q
            if pad_len:
                A = jnp.pad(A, ((0, 0), (0, pad_len), (0, 0)))
                B = jnp.pad(B, ((0, 0), (0, pad_len), (0, 0), (0, 0)))
                C = jnp.pad(C, ((0, 0), (0, pad_len), (0, 0), (0, 0)))
                dt = jnp.pad(dt, ((0, 0), (0, pad_len), (0, 0)))
                x = jnp.pad(x, ((0, 0), (0, pad_len), (0, 0), (0, 0)))
            T_pad = seq_len + pad_len
            n_chunks = T_pad // Q
            A_c = A.reshape(batch, n_chunks, Q, n_heads)
            B_c = B.reshape(batch, n_chunks, Q, G, N)
            C_c = C.reshape(batch, n_chunks, Q, G, N)
            dt_c = dt.reshape(batch, n_chunks, Q, n_heads)
            x_c = x.reshape(batch, n_chunks, Q, n_heads, P)
            log_a = A_c * dt_c
            cum_log_a = jnp.cumsum(log_a, axis=2)
            chunk_log_decay = cum_log_a[:, :, -1, :]
            log_diff = cum_log_a[:, :, :, None, :] - cum_log_a[:, :, None, :, :]
            causal = jnp.tril(jnp.ones((Q, Q), dtype=jnp.bool_))[None, None, :, :, None]
            L = jnp.exp(jnp.where(causal, log_diff, -jnp.inf))
            CB = jnp.einsum('bcign,bcjgn->bcijg', C_c, B_c)
            L_rs = L.reshape(batch, n_chunks, Q, Q, G, Hg)
            dt_rs = dt_c.reshape(batch, n_chunks, Q, G, Hg)
            x_rs = x_c.reshape(batch, n_chunks, Q, G, Hg, P)
            y_intra = jnp.einsum('bcijGH,bcijG,bcjGH,bcjGHp->bciGHp', L_rs, CB, dt_rs, x_rs)
            decay_to_end = jnp.exp(chunk_log_decay[:, :, None, :] - cum_log_a)
            decay_to_end_rs = decay_to_end.reshape(batch, n_chunks, Q, G, Hg)
            state_local = jnp.einsum('bcjGH,bcjGH,bcjGn,bcjGHp->bcGHnp', decay_to_end_rs, dt_rs, B_c, x_rs)
            chunk_decay = jnp.exp(chunk_log_decay).reshape(batch, n_chunks, G, Hg)

            def scan_op(left, right):
                d_l, s_l = left
                d_r, s_r = right
                return (d_l * d_r, d_r[..., None, None] * s_l + s_r)
            _, state_at_end = jax.lax.associative_scan(scan_op, (chunk_decay, state_local), axis=1)
            state_at_start = jnp.concatenate([jnp.zeros_like(state_at_end[:, :1]), state_at_end[:, :-1]], axis=1)
            decay_from_start = jnp.exp(cum_log_a).reshape(batch, n_chunks, Q, G, Hg)
            y_inter = jnp.einsum('bciGH,bciGn,bcGHnp->bciGHp', decay_from_start, C_c, state_at_start)
            y = (y_intra + y_inter).reshape(batch, T_pad, n_heads, P)
            if pad_len:
                y = y[:, :seq_len]
            return y
        residual = x
        b, t = (x.shape[0], x.shape[1])
        h = x * jax.lax.rsqrt(jnp.mean(x * x, axis=-1, keepdims=True) + RMS_EPS) * norm_scale
        proj = h @ in_proj_w
        gate = proj[..., :D_INNER]
        ssm_in = proj[..., D_INNER:2 * D_INNER]
        dt_raw = proj[..., 2 * D_INNER:2 * D_INNER + N_HEADS]
        Bm = proj[..., 2 * D_INNER + N_HEADS:2 * D_INNER + N_HEADS + GS].reshape(b, t, N_GROUPS, D_STATE)
        Cm = proj[..., 2 * D_INNER + N_HEADS + GS:].reshape(b, t, N_GROUPS, D_STATE)
        xp = jnp.pad(ssm_in, ((0, 0), (D_CONV - 1, 0), (0, 0)))
        w_t = conv_weight.T[:, None, :]
        y = jax.lax.conv_general_dilated(jnp.transpose(xp, (0, 2, 1)), w_t, window_strides=(1,), padding='VALID', feature_group_count=D_INNER)
        ssm_in = jnp.transpose(y, (0, 2, 1)) + conv_bias
        ssm_in = jax.nn.silu(ssm_in)
        dt = jax.nn.softplus(dt_raw + dt_bias)
        A = -jnp.exp(A_log)
        A_f = jnp.broadcast_to(A[None, None, :], (b, t, N_HEADS))
        x_h = ssm_in.reshape(b, t, N_HEADS, HEAD_DIM)
        y_ssd = _ssd_scan(A_f, Bm, Cm, dt, x_h).reshape(b, t, D_INNER)
        y_ssd = y_ssd + D * ssm_in
        y_ssd = y_ssd * jax.nn.silu(gate)
        return residual + y_ssd @ out_proj_w

    def _L0_ffn_ref(x, gate_w, fc1_w, fc2_w, proj_w):
        import jax, jax.numpy as jnp
        import numpy as np
        B, T, C = (2, 256, 256)
        E = 8
        K = 2
        I = 704
        b, t, c = x.shape
        xt = x.reshape(-1, c)
        router = xt @ gate_w.T
        probs, idx = jax.lax.top_k(router, K)
        probs = jax.nn.softmax(probs.astype(jnp.float32), axis=-1).astype(x.dtype)
        onehot = jax.nn.one_hot(idx, E, dtype=x.dtype)
        comb = jnp.einsum('nk,nke->ne', probs, onehot)
        y = jnp.zeros_like(xt)
        for e in range(E):
            h = jax.nn.silu(xt @ fc1_w[e].T) * (xt @ fc2_w[e].T)
            y = y + comb[:, e:e + 1] * (h @ proj_w[e].T)
        return y.reshape(b, t, c)

    def _L1_attn_ref(hidden_states, Wq, Wk, Wv, Wo):
        import jax, jax.numpy as jnp
        import numpy as np
        B, S, HID = (1, 256, 256)
        H, KVH, HD = (32, 8, 64)
        THETA = 10000.0

        def _rotate_half(x):
            x1, x2 = jnp.split(x, 2, axis=-1)
            return jnp.concatenate([-x2, x1], axis=-1)

        def _rope_cos_sin(seq_len, head_dim, theta, dtype):
            inv_freq = 1.0 / theta ** (jnp.arange(0, head_dim, 2, dtype=jnp.float32) / head_dim)
            pos = jnp.arange(seq_len, dtype=jnp.float32)
            freqs = pos[:, None] * inv_freq[None, :]
            emb = jnp.concatenate([freqs, freqs], axis=-1)
            return (jnp.cos(emb).astype(dtype), jnp.sin(emb).astype(dtype))
        b, s, _ = hidden_states.shape
        dtype = hidden_states.dtype
        q = (hidden_states @ Wq.T).reshape(b, s, H, HD).transpose(0, 2, 1, 3)
        k = (hidden_states @ Wk.T).reshape(b, s, KVH, HD).transpose(0, 2, 1, 3)
        v = (hidden_states @ Wv.T).reshape(b, s, KVH, HD).transpose(0, 2, 1, 3)
        cos, sin = _rope_cos_sin(s, HD, THETA, dtype)
        apply_rope = lambda x: x * cos + _rotate_half(x) * sin
        q = apply_rope(q)
        k = apply_rope(k)
        groups = H // KVH
        k = jnp.repeat(k, groups, axis=1)
        v = jnp.repeat(v, groups, axis=1)
        scale = 1.0 / jnp.sqrt(jnp.asarray(HD, dtype=dtype))
        logits = jnp.einsum('bhqd,bhkd->bhqk', q, k) * scale
        causal = jnp.tril(jnp.ones((s, s), dtype=bool))
        logits = jnp.where(causal, logits, jnp.finfo(dtype).min)
        attn = jax.nn.softmax(logits, axis=-1)
        out = jnp.einsum('bhqk,bhkd->bhqd', attn, v)
        out = out.transpose(0, 2, 1, 3).reshape(b, s, H * HD)
        return out @ Wo.T

    def _L1_ffn_ref(x, gamma, beta, weight, bias, alpha):
        import jax, jax.numpy as jnp
        import numpy as np
        D_IN = 256
        D_OUT = 256
        LN_EPS = 1e-05
        mu = jnp.mean(x, axis=-1, keepdims=True)
        var = jnp.mean(jnp.square(x - mu), axis=-1, keepdims=True)
        xn = (x - mu) * jax.lax.rsqrt(var + LN_EPS) * gamma + beta
        a = jnp.sign(xn)
        centered = weight - jnp.mean(weight, axis=1, keepdims=True)
        signed_w = jnp.sign(centered)
        out = jnp.einsum('bsi,oi->bso', a, signed_w) + bias
        return out * alpha
    x = L0_attn_x
    xn = _layernorm(x, axis=-1)
    s = _L0_attn_ref(xn, L0_attn_norm_scale, L0_attn_in_proj_w, L0_attn_conv_weight, L0_attn_conv_bias, L0_attn_A_log, L0_attn_dt_bias, L0_attn_D, L0_attn_out_proj_w)
    g = _silu(_L0_ffn_ref(xn, L0_ffn_gate_w, L0_ffn_fc1_w, L0_ffn_fc2_w, L0_ffn_proj_w))
    x = x + s * g
    xn = _layernorm(x, axis=-1)
    s = _L1_attn_ref(xn, L1_attn_Wq, L1_attn_Wk, L1_attn_Wv, L1_attn_Wo)
    g = _silu(_L1_ffn_ref(xn, L1_ffn_gamma, L1_ffn_beta, L1_ffn_weight, L1_ffn_bias, L1_ffn_alpha))
    x = x + s * g
    return x

_drawn_inputs = setup_inputs


def setup_inputs(seed=0):
    import zlib

    import numpy as np

    out = dict(_drawn_inputs(seed))
    spreads = {'L0_attn_norm_scale': (1.0, 0.6),
     'L0_attn_conv_bias': (0.0, 0.8),
     'L0_attn_D': (1.0, 0.6),
     'L1_ffn_gamma': (1.0, 0.6),
     'L1_ffn_beta': (0.0, 0.8),
     'L1_ffn_alpha': (1.0, 0.6)}
    factors = {'L0_attn_in_proj_w': 8.0,
     'L0_attn_conv_weight': 8.0,
     'L0_attn_A_log': 8.0,
     'L0_attn_dt_bias': 8.0,
     'L0_attn_out_proj_w': 8.0,
     'L1_ffn_bias': 64.0,
     'L1_attn_Wq': 8.0,
     'L1_attn_Wk': 8.0,
     'L1_attn_Wv': 8.0,
     'L1_attn_Wo': 8.0,
     'L1_ffn_weight': 8.0}
    for name, (base, spread) in spreads.items():
        noise = np.random.default_rng([zlib.crc32(name.encode()), seed]).standard_normal(out[name].shape)
        drawn = base * np.exp(spread * noise) if base else spread * noise
        out[name] = jnp.asarray(drawn.astype(out[name].dtype))
    for name, factor in factors.items():
        out[name] = (out[name] * factor).astype(out[name].dtype)
    return out
```

```python
import concourse.bass as bass
from concourse import mybir
from contextlib import ExitStack

F32 = mybir.dt.float32
F32R = mybir.dt.float32r
BF16 = mybir.dt.bfloat16
U32 = mybir.dt.uint32

P = 128
BATCH, SEQ, C = 2, 512, 256
T = BATCH * SEQ
NT = T // P
TB = SEQ // P
KC = C // P
HALF = SEQ
DI, NH = 512, 4
NCH = DI // P
PROJ = 2 * DI + NH + 2 * P
DT0 = 2 * DI
B0, C0 = DT0 + NH, DT0 + NH + P
TAPS = 4
E, I = 8, 704
FULL = I // P
TAIL = I - FULL * P
NTAIL = E * TAIL // P
WM = 3 * C
FC2, PJ = C, 2 * C
H, KVH, HD = 32, 8, 64
GQ = H // KVH
GW = GQ * HD + 2 * HD
NR = GQ + 1
PAIRS = BATCH * GQ // 2
NCOL = P * TB * (TB + 1) // 2
PARAMS = {}
_at = 0
for _n, _k in (("norm_scale", KC), ("conv_w", NCH * TAPS), ("conv_b", NCH), ("D", NCH), ("dt_bias", NH),
               ("A_log", NH), ("gamma", KC), ("beta", KC), ("bias", KC), ("alpha", KC), ("gate_w", KC * E)):
    PARAMS[_n] = (_at, _k)
    _at += _k
NPARAM = _at
NCONST = 3 * P + E
NCOMB = E + NTAIL
MASKED = -1e30
PROJS = [("ssm", m) for m in range(NCH)] + [("B", 0), ("C", 0)] + [("gate", m) for m in range(NCH)]
POFF = [P * j * (j + 1) // 2 for j in range(TB)]
SCORES = [[(0, 3, 0)], [(0, 2, 0), (0, 0, 3 * P)], [(1, 3, 0)], [(1, 2, 0), (1, 0, 3 * P)], [(0, 1, 0), (1, 1, 2 * P)]]
TURNED = [[(0, 0, 0)], [(0, 1, 0), (0, 3, 3 * P)], [(1, 0, 0)], [(1, 1, 0), (1, 3, 3 * P)], [(0, 2, 0), (1, 2, 2 * P)]]
LAG = 8
SLOTS = 3


def schedule(prep):
    at = [(0, 0, "VO", 0, 0)]
    if prep:
        at += [(0, 1, "VQ", 0, 0)]
        for t in range(NT):
            at += [(4 * t, 8, "Q", t, 0), (4 * t + 1, 8, "R", t, 0), (4 * t + 2, 8, "X", t, 0), (4 * t + 3, 8, "X", t, 1)]
    for r in range(PAIRS):
        for k in range(5):
            n = 5 * r + k
            at += [(n, 2, "S", r, k), (n + LAG, 4, "T", r, k), (n + LAG + 1, 5, "A", r, k)]
        at += [(5 * r + 5, 3, "N", r, 0), (5 * r + LAG + 6, 6, "O", r, 0)]
    for b in range(BATCH):
        for m in range(KC):
            at += [(5 * (2 * b + 1) + LAG + 7 + m, 7, "W", b * KC + m, 0)]
    return [(op, i, k) for _, _, op, i, k in sorted(at)]


PREP = [(op, i, k) for _, _, op, i, k in sorted(
    [(2 * t, 0, "Q", t, 0) for t in range(NT)] + [(2 * t + 1, 1, "R", t, 0) for t in range(NT)]
    + [(2 * t + 2, 2, "X", t, 0) for t in range(NT)] + [(2 * t + 3, 3, "X", t, 1) for t in range(NT)])]


def layered_kernel(nc, x, params, consts, select, rope, w_in, w_out, w_moe, w_moe_tail, w_qkv, w_o, w_sign, out):
    ALU = mybir.AluOpType
    ACT = mybir.ActivationFunctionType
    AX = mybir.AxisListType
    ctx = ExitStack()
    with ctx:
        def sem(name):
            return ctx.enter_context(nc.semaphore(name))

        def sb(name, shape, dt=F32, scope=ctx):
            return scope.enter_context(nc.sbuf_tensor(name, shape, dt))

        bank = [ctx.enter_context(nc.psum_tensor(f"bank{i}", [P, HALF], F32)) for i in range(8)]

        cst = sb("cst", [P, NCONST])
        ident, upto, after = cst[:, 0:P], cst[:, P:2 * P], cst[:, 2 * P:3 * P]
        expert_no = cst[:, 3 * P:3 * P + E]
        ones = sb("ones", [P, P])
        par = sb("par", [P, NPARAM])
        x_tok = sb("x_tok", [P, NT, C])
        xnT = sb("xnT", [P, KC, T])
        xnT_hi = sb("xnT_hi", [P, KC, T], F32R)
        xnT_lo = sb("xnT_lo", [P, KC, T], F32R)
        sT = sb("sT", [P, KC, T])
        stats = sb("stats", [P, NT, 6])
        mv = sb("mv", [P, NT, 2])
        sv = sb("sv", [P, 10, NT])

        def col(name, i=0):
            return par[:, PARAMS[name][0] + i:PARAMS[name][0] + i + 1]

        def cols(name):
            return par[:, PARAMS[name][0]:PARAMS[name][0] + PARAMS[name][1]]

        s1 = ExitStack()
        w_in_sb = sb("w_in_sb", [P, KC, PROJ], F32, s1)
        w_in_hi = sb("w_in_hi", [P, KC, PROJ], F32R, s1)
        w_in_lo = sb("w_in_lo", [P, KC, PROJ], F32R, s1)
        w_out_sb = sb("w_out_sb", [P, NCH, C], F32, s1)
        w_out_hi = sb("w_out_hi", [P, NCH, C], F32R, s1)
        w_out_lo = sb("w_out_lo", [P, NCH, C], F32R, s1)
        xs = sb("xs", [P, NCH, T], F32, s1)
        norm_tok = xs[:, :, :].rearrange("p a (b c) -> p (a b) c", c=C)
        xn_tok, h_tok = norm_tok[:, 0:NT, :], norm_tok[:, NT:2 * NT, :]
        hT = sT
        y_hi = sb("y_hi", [P, NCH, T], F32R, s1)
        y_lo = sb("y_lo", [P, NCH, T], F32R, s1)
        hT_hi, hT_lo = y_hi[:, 0:KC, :], y_lo[:, 0:KC, :]
        ssm = sb("ssm", [P, NCH, TAPS - 1 + SEQ], F32, s1)
        gate = sb("gate", [P, NCH, T], F32, s1)
        BT = sb("BT", [P, T], F32, s1)
        CT = sb("CT", [P, T], F32, s1)
        dtB = sb("dtB", [P, NT, NH + P], F32, s1)
        dts = sb("dts", [P, 8, NT, NH], F32, s1)
        a_neg = sb("a_neg", [P, NH], F32, s1)
        decay_in = sb("decay_in", [P, NH, P], F32, s1)
        within = sb("within", [P, NH, P], F32, s1)
        since = sb("since", [P, NH, P], F32, s1)
        cbm = sb("cbm", [P, P], F32, s1)
        mix = sb("mix", [P, NH, P], F32, s1)
        c_dec = sb("c_dec", [P, NH, P], F32, s1)
        x_t = sb("x_t", [P, NH, P], F32, s1)
        x_dt = sb("x_dt", [P, NH, P], F32, s1)
        x_end = sb("x_end", [P, NH, P], F32, s1)
        w_end = sb("w_end", [P, NH], F32, s1)
        state = sb("state", [P, NH, P], F32, s1)
        dx = sb("dx", [P, NCH, P], F32, s1)
        s1.close()

        s2 = ExitStack()
        sel = sb("sel", [2 * E, NCOMB * P], F32, s2)
        sel_r = sb("sel_r", [2 * E, NCOMB * P], F32R, s2)
        wraw = sb("wraw", [P, FULL, WM], F32, s2)
        w_hi = sb("w_hi", [P, FULL, WM], F32R, s2)
        w_lo = sb("w_lo", [P, FULL, WM], F32R, s2)
        comb = sb("comb", [P, NCOMB, T], F32, s2)
        route = sb("route", [P, NT, E], F32, s2)
        top = sb("top", [P, NT, E], F32, s2)
        topi = sb("topi", [P, NT, E], U32, s2)
        topf = sb("topf", [P, NT, 2], F32, s2)
        pr = sb("pr", [P, 6, NT], F32, s2)
        onehot = sb("onehot", [P, NT, 2, E], F32, s2)
        cmb = sb("cmb", [P, NT, E], F32, s2)
        cmb_hl = sb("cmb_hl", [P, NT, 2 * E], F32, s2)
        cmb_h = sb("cmb_h", [P, NT, E], F32R, s2)
        combT = sb("combT", [2 * E, T], F32R, s2)
        zero_b = sb("zero_b", [P, HALF], BF16, s2)
        act_s = sb("act_s", [P, 2, HALF], F32, s2)
        act_c = sb("act_c", [P, 2, HALF], F32, s2)
        act_h = sb("act_h", [P, 2, HALF], F32, s2)
        h_hi = sb("h_hi", [P, 2, HALF], F32R, s2)
        h_lo = sb("h_lo", [P, 2, HALF], F32R, s2)
        gT = sb("gT", [P, KC, T], F32, s2)
        s2.close()

        s3 = ExitStack()
        prob = sb("prob", [P, SLOTS, 2, NCOL], F32, s3)
        before = prob[:, :, :, :].rearrange("p s h n -> p (s h n)")
        xn1 = before[:, 0:NT * C].rearrange("p (t c) -> p t c", c=C)
        xn2 = before[:, NT * C:2 * NT * C].rearrange("p (t c) -> p t c", c=C)
        wsg = before[:, 2 * NT * C:2 * NT * C + KC * C].rearrange("p (k c) -> p k c", c=C)
        wcen = before[:, 2 * NT * C + KC * C:2 * NT * C + 2 * KC * C].rearrange("p (k c) -> p k c", c=C)
        signT = sb("signT", [P, KC, T], BF16, s3)
        g1T = xnT
        wst = sb("wst", [P, KC, 4], F32, s3)
        wsT = sb("wsT", [P, KC, C], BF16, s3)
        ab = sb("ab", [P, KC], F32, s3)
        rp = sb("rp", [P, TB, 2, HD], F32, s3)
        id_b = sb("id_b", [P, P], BF16, s3)
        mask_b = sb("mask_b", [P, P], BF16, s3)
        qkv_raw = sb("qkv_raw", [P, KC, GW], F32, s3)
        qkv_hi = sb("qkv_hi", [P, KC, GW], F32R, s3)
        qkv_lo = sb("qkv_lo", [P, KC, GW], F32R, s3)
        wo_raw = sb("wo_raw", [P, 2, C], F32, s3)
        wo_hi = sb("wo_hi", [P, 2, C], F32R, s3)
        wo_lo = sb("wo_lo", [P, 2, C], F32R, s3)
        qk = sb("qk", [P, 2, NR, HD], F32, s3)
        rot = sb("rot", [P, 2, NR, HD], F32, s3)
        qkr = sb("qkr", [P, 2, NR, HD], F32, s3)
        qk_hl = sb("qk_hl", [P, 2, NR + 1, 2, HD], F32R, s3)
        qT = sb("qT", [P, 2, GQ, T], F32R, s3)
        kT = sb("kT", [P, 2, 2, T], F32R, s3)
        v_hi = sb("v_hi", [P, 2, NT, 3 * HD], F32R, s3)
        v_lo = sb("v_lo", [P, 2, NT, 3 * HD], F32R, s3)
        nmax = sb("nmax", [P, SLOTS, 2, TB], F32, s3)
        rsum = sb("rsum", [P, SLOTS, 2, TB], F32, s3)
        rinv = sb("rinv", [P, SLOTS, 2, TB], F32, s3)
        p_hi = sb("p_hi", [P, 2, HALF], F32R, s3)
        p_lo = sb("p_lo", [P, 2, HALF], F32R, s3)
        o_hi = sb("o_hi", [P, 2, 2, HALF], F32R, s3)
        o_lo = sb("o_lo", [P, 2, 2, HALF], F32R, s3)
        s3.close()

        x_in = [sem(f"x_in{b}") for b in range(BATCH)]
        par_in, cst_in, w_in_in, w_out_in, sel_in = (sem(n) for n in ("par_in", "cst_in", "w_in_in", "w_out_in", "sel_in"))
        wsg_in, rope_in = sem("wsg_in"), sem("rope_in")
        slot_in = [sem(f"slot_in{i}") for i in range(FULL)]
        qkv_in, wo_in = sem("qkv_in"), sem("wo_in")
        out_done = sem("out_done")
        phase_done = sem("phase_done")
        vstep = sem("vstep")
        gstep = sem("gstep")
        astep = sem("astep")
        var_ready, root_ready = sem("var_ready"), sem("root_ready")
        scale_ready = sem("scale_ready")
        xn_ready, h_ready = sem("xn_ready"), sem("h_ready")
        tr_full, tr_taken = sem("tr_full"), sem("tr_taken")
        hi_done, lo_done = sem("hi_done"), sem("lo_done")
        ones_ready = sem("ones_ready")
        w_in_ready, w_out_hi_done, w_out_ready = sem("w_in_ready"), sem("w_out_hi_done"), sem("w_out_ready")
        w_in_hi_done = sem("w_in_hi_done")
        dtb_full, dtb_taken = sem("dtb_full"), sem("dtb_taken")
        pr_full, pr_taken = sem("pr_full"), sem("pr_taken")
        ssm_in, conv_start, conv_done, xs_ready = sem("ssm_in"), sem("conv_start"), sem("conv_done"), sem("xs_ready")
        gate_ready = sem("gate_ready")
        e_in, e_out = sem("e_in"), sem("e_out")
        dt_ready, decay_ready = sem("dt_ready"), sem("decay_ready")
        decay_full, cb_full, xt_full = sem("decay_full"), sem("cb_full"), sem("xt_full")
        exps_ready = sem("exps_ready")
        xt_ready, mix_ready, cdec_ready, xend_ready, cbm_ready = (sem(n) for n in ("xt_ready", "mix_ready", "cdec_ready", "xend_ready", "cbm_ready"))
        y_full, state_full, state_dec, state_ready, dx_ready, y_ready = (sem(n) for n in ("y_full", "state_full", "state_dec", "state_ready", "dx_ready", "y_ready"))
        y_hi_done, y_lo_done, s_full, s_part = sem("y_hi_done"), sem("y_lo_done"), sem("s_full"), sem("s_part")
        sel_ready, route_full, comb_ready, combt_full, combt_ready, spread_full, spread_taken = (sem(n) for n in (
            "sel_ready", "route_full", "comb_ready", "combt_full", "combt_ready", "spread_full", "spread_taken"))
        diff_ready, e2_ready = sem("diff_ready"), sem("e2_ready")
        whi_done, wlo_done, wslot_free = sem("whi_done"), sem("wlo_done"), sem("wslot_free")
        zero_ready = sem("zero_ready")
        ab_full, silu_done, weighted, h_made, hhi_done, hlo_done, hslot_free = (sem(n) for n in (
            "ab_full", "silu_done", "weighted", "h_made", "hhi_done", "hlo_done", "hslot_free"))
        moe_full, g_ready, sg_ready, back_full, x_ready = sem("moe_full"), sem("g_ready"), sem("sg_ready"), sem("back_full"), sem("x_ready")

        stat_ready, aggr_ready, pad_ready, az_ready, z_ready, u_ready, lg_ready, xdt_ready = (sem(n) for n in (
            "stat_ready", "aggr_ready", "pad_ready", "az_ready", "z_ready", "u_ready", "lg_ready", "xdt_ready"))
        silu_seen, top_ready, topi_ready, spread_a, spread_v = (sem(n) for n in ("silu_seen", "top_ready", "topi_ready", "spread_a", "spread_v"))
        wcen_ready, wsign_ready, wsT_full, wsT_ready, sign_ready, sign_full, ab_ready, g1_ready, mask_ready, vpad_ready = (
            sem(n) for n in ("wcen_ready", "wsign_ready", "wsT_full", "wsT_ready", "sign_ready", "sign_full", "ab_ready",
                             "g1_ready", "mask_ready", "vpad_ready"))
        qkvhi_done, qkvlo_done, wohi_done, wolo_done, qkv_full, qk_copied, b6_free, turned, rope_done = (sem(n) for n in (
            "qkvhi_done", "qkvlo_done", "wohi_done", "wolo_done", "qkv_full", "qk_copied", "b6_free", "turned", "rope_done"))
        qkhi_done, qklo_done, tq_full, tq_taken = (sem(n) for n in ("qkhi_done", "qklo_done", "tq_full", "tq_taken"))
        score_full, max_ready, exp_done, rinv_ready, prob_ready, pt_full, phi_done, plo_done, av_done = (sem(n) for n in (
            "score_full", "max_ready", "exp_done", "rinv_ready", "prob_ready", "pt_full", "phi_done", "plo_done", "av_done"))
        ohi_done, olo_done, wo_full = sem("ohi_done"), sem("olo_done"), sem("wo_full")

        ends = {}

        def end_phase(eng):
            k = ends[eng.engine] = ends.get(eng.engine, 0) + 1
            eng.drain().then_inc(phase_done, 1)
            eng.wait_ge(phase_done, 5 * k)

        def stepper(eng, signal):
            n = [0]

            def then(ins):
                n[0] += 1
                ins.then_inc(signal, 1)
                eng.wait_ge(signal, n[0])
            return then

        vec = nc.vector
        TT, TS, STT = vec.tensor_tensor, vec.tensor_scalar, vec.scalar_tensor_tensor
        pool = nc.gpsimd
        mm = nc.tensor.matmul

        block = ctx.enter_context(nc.Block())

        @block.sync
        def _(sp):
            xv = x.rearrange("(t p) c -> p t c", p=P)
            sp.dma_start(x_tok[:, 0:TB, :], xv[:, 0:TB, :]).then_inc(x_in[0], 16)
            sp.dma_start(x_tok[:, TB:NT, :], xv[:, TB:NT, :]).then_inc(x_in[1], 16)
            sp.dma_start(cst[:, :], consts).then_inc(cst_in, 16)
            sp.dma_start(par[:, :], params).then_inc(par_in, 16)
            sp.dma_start(w_in_sb[:, :, :], w_in).then_inc(w_in_in, 16)
            sp.dma_start(w_out_sb[:, :, :], w_out).then_inc(w_out_in, 16)
            end_phase(sp)
            sp.dma_start(sel[:, :], select).then_inc(sel_in, 16)
            for i in range(FULL):
                sp.dma_start(wraw[:, i, :], w_moe[i, :, :]).then_inc(slot_in[i], 16)
            wv = w_moe.rearrange("(e i) p n -> e i p n", i=FULL)
            with sp.Fori(0, E - 1) as e:
                for i in range(FULL):
                    sp.wait_ge(wlo_done, e * FULL + (i + 1))
                    sp.dma_start(wraw[:, i, :], wv[bass.ds(e + 1, 1), i, :, :].rearrange("a p n -> (a p) n")).then_inc(slot_in[i], 16)
            for i in range(NTAIL):
                sp.wait_ge(wlo_done, (E - 1) * FULL + i + 1)
                sp.dma_start(wraw[:, i, :], w_moe_tail[i, :, :]).then_inc(slot_in[i], 16)
            end_phase(sp)
            sp.dma_start(wsg[:, :, :], w_sign).then_inc(wsg_in, 16)
            sp.dma_start(qkv_raw[:, :, :], w_qkv[0, :, :, :]).then_inc(qkv_in, 16)
            sp.dma_start(rp[:, :, :, :], rope).then_inc(rope_in, 16)
            sp.dma_start(wo_raw[:, :, :], w_o[0, :, :, :]).then_inc(wo_in, 16)
            with sp.Fori(0, KVH - 1) as g:
                sp.wait_ge(qkvlo_done, g + 1)
                sp.dma_start(qkv_raw[:, :, :], w_qkv[bass.ds(g + 1, 1), :, :, :].rearrange("a p k n -> (a p) k n")).then_inc(qkv_in, 16)
                sp.wait_ge(wolo_done, g + 1)
                sp.dma_start(wo_raw[:, :, :], w_o[bass.ds(g + 1, 1), :, :, :].rearrange("a p k n -> (a p) k n")).then_inc(wo_in, 16)
            sp.wait_ge(x_ready, 2 * NT // 2)
            sp.dma_start(out.rearrange("(t p) c -> p t c", p=P), x_tok[:, :, :]).then_inc(out_done, 16)
            sp.wait_ge(out_done, 16)

        @block.vector
        def _(dve):
            then = stepper(dve, vstep)

            def norm_stats(src, ready=None):
                for t in range(NT):
                    if ready:
                        ready(t)
                    ins = vec.bn_stats(stats[:, t, :], src[:, t, :])
                    ins.then_inc(stat_ready, 1)
                dve.wait_ge(stat_ready, NT * norms[0] + NT)
                for t in range(NT):
                    ins = vec.bn_aggr(mv[:, t, :], stats[:, t, :])
                    ins.then_inc(aggr_ready, 1)
                dve.wait_ge(aggr_ready, NT * norms[0] + NT)
                norms[0] += 1

            norms = [0]
            roots = [0]

            def rsqrt(dst, src, eps):
                TS(root_arg, src, eps, None, ALU.add).then_inc(var_ready, 1)
                roots[0] += 1
                dve.wait_ge(root_ready, roots[0])
                then(vec.reciprocal(dst, root))
                then(TT(sv[:, 3, :], root_arg, dst, ALU.mult))
                then(TT(sv[:, 3, :], sv[:, 3, :], dst, ALU.mult))
                then(TS(sv[:, 3, :], sv[:, 3, :], -0.5, 1.5, ALU.mult, ALU.add))
                then(TT(dst, dst, sv[:, 3, :], ALU.mult))

            root_arg, root = sv[:, 0, :], sv[:, 2, :]
            rstd, rrms = sv[:, 4, :], sv[:, 5, :]

            vec.memset(ones[:, :], 1.0).then_inc(ones_ready, 1)
            vec.memset(ssm[:, :, 0:TAPS - 1], 0.0).then_inc(pad_ready, 1)
            norm_stats(x_tok, lambda t: dve.wait_ge(x_in[t // TB], 16))
            rsqrt(rstd, mv[:, :, 1], 1e-5)
            then(TT(sv[:, 6, :], mv[:, :, 1], rstd, ALU.mult))
            then(TT(sv[:, 6, :], sv[:, 6, :], rstd, ALU.mult))
            for t in range(NT):
                TS(xn_tok[:, t, :], x_tok[:, t, :], mv[:, t, 0:1], rstd[:, t:t + 1], ALU.subtract, ALU.mult).then_inc(xn_ready, 1)
            rsqrt(rrms, sv[:, 6, :], 1e-6)
            dve.wait_ge(xn_ready, NT)
            for t in range(NT):
                TS(h_tok[:, t, :], xn_tok[:, t, :], rrms[:, t:t + 1], None, ALU.mult).then_inc(h_ready, 1)
            for k in range(2 * KC * BATCH):
                b, c = k // KC % BATCH, k % KC
                cs = slice(b * HALF, (b + 1) * HALF)
                dve.wait_ge(hi_done, k + 1)
                if k < KC * BATCH:
                    TT(xnT_lo[:, c, cs], bank[k][:, :], xnT_hi[:, c, cs].bitcast(F32), ALU.subtract).then_inc(lo_done, 1)
                else:
                    TT(hT_lo[:, c, cs], hT[:, c, cs], hT_hi[:, c, cs].bitcast(F32), ALU.subtract).then_inc(lo_done, 1)
            for t in range(NT):
                dve.wait_ge(dtb_full, t + 1)
                vec.tensor_copy(dtB[:, t, :], bank[t % 2][:, 0:NH + P]).then_inc(dtb_taken, 1)
            dve.wait_ge(dtb_taken, NT)
            dve.wait_ge(par_in, 16)
            v, az, z, u, d, lg = (dts[:, i, :, :] for i in range(6))
            dt, la = dts[:, 6, :, :], dts[:, 7, :, :]
            then(TT(v, dtB[:, :, 0:NH], cols("dt_bias").unsqueeze(1).to_broadcast([P, NT, NH]), ALU.add))
            then(TS(az, v, -1.0, None, ALU.mult))
            TT(az, az, v, ALU.min).then_inc(az_ready, 1)
            dve.wait_ge(z_ready, 1)
            then(TS(u, z, 1.0, None, ALU.add))
            TS(d, u, -1.0, None, ALU.add).then_inc(u_ready, 1)
            dve.wait_ge(lg_ready, 1)
            dve.wait_ge(u_ready, 1)
            then(TS(az, d, 0.0, None, ALU.is_equal))
            then(TT(d, d, az, ALU.add))
            then(TT(lg, lg, az, ALU.add))
            then(TT(lg, lg, z, ALU.mult))
            then(vec.reciprocal(u, d))
            then(TT(lg, lg, u, ALU.mult))
            then(TS(v, v, 0.0, None, ALU.max))
            then(TT(dt, v, lg, ALU.add))
            dve.wait_ge(astep, 1)
            then(TS(a_neg[:, :], a_neg[:, :], -1.0, None, ALU.mult))
            TT(la, dt, a_neg[:, :].unsqueeze(1).to_broadcast([P, NT, NH]), ALU.mult).then_inc(dt_ready, 1)
            for b in range(BATCH):
                for m in range(NCH):
                    n = b * NCH + m
                    cs = slice(b * HALF, (b + 1) * HALF)
                    dve.wait_ge(conv_start, n + 1)
                    if n == 0:
                        dve.wait_ge(pad_ready, 1)
                    for j in range(TAPS - 1):
                        ins = STT(out=xs[:, m, cs], in0=ssm[:, m, j:j + SEQ], scalar=col("conv_w", m * TAPS + j),
                                  in1=xs[:, m, cs], op0=ALU.mult, op1=ALU.add)
                        ins.then_inc(conv_done, 1)
                        dve.wait_ge(conv_done, (TAPS - 1) * n + j + 1)
            def lower_y(c):
                ts = slice(c * P, (c + 1) * P)
                dve.wait_ge(y_hi_done, c + 1)
                TT(y_lo[:, :, ts], gate[:, :, ts], y_hi[:, :, ts].bitcast(F32), ALU.subtract).then_inc(y_lo_done, 1)

            def residual(b):
                cs = slice(b * HALF, (b + 1) * HALF)
                for m in range(KC):
                    dve.wait_ge(s_full, b * KC + m + 1)
                    TT(sT[:, m, cs], bank[6 + m][:, :], xnT[:, m, cs], ALU.add).then_inc(s_part, 1)

            for c in range(NT):
                ts = slice(c * P, (c + 1) * P)
                dve.wait_ge(cb_full, c + 1)
                if c:
                    dve.wait_ge(mix_ready, c)
                TT(cbm[:, :], bank[2][:, 0:P], upto, ALU.mult).then_inc(cbm_ready, 1)
                dve.wait_ge(exps_ready, c + 1)
                dve.wait_ge(dt_ready, 1)
                if c:
                    dve.wait_ge(state_full, c)
                then(TT(w_end[:, :], dt[:, c, :], within[:, :, P - 1], ALU.mult))
                dve.wait_ge(xt_full, c + 1)
                xt = bank[3][:, :].rearrange("p (h q) -> p h q", h=NH)
                TT(x_dt[:, :, :], xt, dt[:, c, :].unsqueeze(2).to_broadcast([P, NH, P]), ALU.mult).then_inc(xdt_ready, 1)
                TT(x_end[:, :, :], xt, w_end[:, :].unsqueeze(2).to_broadcast([P, NH, P]), ALU.mult).then_inc(xend_ready, 1)
                dve.wait_ge(y_full, c + 1)
                dve.wait_ge(dx_ready, c + 1)
                yv = bank[4][:, :].rearrange("p (h q) -> p h q", h=NH)
                then(TT(dx[:, :, :], yv, dx[:, :, :], ALU.add))
                TT(gate[:, :, ts], dx[:, :, :], gate[:, :, ts], ALU.mult).then_inc(y_ready, 1)
                dve.wait_ge(state_full, c + 1)
                sv_ = bank[5][:, :].rearrange("p (h q) -> p h q", h=NH)
                if c % TB == 0:
                    vec.tensor_copy(state[:, :, :], sv_).then_inc(state_ready, 1)
                else:
                    dve.wait_ge(state_dec, c - c // TB)
                    TT(state[:, :, :], state[:, :, :], sv_, ALU.add).then_inc(state_ready, 1)
                if c:
                    lower_y(c - 1)
                if c == TB:
                    residual(0)
            lower_y(NT - 1)
            residual(1)
            end_phase(dve)

            vec.memset(zero_b[:, :], 0.0).then_inc(zero_ready, 1)
            dve.wait_ge(route_full, 1)
            then(vec.tensor_copy(route[:, :, :], bank[0][:, 0:NT * E].rearrange("p (t e) -> p t e", e=E)))
            for t in range(NT):
                vec.max(top[:, t, :], route[:, t, :]).then_inc(top_ready, 1)
            dve.wait_ge(top_ready, NT)
            for t in range(NT):
                vec.max_index(topi[:, t, :], top[:, t, :], route[:, t, :]).then_inc(topi_ready, 1)
            dve.wait_ge(topi_ready, NT)
            TT(pr[:, 0, :], top[:, :, 1], top[:, :, 0], ALU.subtract).then_inc(diff_ready, 1)
            then(vec.tensor_copy(topf[:, :, :], topi[:, :, 0:2]))
            for k in range(2):
                then(TT(onehot[:, :, k, :], expert_no.unsqueeze(1).to_broadcast([P, NT, E]),
                        topf[:, :, k].unsqueeze(2).to_broadcast([P, NT, E]), ALU.is_equal))
            dve.wait_ge(e2_ready, 1)
            then(TS(pr[:, 2, :], pr[:, 1, :], 1.0, None, ALU.add))
            then(vec.reciprocal(pr[:, 3, :], pr[:, 2, :]))
            then(TT(pr[:, 4, :], pr[:, 1, :], pr[:, 3, :], ALU.mult))
            for k in range(2):
                then(TT(onehot[:, :, k, :], onehot[:, :, k, :],
                        pr[:, 3 + k, :].unsqueeze(2).to_broadcast([P, NT, E]), ALU.mult))
            then(TT(cmb[:, :, :], onehot[:, :, 0, :], onehot[:, :, 1, :], ALU.add))
            then(vec.tensor_copy(cmb_h[:, :, :], cmb[:, :, :]))
            then(vec.tensor_copy(cmb_hl[:, :, 0:E], cmb_h[:, :, :].bitcast(F32)))
            TT(cmb_hl[:, :, E:2 * E], cmb[:, :, :], cmb_h[:, :, :].bitcast(F32), ALU.subtract).then_inc(comb_ready, 1)
            for n in range(1, 2 * NCOMB, 2):
                dve.wait_ge(spread_full, n + 1)
                vec.tensor_copy(comb[:, n // 2, HALF:T], bank[n % 4][:, :]).then_inc(spread_v, 1)

            def expert(e, chunks):
                for i in range(chunks):
                    for s in range(2):
                        u = e * (2 * FULL) + (2 * i + s)
                        dve.wait_ge(ab_full, u + 1)
                        dve.wait_ge(weighted, u + 1)
                        TT(act_h[:, s, :], act_c[:, s, :], bank[2 + s][:, :], ALU.mult).then_inc(h_made, 1)
                        dve.wait_ge(hhi_done, u + 1)
                        TT(h_lo[:, s, :], act_h[:, s, :], h_hi[:, s, :].bitcast(F32), ALU.subtract).then_inc(hlo_done, 1)

            with dve.Fori(0, E) as e:
                expert(e, FULL)
            expert(E, NTAIL)
            for n in range(KC * BATCH):
                m, s = n // 2, n % 2
                cs = slice(s * HALF, (s + 1) * HALF)
                dve.wait_ge(g_ready, n + 1)
                TT(sT[:, m, cs], sT[:, m, cs], gT[:, m, cs], ALU.mult).then_inc(sg_ready, 1)
            for n in range(NT // 2):
                dve.wait_ge(back_full, n + 1)
                xt2 = x_tok[:, 2 * n:2 * n + 2, :]
                TT(xt2, xt2, bank[n][:, :].rearrange("p (t c) -> p t c", c=C), ALU.add).then_inc(x_ready, 1)
            end_phase(dve)

            norm_stats(x_tok)
            rsqrt(rstd, mv[:, :, 1], 1e-5)
            for t in range(NT):
                TS(xn1[:, t, :], x_tok[:, t, :], mv[:, t, 0:1], rstd[:, t:t + 1], ALU.subtract, ALU.mult).then_inc(xn_ready, 1)
            dve.wait_ge(xn_ready, 2 * NT)
            norm_stats(xn1)
            rsqrt(rrms, mv[:, :, 1], 1e-5)
            for t in range(NT):
                TS(xn2[:, t, :], xn1[:, t, :], mv[:, t, 0:1], rrms[:, t:t + 1], ALU.subtract, ALU.mult).then_inc(h_ready, 1)
            dve.wait_ge(wsg_in, 16)
            then(vec.reduce_sum(wst[:, :, 0:1], wsg[:, :, :], axis=AX.X))
            then(TS(wst[:, :, 1:2], wst[:, :, 0:1], 1.0 / C, None, ALU.mult))
            for m in range(KC):
                TS(wcen[:, m, :], wsg[:, m, :], wst[:, m, 1:2], None, ALU.subtract).then_inc(wcen_ready, 1)
            TT(ab[:, :], cols("alpha"), cols("bias"), ALU.mult).then_inc(ab_ready, 1)
            then(vec.memset(sT[:, :, :], 0.0))
            vec.memset(v_lo[:, :, :, 0:HD].bitcast(F32), 0.0).then_inc(vpad_ready, 1)
            for k in range(KC * BATCH):
                b, c = k // KC, k % KC
                cs = slice(b * HALF, (b + 1) * HALF)
                dve.wait_ge(hi_done, 2 * KC * BATCH + k + 1)
                TT(xnT_lo[:, c, cs], bank[k][:, :], xnT_hi[:, c, cs].bitcast(F32), ALU.subtract).then_inc(lo_done, 1)

            def prep_v(g, a, t):
                tt = g * NT + t
                dve.wait_ge(qk_copied, tt + 1)
                TT(v_lo[:, a, t, HD:2 * HD], bank[6][:, NR * HD:GW], v_hi[:, a, t, HD:2 * HD].bitcast(F32),
                   ALU.subtract).then_inc(b6_free, 1)

            def attend(g, a, prep):
                for op, i, k in schedule(prep):
                    q = g * PAIRS + i
                    u = q * 5 + k
                    if op == "S":
                        bk = bank[(i + k) % 2]
                        dve.wait_ge(score_full, u + 1)
                        segs = SCORES[k]
                        if k == 4:
                            vec.tensor_reduce(out=nmax[:, i % SLOTS, :, 1:2], in_=bk[:, :].rearrange("p (h n) -> p h n", h=2),
                                              op=ALU.max, axis=AX.X, negate=True).then_inc(max_ready, 1)
                        else:
                            for h, j, at in segs:
                                ins = vec.tensor_reduce(out=nmax[:, i % SLOTS, h, j:j + 1], in_=bk[:, at:at + (j + 1) * P],
                                                        op=ALU.max, axis=AX.X, negate=True)
                            ins.then_inc(max_ready, 1)
                    elif op == "N":
                        dve.wait_ge(exp_done, q * 5 + 5 + 2)
                        vec.reciprocal(rinv[:, i % SLOTS, :, :], rsum[:, i % SLOTS, :, :]).then_inc(rinv_ready, 1)
                    elif op == "T":
                        b_ = (i + k) % 2
                        dve.wait_ge(phi_done, u + 1)
                        TT(p_lo[:, b_, :], bank[2 + b_][:, :], p_hi[:, b_, :].bitcast(F32), ALU.subtract).then_inc(plo_done, 1)
                    elif op == "O":
                        b, m = i // 2, i % 2
                        dve.wait_ge(ohi_done, q + 1)
                        TT(o_lo[:, b, m, :], bank[4 + m][:, :], o_hi[:, b, m, :].bitcast(F32), ALU.subtract).then_inc(olo_done, 1)
                    elif op == "W":
                        b, m = i // KC, i % KC
                        cs = slice(b * HALF, (b + 1) * HALF)
                        dve.wait_ge(wo_full, g * (BATCH * KC) + (i + 2))
                        TT(sT[:, m, cs], sT[:, m, cs], bank[6][:, :], ALU.add).then_inc(b6_free, 1)
                    elif op == "Q":
                        prep_v(g + 1, 1 - a, i)

            dve.wait_ge(vpad_ready, 1)
            for t in range(NT):
                prep_v(0, 0, t)
            with dve.Fori(0, KVH // 2 - 1) as gp:
                for a in range(2):
                    attend(gp * 2 + a, a, True)
            attend(KVH - 2, 0, True)
            attend(KVH - 1, 1, False)
            dve.wait_ge(b6_free, NT * KVH + BATCH * KC * KVH)
            for n in range(KC * BATCH):
                m, s = n // 2, n % 2
                cs = slice(s * HALF, (s + 1) * HALF)
                dve.wait_ge(g1_ready, n + 1)
                TT(sT[:, m, cs], sT[:, m, cs], g1T[:, m, cs], ALU.mult).then_inc(sg_ready, 1)
            for n in range(NT // 2):
                dve.wait_ge(back_full, NT // 2 + n + 1)
                xt2 = x_tok[:, 2 * n:2 * n + 2, :]
                TT(xt2, xt2, bank[n][:, :].rearrange("p (t c) -> p t c", c=C), ALU.add).then_inc(x_ready, 1)

        @block.scalar
        def _(act):
            actv = nc.scalar.activation

            def root(n):
                act.wait_ge(var_ready, n + 1)
                actv(sv[:, 2, :], sv[:, 0, :], ACT.Sqrt).then_inc(root_ready, 1)

            root(0)
            root(1)
            act.wait_ge(par_in, 16)
            act.wait_ge(cst_in, 16)
            for k in range(2 * KC * BATCH):
                b, c = k // KC % BATCH, k % KC
                cs = slice(b * HALF, (b + 1) * HALF)
                act.wait_ge(tr_full, k + 1)
                if k < KC * BATCH:
                    actv(xnT[:, c, cs], bank[k][:, :], ACT.Copy)
                    actv(xnT_hi[:, c, cs], bank[k][:, :], ACT.Copy).then_inc(hi_done, 1)
                else:
                    actv(hT[:, c, cs], bank[k][:, :], ACT.Copy, scale=col("norm_scale", c))
                    actv(hT_hi[:, c, cs], bank[k][:, :], ACT.Copy, scale=col("norm_scale", c)).then_inc(hi_done, 1)
            act.wait_ge(w_in_in, 16)
            actv(w_in_hi[:, :, :], w_in_sb[:, :, :], ACT.Copy).then_inc(w_in_hi_done, 1)
            actv(a_neg[:, :], cols("A_log"), ACT.Exp).then_inc(astep, 1)
            act.wait_ge(az_ready, 1)
            actv(dts[:, 2, :, :], dts[:, 1, :, :], ACT.Exp).then_inc(z_ready, 1)
            act.wait_ge(u_ready, 1)
            actv(dts[:, 5, :, :], dts[:, 3, :, :], ACT.Ln).then_inc(lg_ready, 1)
            act.wait_ge(w_out_in, 16)
            actv(w_out_hi[:, :, :], w_out_sb[:, :, :], ACT.Copy).then_inc(w_out_hi_done, 1)
            n = 0
            for b in range(BATCH):
                cs = slice(b * HALF, (b + 1) * HALF)
                for kind, m in PROJS:
                    bk = bank[2 + n % 6]
                    act.wait_ge(pr_full, n + 1)
                    if kind == "ssm":
                        if b:
                            act.wait_ge(conv_done, (TAPS - 1) * (m + 1))
                        actv(ssm[:, m, TAPS - 1:TAPS - 1 + SEQ], bk[:, :], ACT.Copy).then_inc(ssm_in, 1)
                        actv(xs[:, m, cs], bk[:, :], ACT.Identity, scale=col("conv_w", m * TAPS + TAPS - 1),
                             bias=col("conv_b", m)).then_inc(conv_start, 1)
                    elif kind == "B":
                        actv(BT[:, cs], bk[:, :], ACT.Copy).then_inc(pr_taken, 1)
                    elif kind == "C":
                        actv(CT[:, cs], bk[:, :], ACT.Copy).then_inc(pr_taken, 1)
                    else:
                        actv(gate[:, m, cs], bk[:, :], ACT.Silu).then_inc(pr_taken, 1)
                    n += 1
                for m in range(NCH):
                    act.wait_ge(conv_done, (TAPS - 1) * (b * NCH + m + 1))
                    actv(xs[:, m, cs], xs[:, m, cs], ACT.Silu).then_inc(xs_ready, 1)
            def upper_y(c):
                ts = slice(c * P, (c + 1) * P)
                act.wait_ge(y_ready, c + 1)
                actv(y_hi[:, :, ts], gate[:, :, ts], ACT.Copy).then_inc(y_hi_done, 1)

            for c in range(NT):
                act.wait_ge(decay_full, c + 1)
                if c:
                    act.wait_ge(mix_ready, c)
                    act.wait_ge(xend_ready, c)
                actv(within[:, :, :], bank[0][:, :].rearrange("p (h q) -> p h q", h=NH), ACT.Exp)
                if c:
                    act.wait_ge(cdec_ready, c)
                    if c // TB or c % TB > 1:
                        act.wait_ge(state_dec, (c - 1) - (c - 1) // TB)
                actv(since[:, :, :], bank[1][:, :].rearrange("p (h q) -> p h q", h=NH), ACT.Exp).then_inc(exps_ready, 1)
                if c:
                    upper_y(c - 1)
            upper_y(NT - 1)
            end_phase(act)

            act.wait_ge(sel_in, 16)
            actv(sel_r[:, :], sel[:, :], ACT.Copy).then_inc(sel_ready, 1)
            act.wait_ge(diff_ready, 1)
            actv(pr[:, 1, :], pr[:, 0, :], ACT.Exp).then_inc(e2_ready, 1)
            for s in range(2):
                act.wait_ge(combt_full, s + 1)
                actv(combT[:, s * HALF:(s + 1) * HALF], bank[1 + s][0:2 * E, :], ACT.Copy).then_inc(combt_ready, 1)

            def split_hi(slot, n, arrived):
                act.wait_ge(slot_in[slot], arrived)
                act.wait_ge(hslot_free, n * 2 + 2)
                actv(w_hi[:, slot, :], wraw[:, slot, :], ACT.Copy).then_inc(whi_done, 1)

            split_hi(0, 0, 16)
            for n in range(0, 2 * NCOMB, 2):
                act.wait_ge(spread_full, n + 1)
                actv(comb[:, n // 2, 0:HALF], bank[n % 4][:, :], ACT.Copy).then_inc(spread_a, 1)
            split_hi(1, 1, 16)

            def expert(e, chunks, tail_next):
                for i in range(chunks):
                    for s in range(2):
                        u = e * (2 * FULL) + (2 * i + s)
                        act.wait_ge(ab_full, u + 1)
                        actv(act_s[:, s, :], bank[s][:, :], ACT.Silu).then_inc(silu_done, 1)
                        if s == 0 and (i + 2 < chunks or tail_next):
                            j = i + 2
                            split_hi(j % FULL, e * FULL + j, (e + (1 + j // FULL)) * 16)
                        act.wait_ge(h_made, u + 1)
                        act.wait_ge(hslot_free, u + (2 * FULL - 1))
                        actv(h_hi[:, s, :], act_h[:, s, :], ACT.Copy).then_inc(hhi_done, 1)

            with act.Fori(0, E) as e:
                expert(e, FULL, True)
            expert(E, NTAIL, False)
            act.wait_ge(hslot_free, 2 * (E * FULL + NTAIL + FULL))
            for n in range(KC * BATCH):
                m, s = n // 2, n % 2
                actv(gT[:, m, s * HALF:(s + 1) * HALF], bank[4 + n][:, :], ACT.Silu).then_inc(g_ready, 1)
            end_phase(act)

            root(2)
            root(3)
            for k in range(2 * KC * BATCH):
                b, c = k // KC % BATCH, k % KC
                cs = slice(b * HALF, (b + 1) * HALF)
                act.wait_ge(tr_full, 2 * KC * BATCH + k + 1)
                if k < KC * BATCH:
                    actv(xnT_hi[:, c, cs], bank[k][:, :], ACT.Copy).then_inc(hi_done, 1)
                else:
                    actv(signT[:, c, cs], bank[k][:, :], ACT.Sign, scale=col("gamma", c), bias=col("beta", c)).then_inc(sign_ready, 1)
            for m in range(KC):
                act.wait_ge(wcen_ready, m + 1)
                actv(wsg[:, m, :], wcen[:, m, :], ACT.Sign).then_inc(wsign_ready, 1)
            act.wait_ge(wsT_full, 1)
            actv(wsT[:, :, :], bank[4][:, :].rearrange("p (k o) -> p k o", k=KC), ACT.Copy).then_inc(wsT_ready, 1)
            actv(id_b[:, :], ident, ACT.Copy).then_inc(mask_ready, 1)
            actv(mask_b[:, :], after, ACT.Copy, scale=MASKED).then_inc(mask_ready, 1)
            act.wait_ge(ab_ready, 1)
            for n in range(KC * BATCH):
                m, s = n // 2, n % 2
                act.wait_ge(sign_full, n + 1)
                actv(g1T[:, m, s * HALF:(s + 1) * HALF], bank[n][:, :], ACT.Silu, scale=col("alpha", m),
                     bias=ab[:, m:m + 1]).then_inc(g1_ready, 1)

            def weights_q(g):
                act.wait_ge(qkv_in, g * 16 + 16)
                if not isinstance(g, int) or g:
                    act.wait_ge(qkv_full, g * NT)
                actv(qkv_hi[:, :, :], qkv_raw[:, :, :], ACT.Copy).then_inc(qkvhi_done, 1)

            def prep_copy(g, a, t):
                tt = g * NT + t
                act.wait_ge(qkv_full, tt + 1)
                if not isinstance(tt, int) or tt > 1:
                    act.wait_ge(rope_done, tt - 1)
                if t == 0 and not (isinstance(g, int) and g == 0):
                    act.wait_ge(av_done, (g - 1) * (5 * PAIRS) + 2)
                actv(qk[:, t % 2, :, :], bank[6][:, 0:NR * HD].rearrange("p (h d) -> p h d", d=HD), ACT.Copy)
                actv(v_hi[:, a, t, HD:2 * HD], bank[6][:, NR * HD:GW], ACT.Copy).then_inc(qk_copied, 1)

            def prep_hi(g, t):
                tt = g * NT + t
                act.wait_ge(rope_done, tt + 1)
                if not isinstance(tt, int) or tt > 1:
                    act.wait_ge(tq_full, tt * 2 - 2)
                actv(qk_hl[:, t % 2, 0:NR, 0, :], qkr[:, t % 2, :, :], ACT.Copy)
                actv(qk_hl[:, t % 2, NR, 0, :], qkr[:, t % 2, GQ, :], ACT.Copy).then_inc(qkhi_done, 1)

            def prep_take(g, a, t, k):
                tt = g * NT + t
                act.wait_ge(tq_full, tt * 2 + (1 + k))
                dst = qT[:, a, :, t * P:(t + 1) * P] if k == 0 else kT[:, a, :, t * P:(t + 1) * P]
                n = GQ if k == 0 else 2
                actv(dst, bank[7][:, 0:n * P].rearrange("p (h n) -> p h n", n=P), ACT.Copy,
                     scale=1.0 if k == 0 else HD ** -0.5).then_inc(tq_taken, 1)

            def attend(g, a, prep):
                for op, i, k in schedule(prep):
                    q = g * PAIRS + i
                    u = q * 5 + k
                    if op == "S":
                        bk = bank[(i + k) % 2]
                        act.wait_ge(max_ready, u + 1)
                        for h, j, at in SCORES[k]:
                            ins = actv(prob[:, i % SLOTS, h, POFF[j]:POFF[j] + (j + 1) * P], bk[:, at:at + (j + 1) * P], ACT.Exp,
                                       bias=nmax[:, i % SLOTS, h, j:j + 1], accum_out=rsum[:, i % SLOTS, h, j:j + 1])
                        ins.then_inc(exp_done, 1)
                    elif op == "T":
                        b_ = (i + k) % 2
                        act.wait_ge(pt_full, u + 1)
                        act.wait_ge(av_done, u + 1)
                        actv(p_hi[:, b_, :], bank[2 + b_][:, :], ACT.Copy).then_inc(phi_done, 1)
                    elif op == "O":
                        b, m = i // 2, i % 2
                        act.wait_ge(av_done, q * 5 + 7)
                        act.wait_ge(wo_full, g * (BATCH * KC) + 1)
                        actv(o_hi[:, b, m, :], bank[4 + m][:, :], ACT.Copy).then_inc(ohi_done, 1)
                    elif op == "VO":
                        act.wait_ge(wo_in, g * 16 + 16)
                        act.wait_ge(wo_full, g * (BATCH * KC) + 1)
                        actv(wo_hi[:, :, :], wo_raw[:, :, :], ACT.Copy).then_inc(wohi_done, 1)
                    elif op == "VQ":
                        weights_q(g + 1)
                    elif op == "Q":
                        prep_copy(g + 1, 1 - a, i)
                    elif op == "R":
                        prep_hi(g + 1, i)
                    elif op == "X":
                        prep_take(g + 1, 1 - a, i, k)

            act.sem_inc(exp_done, 2)
            weights_q(0)
            act.wait_ge(vpad_ready, 4)
            for op, i, k in PREP:
                if op == "Q":
                    prep_copy(0, 0, i)
                elif op == "R":
                    prep_hi(0, i)
                elif op == "X":
                    prep_take(0, 0, i, k)
            with act.Fori(0, KVH // 2 - 1) as gp:
                for a in range(2):
                    attend(gp * 2 + a, a, True)
            attend(KVH - 2, 0, True)
            attend(KVH - 1, 1, False)

        @block.gpsimd
        def _(gp_):
            GT = pool.tensor_tensor
            gp_.wait_ge(w_in_hi_done, 1)
            GT(w_in_lo[:, :, :], w_in_sb[:, :, :], w_in_hi[:, :, :].bitcast(F32), ALU.subtract).then_inc(w_in_ready, 1)
            gp_.wait_ge(w_out_hi_done, 1)
            GT(w_out_lo[:, :, :], w_out_sb[:, :, :], w_out_hi[:, :, :].bitcast(F32), ALU.subtract).then_inc(w_out_ready, 1)
            gp_.wait_ge(dt_ready, 1)

            def decay(c):
                if c:
                    gp_.wait_ge(decay_full, c)
                GT(decay_in[:, :, :], upto.unsqueeze(1).to_broadcast([P, NH, P]),
                   dts[:, 7, c, :].unsqueeze(2).to_broadcast([P, NH, P]), ALU.mult).then_inc(decay_ready, 1)

            decay(0)
            for c in range(NT):
                b = c // TB
                ts = slice(c * P, (c + 1) * P)
                gp_.wait_ge(xs_ready, (b + 1) * NCH)
                if c:
                    gp_.wait_ge(y_ready, c)
                GT(dx[:, :, :], xs[:, :, ts], cols("D").unsqueeze(2).to_broadcast([P, NCH, P]), ALU.mult).then_inc(dx_ready, 1)
                gp_.wait_ge(exps_ready, c + 1)
                gp_.wait_ge(cbm_ready, c + 1)
                if c:
                    gp_.wait_ge(y_full, c)
                GT(mix[:, :, :], within[:, :, :], cbm[:, :].unsqueeze(1).to_broadcast([P, NH, P]), ALU.mult).then_inc(mix_ready, 1)
                if c + 1 < NT and not c % TB:
                    decay(c + 1)
                if c % TB:
                    GT(c_dec[:, :, :], since[:, :, :], CT[:, ts].unsqueeze(1).to_broadcast([P, NH, P]), ALU.mult).then_inc(cdec_ready, 1)
                    if c + 1 < NT:
                        decay(c + 1)
                    gp_.wait_ge(y_full, c + 1)
                    gp_.wait_ge(state_ready, c)
                    GT(state[:, :, :], state[:, :, :], since[:, :, P - 1].unsqueeze(2).to_broadcast([P, NH, P]), ALU.mult).then_inc(state_dec, 1)
                else:
                    gp_.sem_inc(cdec_ready, 1)
            end_phase(gp_)

            def split_lo(slot, n):
                gp_.wait_ge(whi_done, n + 1)
                GT(w_lo[:, slot, :], wraw[:, slot, :], w_hi[:, slot, :].bitcast(F32), ALU.subtract).then_inc(wlo_done, 1)

            split_lo(0, 0)
            split_lo(1, 1)
            gp_.wait_ge(spread_a, NCOMB)
            gp_.wait_ge(spread_v, NCOMB)

            def expert(e, chunks, tail_next):
                for i in range(chunks):
                    which = bass.ds(e, 1) if chunks == FULL else slice(E + i, E + i + 1)
                    for s in range(2):
                        u = e * (2 * FULL) + (2 * i + s)
                        gp_.wait_ge(silu_done, u + 1)
                        gp_.sem_inc(silu_seen, 1)
                        GT(act_c[:, s, :], act_s[:, s, :], comb[:, which, s * HALF:(s + 1) * HALF].rearrange("p a n -> p (a n)"),
                           ALU.mult).then_inc(weighted, 1)
                        if s == 0 and (i + 2 < chunks or tail_next):
                            split_lo((i + 2) % FULL, e * FULL + (i + 2))

            with gp_.Fori(0, E) as e:
                expert(e, FULL, True)
            expert(E, NTAIL, False)
            end_phase(gp_)

            pool.memset(v_hi[:, :, :, 0:HD].bitcast(F32), 0.0).then_inc(vpad_ready, 1)
            pool.memset(v_hi[:, :, :, 2 * HD:3 * HD].bitcast(F32), 0.0).then_inc(vpad_ready, 1)
            pool.memset(v_lo[:, :, :, 2 * HD:3 * HD].bitcast(F32), 0.0).then_inc(vpad_ready, 1)

            def weights_q(g):
                gp_.wait_ge(qkvhi_done, g + 1)
                GT(qkv_lo[:, :, :], qkv_raw[:, :, :], qkv_hi[:, :, :].bitcast(F32), ALU.subtract).then_inc(qkvlo_done, 1)

            def prep_rope(g, t):
                tt = g * NT + t
                sl = t % 2
                hd2 = HD // 2
                cosv = rp[:, t % TB, 0, :].unsqueeze(1).to_broadcast([P, NR, HD])
                sinv = rp[:, t % TB, 1, :].unsqueeze(1).to_broadcast([P, NR, HD])
                gp_.wait_ge(qk_copied, tt + 1)
                GT(qkr[:, sl, :, :], qk[:, sl, :, :], cosv, ALU.mult).then_inc(turned, 1)
                GT(rot[:, sl, :, 0:hd2], qk[:, sl, :, hd2:HD], sinv[:, :, 0:hd2], ALU.mult).then_inc(turned, 1)
                GT(rot[:, sl, :, hd2:HD], qk[:, sl, :, 0:hd2], sinv[:, :, hd2:HD], ALU.mult).then_inc(turned, 1)
                gp_.wait_ge(turned, tt * 3 + 3)
                GT(qkr[:, sl, :, :], qkr[:, sl, :, :], rot[:, sl, :, :], ALU.add).then_inc(rope_done, 1)

            def prep_lo(g, t):
                tt = g * NT + t
                gp_.wait_ge(qkhi_done, tt + 1)
                GT(qk_hl[:, t % 2, 0:NR, 1, :], qkr[:, t % 2, :, :], qk_hl[:, t % 2, 0:NR, 0, :].bitcast(F32),
                   ALU.subtract).then_inc(qklo_done, 1)

            def attend(g, a, prep):
                for op, i, k in schedule(prep):
                    q = g * PAIRS + i
                    if op == "N":
                        gp_.wait_ge(rinv_ready, q + 1)
                        for h in range(2):
                            for j in range(TB):
                                seg = prob[:, i % SLOTS, h, POFF[j]:POFF[j] + (j + 1) * P]
                                ins = GT(seg, seg, rinv[:, i % SLOTS, h, j:j + 1].to_broadcast([P, (j + 1) * P]), ALU.mult)
                            ins.then_inc(prob_ready, 1)
                    elif op == "VO":
                        gp_.wait_ge(wohi_done, g + 1)
                        GT(wo_lo[:, :, :], wo_raw[:, :, :], wo_hi[:, :, :].bitcast(F32), ALU.subtract).then_inc(wolo_done, 1)
                    elif op == "VQ":
                        weights_q(g + 1)
                    elif op == "Q":
                        prep_rope(g + 1, i)
                    elif op == "R":
                        prep_lo(g + 1, i)

            weights_q(0)
            gp_.wait_ge(rope_in, 16)
            for op, i, k in PREP:
                if op == "Q":
                    prep_rope(0, i)
                elif op == "R":
                    prep_lo(0, i)
            with gp_.Fori(0, KVH // 2 - 1) as gp:
                for a in range(2):
                    attend(gp * 2 + a, a, True)
            attend(KVH - 2, 0, True)
            attend(KVH - 1, 1, False)

        @block.tensor
        def _(pe):
            def tr(dst, src):
                return nc.tensor.transpose(dst, src, ident)

            def split3(dst, w_h, w_l, m_h, m_l, start, stop):
                mm(dst, w_l, m_h, start=start, stop=False)
                mm(dst, w_h, m_l, start=False, stop=False)
                return mm(dst, w_h, m_h, start=False, stop=stop)

            pe.wait_ge(cst_in, 16)
            for k in range(2 * KC * BATCH):
                b, c = k // KC % BATCH, k % KC
                src, ready = (xn_tok, xn_ready) if k < KC * BATCH else (h_tok, h_ready)
                pe.wait_ge(ready, (b + 1) * TB)
                for t in range(TB):
                    ins = tr(bank[k][:, t * P:(t + 1) * P], src[:, b * TB + t, c * P:(c + 1) * P])
                ins.then_inc(tr_full, 1)
            pe.wait_ge(lo_done, 2 * KC * BATCH)
            pe.wait_ge(w_in_in, 16)
            for t in range(NT):
                if t > 1:
                    pe.wait_ge(dtb_taken, t - 1)
                for c in range(KC):
                    ins = mm(bank[t % 2][:, 0:NH + P], hT[:, c, t * P:(t + 1) * P], w_in_sb[:, c, DT0:DT0 + NH + P],
                             start=c == 0, stop=c == KC - 1)
                ins.then_inc(dtb_full, 1)
            pe.wait_ge(w_in_ready, 1)
            n = 0
            for b in range(BATCH):
                cs = slice(b * HALF, (b + 1) * HALF)
                for kind, m in PROJS:
                    at = {"gate": m * P, "ssm": DI + m * P, "B": B0, "C": C0}[kind]
                    bk = bank[2 + n % 6]
                    if n >= 6:
                        taken = [j for j in range(n - 5)]
                        convs = sum(PROJS[j % len(PROJS)][0] == "ssm" for j in taken)
                        pe.wait_ge(conv_start, convs)
                        if len(taken) > convs:
                            pe.wait_ge(pr_taken, len(taken) - convs)
                    for c in range(KC):
                        ins = split3(bk[:, :], w_in_hi[:, c, at:at + P], w_in_lo[:, c, at:at + P],
                                     hT_hi[:, c, cs], hT_lo[:, c, cs], c == 0, c == KC - 1)
                    ins.then_inc(pr_full, 1)
                    n += 1
            def out_product(b):
                cs = slice(b * HALF, (b + 1) * HALF)
                pe.wait_ge(w_out_ready, 1)
                pe.wait_ge(y_lo_done, (b + 1) * TB)
                for m in range(KC):
                    if b:
                        pe.wait_ge(s_part, m + 1)
                    for k in range(NCH):
                        ins = split3(bank[6 + m][:, :], w_out_hi[:, k, m * P:(m + 1) * P], w_out_lo[:, k, m * P:(m + 1) * P],
                                     y_hi[:, k, cs], y_lo[:, k, cs], k == 0, k == NCH - 1)
                    ins.then_inc(s_full, 1)

            pe.wait_ge(ones_ready, 1)
            pe.wait_ge(pr_taken, BATCH * (NCH + 2))
            pe.wait_ge(conv_start, BATCH * NCH)
            for c in range(NT):
                b = c // TB
                ts = slice(c * P, (c + 1) * P)
                pe.wait_ge(decay_ready, c + 1)
                if c:
                    pe.wait_ge(exps_ready, c)
                else:
                    pe.wait_ge(dtb_taken, NT)
                dec = decay_in[:, :, :].rearrange("p h q -> p (h q)")
                mm(bank[0][:, :], after, dec, start=True, stop=True)
                mm(bank[1][:, :], ones[:, :], dec, start=True, stop=True).then_inc(decay_full, 1)
                if c:
                    pe.wait_ge(cbm_ready, c)
                mm(bank[2][:, 0:P], BT[:, ts], CT[:, ts], start=True, stop=True).then_inc(cb_full, 1)
                pe.wait_ge(xs_ready, (b + 1) * NCH)
                if c:
                    pe.wait_ge(xend_ready, c)
                for h in range(NH):
                    ins = tr(bank[3][:, h * P:(h + 1) * P], xs[:, h, ts])
                ins.then_inc(xt_full, 1)
                pe.wait_ge(mix_ready, c + 1)
                pe.wait_ge(xdt_ready, c + 1)
                if c % TB:
                    pe.wait_ge(cdec_ready, c + 1)
                if c:
                    pe.wait_ge(state_ready, c)
                    pe.wait_ge(y_ready, c)
                for h in range(NH):
                    dst = bank[4][:, h * P:(h + 1) * P]
                    ins = mm(dst, x_dt[:, h, :], mix[:, h, :], start=True, stop=c % TB == 0)
                    if c % TB:
                        ins = mm(dst, state[:, h, :], c_dec[:, h, :], start=False, stop=True)
                ins.then_inc(y_full, 1)
                pe.wait_ge(xend_ready, c + 1)
                mm(bank[5][:, :], dtB[:, c, NH:NH + P], x_end[:, :, :].rearrange("p h q -> p (h q)"),
                   start=True, stop=True).then_inc(state_full, 1)
                if c == TB:
                    out_product(0)
            out_product(1)
            end_phase(pe)

            pe.sem_inc(hslot_free, 2 * FULL)
            for t in range(NT):
                for c in range(KC):
                    ins = mm(bank[0][:, t * E:(t + 1) * E], xnT[:, c, t * P:(t + 1) * P],
                             par[:, PARAMS["gate_w"][0] + c * E:PARAMS["gate_w"][0] + (c + 1) * E], start=c == 0, stop=c == KC - 1)
            ins.then_inc(route_full, 1)
            pe.wait_ge(zero_ready, 1)
            for n in range(KC * BATCH):
                mm(bank[4 + n][:, :], zero_b[:, 0:P], zero_b[:, :], start=True, stop=False)
            pe.wait_ge(comb_ready, 1)
            for s in range(2):
                for t in range(TB):
                    ins = tr(bank[1 + s][0:2 * E, t * P:(t + 1) * P], cmb_hl[:, s * TB + t, :])
                ins.then_inc(combt_full, 1)
            pe.wait_ge(combt_ready, 2)
            pe.wait_ge(sel_ready, 1)
            for n in range(2 * NCOMB):
                k, s = n // 2, n % 2
                if n >= 4:
                    pe.wait_ge(spread_a if n % 2 == 0 else spread_v, (n - 4) // 2 + 1)
                mm(bank[n % 4][:, :], sel_r[:, k * P:(k + 1) * P], combT[:, s * HALF:(s + 1) * HALF],
                   start=True, stop=True).then_inc(spread_full, 1)
            pe.wait_ge(spread_a, NCOMB)
            pe.wait_ge(spread_v, NCOMB)

            def in_products(slot, s):
                cs = slice(s * HALF, (s + 1) * HALF)
                for bk, at in ((bank[s], 0), (bank[2 + s], FC2)):
                    for c in range(KC):
                        w = slice(at + c * P, at + (c + 1) * P)
                        ins = split3(bk[:, :], w_hi[:, slot, w], w_lo[:, slot, w], xnT_hi[:, c, cs], xnT_lo[:, c, cs],
                                     c == 0, c == KC - 1)
                ins.then_inc(ab_full, 1)

            pe.wait_ge(wlo_done, 1)
            in_products(0, 0)
            in_products(0, 1)

            def expert(e, chunks, tail_next):
                for i in range(chunks):
                    for s in range(2):
                        u = e * (2 * FULL) + (2 * i + s)
                        if i + 1 < chunks or tail_next:
                            if s == 0:
                                pe.wait_ge(wlo_done, e * FULL + (i + 2))
                            pe.wait_ge(h_made, u + 1)
                            in_products((i + 1) % FULL, s)
                        pe.wait_ge(hlo_done, u + 1)
                        last = chunks == NTAIL and i == chunks - 1
                        for m in range(KC):
                            w = slice(PJ + m * P, PJ + (m + 1) * P)
                            ins = split3(bank[4 + 2 * m + s][:, :], w_hi[:, i, w], w_lo[:, i, w], h_hi[:, s, :], h_lo[:, s, :], False, last)
                        ins.then_inc(hslot_free, 1)

            with pe.Fori(0, E) as e:
                expert(e, FULL, True)
            expert(E, NTAIL, False)
            for n in range(NT // 2):
                pe.wait_ge(sg_ready, KC * BATCH)
                for j in range(2 * KC):
                    t, m = 2 * n + j // KC, j % KC
                    ins = tr(bank[n][:, j * P:(j + 1) * P], sT[:, m, t * P:(t + 1) * P])
                ins.then_inc(back_full, 1)
            end_phase(pe)

            for k in range(2 * KC * BATCH):
                b, c = k // KC % BATCH, k % KC
                src, ready = (xn1, xn_ready) if k < KC * BATCH else (xn2, h_ready)
                pe.wait_ge(ready, NT + (b + 1) * TB)
                for t in range(TB):
                    ins = tr(bank[k][:, t * P:(t + 1) * P], src[:, b * TB + t, c * P:(c + 1) * P])
                ins.then_inc(tr_full, 1)
            pe.wait_ge(wsign_ready, KC)
            pe.wait_ge(sign_ready, 1)
            for k in range(KC):
                for m in range(KC):
                    ins = tr(bank[4][:, (k * KC + m) * P:(k * KC + m + 1) * P], wsg[:, m, k * P:(k + 1) * P])
            ins.then_inc(wsT_full, 1)
            pe.wait_ge(wsT_ready, 1)
            pe.wait_ge(sign_ready, KC * BATCH)
            pe.wait_ge(lo_done, 3 * KC * BATCH)
            for n in range(KC * BATCH):
                m, s = n // 2, n % 2
                for c in range(KC):
                    ins = mm(bank[n][:, :], wsT[:, c, m * P:(m + 1) * P], signT[:, c, s * HALF:(s + 1) * HALF],
                             start=c == 0, stop=c == KC - 1)
                ins.then_inc(sign_full, 1)

            def prep_qkv(g, t, event):
                if t == 0:
                    pe.wait_ge(qkvlo_done, g + 1)
                if not isinstance(event, int) or event:
                    pe.wait_ge(b6_free, event)
                for c in range(KC):
                    ts = slice(t * P, (t + 1) * P)
                    ins = split3(bank[6][:, 0:GW], xnT_hi[:, c, ts], xnT_lo[:, c, ts], qkv_hi[:, c, :], qkv_lo[:, c, :],
                                 c == 0, c == KC - 1)
                ins.then_inc(qkv_full, 1)

            def prep_turn(g, t, k):
                tt = g * NT + t
                if k == 0:
                    pe.wait_ge(qklo_done, tt + 1)
                if not isinstance(tt, int) or tt or k:
                    pe.wait_ge(tq_taken, tt * 2 + k)
                flat = qk_hl[:, t % 2, :, :, :].rearrange("p h a d -> p (h a d)").bitcast(F32)
                for j in range(GQ if k == 0 else 2):
                    at = j * P if k == 0 else GQ * P + j * HD
                    ins = tr(bank[7][:, j * P:(j + 1) * P], flat[:, at:at + P])
                ins.then_inc(tq_full, 1)

            def attend(g, a, prep):
                event = g * (NT + BATCH * KC) + NT
                done6 = 0
                for op, i, k in schedule(prep):
                    q = g * PAIRS + i
                    u = q * 5 + k
                    b = i // 2
                    if op == "S":
                        if k == 0 and i % 2 == 0:
                            pe.wait_ge(tq_taken, g * (2 * NT) + (b + 1) * NT)
                        pe.wait_ge(exp_done, u + 1)
                        for h, j, at in SCORES[k]:
                            n = (j + 1) * P
                            dst = bank[(i + k) % 2][:, at:at + n]
                            qs = qT[:, a, 2 * (i % 2) + h, b * HALF + j * P:b * HALF + (j + 1) * P]
                            mm(dst, qs, kT[:, a, 0, b * HALF:b * HALF + n], start=True, stop=False)
                            mm(dst, qs, kT[:, a, 1, b * HALF:b * HALF + n], start=False, stop=False)
                            ins = mm(bank[(i + k) % 2][:, at + j * P:at + n], mask_b[:, :], id_b[:, :], start=False, stop=True)
                        ins.then_inc(score_full, 1)
                    elif op == "T":
                        if k in (0, 2):
                            pe.wait_ge(prob_ready, q * 2 + (1 if k == 0 else 2))
                        pe.wait_ge(plo_done, u + 1)
                        for h, j, at in TURNED[k]:
                            for r in range(j, TB):
                                ins = tr(bank[2 + (i + k) % 2][:, at + (r - j) * P:at + (r - j + 1) * P],
                                         prob[:, i % SLOTS, h, POFF[r] + j * P:POFF[r] + (j + 1) * P])
                        ins.then_inc(pt_full, 1)
                    elif op == "A":
                        pe.wait_ge(plo_done, u + 3)
                        if k == 0:
                            pe.wait_ge(olo_done, q + 1)
                        b_ = (i + k) % 2
                        for h, j, at in TURNED[k]:
                            n = (TB - j) * P
                            dst = bank[4 + i % 2][:, j * P:j * P + n]
                            vs = slice(HD, 3 * HD) if h == 0 else slice(0, 2 * HD)
                            last = k == 4 and h == 1
                            ins = split3(dst, v_hi[:, a, b * TB + j, vs], v_lo[:, a, b * TB + j, vs], p_hi[:, b_, at:at + n],
                                         p_lo[:, b_, at:at + n], k == 0, last)
                        ins.then_inc(av_done, 1)
                    elif op == "W":
                        m = i % KC
                        b = i // KC
                        pe.wait_ge(wolo_done, g + 1)
                        pe.wait_ge(olo_done, g * PAIRS + (2 * b + 4))
                        pe.wait_ge(b6_free, event + done6)
                        done6 += 1
                        for c in range(2):
                            ins = split3(bank[6][:, :], wo_hi[:, c, m * P:(m + 1) * P], wo_lo[:, c, m * P:(m + 1) * P],
                                         o_hi[:, b, c, :], o_lo[:, b, c, :], c == 0, c == 1)
                        ins.then_inc(wo_full, 1)
                    elif op == "Q":
                        prep_qkv(g + 1, i, event + done6)
                        done6 += 1
                    elif op == "X":
                        prep_turn(g + 1, i, k)

            pe.sem_inc(plo_done, 2)
            pe.sem_inc(olo_done, 2)
            pe.sem_inc(av_done, 2)
            pe.sem_inc(wo_full, 1)
            pe.wait_ge(g1_ready, KC * BATCH)
            pe.wait_ge(mask_ready, 2)
            for op, i, k in PREP:
                if op == "Q":
                    prep_qkv(0, i, i)
                elif op == "X":
                    prep_turn(0, i, k)
            with pe.Fori(0, KVH // 2 - 1) as gp:
                for a in range(2):
                    attend(gp * 2 + a, a, True)
            attend(KVH - 2, 0, True)
            attend(KVH - 1, 1, False)
            for n in range(NT // 2):
                pe.wait_ge(sg_ready, 2 * KC * BATCH)
                for j in range(2 * KC):
                    t, m = 2 * n + j // KC, j % KC
                    ins = tr(bank[n][:, j * P:(j + 1) * P], sT[:, m, t * P:(t + 1) * P])
                ins.then_inc(back_full, 1)


def _constants():
    import numpy as np
    p = np.arange(P)
    ident = np.eye(P)
    upto = p[:, None] <= p[None, :]
    after = p[:, None] > p[None, :]
    number = np.broadcast_to(np.arange(E), (P, E))
    consts = np.concatenate([ident, upto, after, number], 1).astype(np.float32)
    select = np.zeros((2, E, NCOMB, P), np.float32)
    for k in range(E):
        select[:, k, k, :] = 1
    for j in range(NTAIL):
        for r in range(P // TAIL):
            select[:, j * (P // TAIL) + r, E + j, r * TAIL:(r + 1) * TAIL] = 1
    freq = (1.0 / np.float32(10000.0) ** (np.arange(0, HD, 2, dtype=np.float32) / np.float32(HD))).astype(np.float32)
    angle = np.arange(SEQ, dtype=np.float32)[:, None] * freq[None, :]
    cos, sin = np.cos(angle), np.sin(angle)
    rope = np.stack([np.concatenate([cos, cos], 1), np.concatenate([-sin, sin], 1)], 1)
    rope = rope.reshape(TB, P, 2, HD).transpose(1, 0, 2, 3)
    return consts, select.reshape(2 * E, NCOMB * P), np.ascontiguousarray(rope, np.float32)


def kernel(**inputs):
    import numpy as np
    import concourse.bacc as bacc
    from concourse.bass_utils import run_bass_kernel_spmd

    a = {k: np.asarray(v) for k, v in inputs.items()}

    def by_column(v):
        return v.reshape(-1, P).T

    def rows(v):
        return np.broadcast_to(v, (P, v.shape[0]))

    consts, select, rope = _constants()
    params = np.concatenate([
        by_column(a["L0_attn_norm_scale"]),
        a["L0_attn_conv_weight"].reshape(TAPS, NCH, P).transpose(2, 1, 0).reshape(P, NCH * TAPS),
        by_column(a["L0_attn_conv_bias"]), by_column(a["L0_attn_D"]),
        rows(a["L0_attn_dt_bias"]), rows(a["L0_attn_A_log"]),
        by_column(a["L1_ffn_gamma"]), by_column(a["L1_ffn_beta"]), by_column(a["L1_ffn_bias"]), by_column(a["L1_ffn_alpha"]),
        a["L0_ffn_gate_w"].reshape(E, KC, P).transpose(2, 1, 0).reshape(P, KC * E)], 1)
    fc = [a[f"L0_ffn_fc{i}_w"].reshape(E, I, KC, P) for i in (1, 2)]
    pj = a["L0_ffn_proj_w"].transpose(0, 2, 1)

    def chunks(f, n):
        return f.reshape(n, P, KC, P).transpose(0, 3, 2, 1).reshape(n, P, C)

    cut = FULL * P
    w_moe = np.concatenate([chunks(f[:, :cut], E * FULL) for f in fc] + [pj[:, :cut].reshape(E * FULL, P, C)], 2)
    w_tail = np.concatenate([chunks(f[:, cut:], NTAIL) for f in fc] + [pj[:, cut:].reshape(NTAIL, P, C)], 2)
    wq = a["L1_attn_Wq"].reshape(KVH, GQ * HD, KC, P)
    wk, wv = (a[f"L1_attn_{n}"].reshape(KVH, HD, KC, P) for n in ("Wk", "Wv"))
    w_qkv = np.concatenate([wq, wk, wv], 1).transpose(0, 3, 2, 1)
    w_o = a["L1_attn_Wo"].reshape(C, KVH, 2, P).transpose(1, 3, 2, 0)
    sent = {
        "x": a["L0_attn_x"].reshape(T, C), "params": params, "consts": consts, "select": select, "rope": rope,
        "w_in": a["L0_attn_in_proj_w"].reshape(KC, P, PROJ).transpose(1, 0, 2),
        "w_out": a["L0_attn_out_proj_w"].reshape(NCH, P, C).transpose(1, 0, 2),
        "w_moe": w_moe, "w_moe_tail": w_tail, "w_qkv": w_qkv, "w_o": w_o,
        "w_sign": a["L1_ffn_weight"].reshape(KC, P, C).transpose(1, 0, 2),
    }
    sent = {f"in_{k}": np.ascontiguousarray(v) for k, v in sent.items()}
    nc = bacc.Bacc("TRN2", target_bir_lowering=False, num_devices=1)
    args = [nc.dram_tensor(k, v.shape, mybir.dt.from_np(v.dtype), kind="ExternalInput").ap() for k, v in sent.items()]
    args.append(nc.dram_tensor("out_x", (T, C), F32, kind="ExternalOutput").ap())
    layered_kernel(nc, *args)
    r = run_bass_kernel_spmd(nc, [sent], core_ids=[0])
    return r.results[0]["out_x"].reshape(BATCH, SEQ, C)
```

```python
import concourse.bass as bass
from concourse import mybir
from contextlib import ExitStack

F32 = mybir.dt.float32
F32R = mybir.dt.float32r
BF16 = mybir.dt.bfloat16
U32 = mybir.dt.uint32

P = 128
BATCH, SEQ, C = 2, 512, 256
T = BATCH * SEQ
NT = T // P
TB = SEQ // P
KC = C // P
HALF = SEQ
DI, NH = 512, 4
NCH = DI // P
PROJ = 2 * DI + NH + 2 * P
DT0 = 2 * DI
B0, C0 = DT0 + NH, DT0 + NH + P
TAPS = 4
E, I = 8, 704
FULL = I // P
TAIL = I - FULL * P
NTAIL = E * TAIL // P
WM = 3 * C
FC2, PJ = C, 2 * C
H, KVH, HD = 32, 8, 64
GQ = H // KVH
GW = GQ * HD + 2 * HD
NR = GQ + 1
PAIRS = BATCH * GQ // 2
NCOL = P * TB * (TB + 1) // 2
PARAMS = {}
_at = 0
for _n, _k in (("norm_scale", KC), ("conv_w", NCH * TAPS), ("conv_b", NCH), ("D", NCH), ("dt_bias", NH),
               ("A_log", NH), ("gamma", KC), ("beta", KC), ("bias", KC), ("alpha", KC), ("gate_w", KC * E)):
    PARAMS[_n] = (_at, _k)
    _at += _k
NPARAM = _at
NCONST = 3 * P + E
NCOMB = E + NTAIL
MASKED = -1e30
PROJS = [("ssm", m) for m in range(NCH)] + [("B", 0), ("C", 0)] + [("gate", m) for m in range(NCH)]
POFF = [P * j * (j + 1) // 2 for j in range(TB)]
SCORES = [[(0, 3, 0)], [(0, 2, 0), (0, 0, 3 * P)], [(0, 1, 0), (1, 1, 2 * P)], [(1, 3, 0)], [(1, 2, 0), (1, 0, 3 * P)]]
MASKS = [(3 * P, 3 * P), (2 * P, 2 * P), (P, 0), (3 * P, 3 * P), (2 * P, 2 * P)]
HEADS_AT = (3, 5)
TURNED = [[(0, 0, 0)], [(0, 1, 0), (0, 3, 3 * P)], [(1, 0, 0)], [(1, 1, 0), (1, 3, 3 * P)], [(0, 2, 0), (1, 2, 2 * P)]]
STEPS = 5 * PAIRS
LAG = 6
TO_V = 2


def schedule(last, this, prep_last, prep):
    ready = [(0, 1, "VQ", 0, 0)]
    for t in range(NT):
        n = 2 * t + STEPS - 2 * NT + 1
        ready += [(n, 8, "Q", t, 0), (n + 2, 6, "R", t, 0), (n + 4, 6.5, "X", t, 0), (n + 5, 6.5, "X", t, 1)]
    own = [(13, 0, "VO", 0, 0)]
    for r in range(PAIRS):
        for k in range(5):
            n = 5 * r + k
            own += [(n, 2, "S", r, k), (n, 4, "E", r, k), (n + LAG, 3, "T", r, k), (n + LAG + TO_V, 5, "A", r, k)]
        for h in range(2):
            own += [(5 * r + HEADS_AT[h], 5, "N", r, h)]
        own += [(5 * r + 4 + LAG + TO_V + 1, 1, "O", r, 0)]
    for b in range(BATCH):
        for m in range(KC):
            own += [(5 * (2 * b + 1) + 4 + LAG + TO_V + 3 + 2 * m, 7, "W", b * KC + m, 0)]
    picked = [(n - late * STEPS, p, late, op, i, k)
              for at, late, wanted in ((own, True, last), (ready, True, prep_last), (own, False, this), (ready, False, prep))
              for n, p, op, i, k in at if wanted and (n >= STEPS) == late]
    return [z[2:] for z in sorted(picked, key=lambda z: z[:2])]


PREP = []
for _late, _op, _i, _k in schedule(False, False, False, True):
    PREP += [(_op, _i, _k)] + ([("F", _i, 0)] if _op == "Q" and _i < 6 else [])
TAKEN_EARLY = sum(z[0] == "X" for z in PREP)
LATE_W = sum(z[1] == "W" for z in schedule(True, False, False, False))


def layered_kernel(nc, x, params, consts, select, rope, w_in, w_out, w_moe, w_moe_tail, w_qkv, w_o, w_sign, out):
    ALU = mybir.AluOpType
    ACT = mybir.ActivationFunctionType
    AX = mybir.AxisListType
    ctx = ExitStack()
    with ctx:
        def sem(name):
            return ctx.enter_context(nc.semaphore(name))

        def sb(name, shape, dt=F32, scope=ctx):
            return scope.enter_context(nc.sbuf_tensor(name, shape, dt))

        bank = [ctx.enter_context(nc.psum_tensor(f"bank{i}", [P, HALF], F32)) for i in range(8)]

        cst = sb("cst", [P, NCONST])
        ident, upto, after = cst[:, 0:P], cst[:, P:2 * P], cst[:, 2 * P:3 * P]
        expert_no = cst[:, 3 * P:3 * P + E]
        ones = sb("ones", [P, P])
        par = sb("par", [P, NPARAM])
        x_tok = sb("x_tok", [P, NT, C])
        xnT = sb("xnT", [P, KC, T])
        xnT_hi = sb("xnT_hi", [P, KC, T], F32R)
        xnT_lo = sb("xnT_lo", [P, KC, T], F32R)
        sT = sb("sT", [P, KC, T])
        stats = sb("stats", [P, NT, 6])
        mv = sb("mv", [P, NT, 2])
        sv = sb("sv", [P, 10, NT])

        def col(name, i=0):
            return par[:, PARAMS[name][0] + i:PARAMS[name][0] + i + 1]

        def cols(name):
            return par[:, PARAMS[name][0]:PARAMS[name][0] + PARAMS[name][1]]

        s1 = ExitStack()
        w_in_sb = sb("w_in_sb", [P, KC, PROJ], F32, s1)
        w_in_hi = sb("w_in_hi", [P, KC, PROJ], F32R, s1)
        w_in_lo = sb("w_in_lo", [P, KC, PROJ], F32R, s1)
        w_out_sb = sb("w_out_sb", [P, NCH, C], F32, s1)
        w_out_hi = sb("w_out_hi", [P, NCH, C], F32R, s1)
        w_out_lo = sb("w_out_lo", [P, NCH, C], F32R, s1)
        xs = sb("xs", [P, NCH, T], F32, s1)
        norm_tok = xs[:, :, :].rearrange("p a (b c) -> p (a b) c", c=C)
        xn_tok, h_tok = norm_tok[:, 0:NT, :], norm_tok[:, NT:2 * NT, :]
        hT = sT
        y_hi = sb("y_hi", [P, NCH, T], F32R, s1)
        y_lo = sb("y_lo", [P, NCH, T], F32R, s1)
        hT_hi, hT_lo = y_hi[:, 0:KC, :], y_lo[:, 0:KC, :]
        ssm = sb("ssm", [P, NCH, TAPS - 1 + SEQ], F32, s1)
        gate = sb("gate", [P, NCH, T], F32, s1)
        BT = sb("BT", [P, T], F32, s1)
        CT = sb("CT", [P, T], F32, s1)
        dtB = sb("dtB", [P, NT, NH + P], F32, s1)
        dts = sb("dts", [P, 8, NT, NH], F32, s1)
        a_neg = sb("a_neg", [P, NH], F32, s1)
        decay_in = sb("decay_in", [P, NH, P], F32, s1)
        within = sb("within", [P, NH, P], F32, s1)
        since = sb("since", [P, NH, P], F32, s1)
        cbm = sb("cbm", [P, P], F32, s1)
        mix = sb("mix", [P, NH, P], F32, s1)
        c_dec = sb("c_dec", [P, NH, P], F32, s1)
        x_t = sb("x_t", [P, NH, P], F32, s1)
        x_dt = sb("x_dt", [P, NH, P], F32, s1)
        x_end = sb("x_end", [P, NH, P], F32, s1)
        w_end = sb("w_end", [P, NH], F32, s1)
        state = sb("state", [P, NH, P], F32, s1)
        dx = sb("dx", [P, NCH, P], F32, s1)
        s1.close()

        s2 = ExitStack()
        sel = sb("sel", [2 * E, NCOMB * P], F32, s2)
        sel_r = sb("sel_r", [2 * E, NCOMB * P], F32R, s2)
        wraw = sb("wraw", [P, FULL, WM], F32, s2)
        w_hi = sb("w_hi", [P, FULL, WM], F32R, s2)
        w_lo = sb("w_lo", [P, FULL, WM], F32R, s2)
        comb = sb("comb", [P, NCOMB, T], F32, s2)
        route = sb("route", [P, NT, E], F32, s2)
        top = sb("top", [P, NT, E], F32, s2)
        topi = sb("topi", [P, NT, E], U32, s2)
        topf = sb("topf", [P, NT, 2], F32, s2)
        pr = sb("pr", [P, 6, NT], F32, s2)
        onehot = sb("onehot", [P, NT, 2, E], F32, s2)
        cmb = sb("cmb", [P, NT, E], F32, s2)
        cmb_hl = sb("cmb_hl", [P, NT, 2 * E], F32, s2)
        cmb_h = sb("cmb_h", [P, NT, E], F32R, s2)
        combT = sb("combT", [2 * E, T], F32R, s2)
        zero_b = sb("zero_b", [P, HALF], BF16, s2)
        act_s = sb("act_s", [P, 2, HALF], F32, s2)
        act_c = sb("act_c", [P, 2, HALF], F32, s2)
        act_h = sb("act_h", [P, 2, HALF], F32, s2)
        h_hi = sb("h_hi", [P, 2, HALF], F32R, s2)
        h_lo = sb("h_lo", [P, 2, HALF], F32R, s2)
        gT = sb("gT", [P, KC, T], F32, s2)
        s2.close()

        s3 = ExitStack()
        prob = sb("prob", [P, 2, 2, NCOL], F32, s3)
        before = prob[:, :, :, :].rearrange("p s h n -> p (s h n)")
        xn1 = before[:, 0:NT * C].rearrange("p (t c) -> p t c", c=C)
        xn2 = before[:, NT * C:2 * NT * C].rearrange("p (t c) -> p t c", c=C)
        wsg = before[:, 2 * NT * C:2 * NT * C + KC * C].rearrange("p (k c) -> p k c", c=C)
        wcen = before[:, 2 * NT * C + KC * C:2 * NT * C + 2 * KC * C].rearrange("p (k c) -> p k c", c=C)
        signT = sb("signT", [P, KC, T], BF16, s3)
        g1T = xnT
        wst = sb("wst", [P, KC, 4], F32, s3)
        wsT = sb("wsT", [P, KC, C], BF16, s3)
        ab = sb("ab", [P, KC], F32, s3)
        rp = sb("rp", [P, TB, 2, HD], F32, s3)
        id_b = sb("id_b", [P, 4 * P], BF16, s3)
        mask_b = sb("mask_b", [P, P], BF16, s3)
        qkv_raw = sb("qkv_raw", [P, KC, GW], F32, s3)
        qkv_hi = sb("qkv_hi", [P, KC, GW], F32R, s3)
        qkv_lo = sb("qkv_lo", [P, KC, GW], F32R, s3)
        wo_raw = sb("wo_raw", [P, 2, C], F32, s3)
        wo_hi = sb("wo_hi", [P, 2, C], F32R, s3)
        wo_lo = sb("wo_lo", [P, 2, C], F32R, s3)
        id_r = sb("id_r", [P, P], F32R, s3)
        rot = sb("rot", [P, 2, NR, HD], F32, s3)
        qkr = sb("qkr", [P, 2, NR, HD], F32, s3)
        qk_hl = sb("qk_hl", [P, 2, NR + 1, 2, HD], F32R, s3)
        qT = sb("qT", [P, 2, GQ, T], F32R, s3)
        kT = sb("kT", [P, 2, 2, T], F32R, s3)
        v_hi = sb("v_hi", [P, 2, NT, 3 * HD], F32R, s3)
        v_lo = sb("v_lo", [P, 2, NT, 3 * HD], F32R, s3)
        nmax = sb("nmax", [P, 2, 2, TB], F32, s3)
        rsum = sb("rsum", [P, 2, 2, TB], F32, s3)
        rinv = sb("rinv", [P, 2, 2, TB], F32, s3)
        p_hi = sb("p_hi", [P, 4, HALF], F32R, s3)
        p_lo = sb("p_lo", [P, 4, HALF], F32R, s3)
        o_hi = sb("o_hi", [P, 2, 2, HALF], F32R, s3)
        o_lo = sb("o_lo", [P, 2, 2, HALF], F32R, s3)
        s3.close()

        x_in = [sem(f"x_in{b}") for b in range(BATCH)]
        par_in, cst_in, w_in_in, w_out_in, sel_in = (sem(n) for n in ("par_in", "cst_in", "w_in_in", "w_out_in", "sel_in"))
        wsg_in, rope_in = sem("wsg_in"), sem("rope_in")
        slot_in = [sem(f"slot_in{i}") for i in range(FULL)]
        qkv_in, wo_in = sem("qkv_in"), sem("wo_in")
        out_done = sem("out_done")
        phase_done = sem("phase_done")
        vstep = sem("vstep")
        gstep = sem("gstep")
        astep = sem("astep")
        var_ready, root_ready = sem("var_ready"), sem("root_ready")
        scale_ready = sem("scale_ready")
        xn_ready, h_ready = sem("xn_ready"), sem("h_ready")
        tr_full, tr_taken = sem("tr_full"), sem("tr_taken")
        hi_done, lo_done = sem("hi_done"), sem("lo_done")
        ones_ready = sem("ones_ready")
        w_in_ready, w_out_hi_done, w_out_ready = sem("w_in_ready"), sem("w_out_hi_done"), sem("w_out_ready")
        w_in_hi_done = sem("w_in_hi_done")
        dtb_full, dtb_taken = sem("dtb_full"), sem("dtb_taken")
        pr_full, pr_taken = sem("pr_full"), sem("pr_taken")
        ssm_in, conv_start, conv_done, xs_ready = sem("ssm_in"), sem("conv_start"), sem("conv_done"), sem("xs_ready")
        gate_ready = sem("gate_ready")
        e_in, e_out = sem("e_in"), sem("e_out")
        dt_ready, decay_ready = sem("dt_ready"), sem("decay_ready")
        decay_full, cb_full, xt_full = sem("decay_full"), sem("cb_full"), sem("xt_full")
        exps_ready = sem("exps_ready")
        xt_ready, mix_ready, cdec_ready, xend_ready, cbm_ready = (sem(n) for n in ("xt_ready", "mix_ready", "cdec_ready", "xend_ready", "cbm_ready"))
        y_full, state_full, state_dec, state_ready, dx_ready, y_ready = (sem(n) for n in ("y_full", "state_full", "state_dec", "state_ready", "dx_ready", "y_ready"))
        y_hi_done, y_lo_done, s_full, s_part = sem("y_hi_done"), sem("y_lo_done"), sem("s_full"), sem("s_part")
        sel_ready, route_full, comb_ready, combt_full, combt_ready, spread_full, spread_taken = (sem(n) for n in (
            "sel_ready", "route_full", "comb_ready", "combt_full", "combt_ready", "spread_full", "spread_taken"))
        diff_ready, e2_ready = sem("diff_ready"), sem("e2_ready")
        whi_done, wlo_done, wslot_free = sem("whi_done"), sem("wlo_done"), sem("wslot_free")
        zero_ready = sem("zero_ready")
        ab_full, silu_done, weighted, h_made, hhi_done, hlo_done, hslot_free = (sem(n) for n in (
            "ab_full", "silu_done", "weighted", "h_made", "hhi_done", "hlo_done", "hslot_free"))
        moe_full, g_ready, sg_ready, back_full, x_ready = sem("moe_full"), sem("g_ready"), sem("sg_ready"), sem("back_full"), sem("x_ready")

        stat_ready, aggr_ready, pad_ready, az_ready, z_ready, u_ready, lg_ready, xdt_ready = (sem(n) for n in (
            "stat_ready", "aggr_ready", "pad_ready", "az_ready", "z_ready", "u_ready", "lg_ready", "xdt_ready"))
        silu_seen, top_ready, topi_ready, spread_a, spread_v = (sem(n) for n in ("silu_seen", "top_ready", "topi_ready", "spread_a", "spread_v"))
        wcen_ready, wsign_ready, wsT_full, wsT_ready, sign_ready, sign_full, ab_ready, g1_ready, mask_ready, vpad_ready = (
            sem(n) for n in ("wcen_ready", "wsign_ready", "wsT_full", "wsT_ready", "sign_ready", "sign_full", "ab_ready",
                             "g1_ready", "mask_ready", "vpad_ready"))
        qkvhi_done, qkvlo_done, wohi_done, wolo_done, qkv_full, qk_copied, b6_free, turned, rope_done = (sem(n) for n in (
            "qkvhi_done", "qkvlo_done", "wohi_done", "wolo_done", "qkv_full", "qk_copied", "b6_free", "turned", "rope_done"))
        qkhi_done, qklo_done, tq_full, tq_taken = (sem(n) for n in ("qkhi_done", "qklo_done", "tq_full", "tq_taken"))
        score_full, max_ready, exp_done, rinv_ready, prob_ready, pt_full, phi_done, plo_done, av_done = (sem(n) for n in (
            "score_full", "max_ready", "exp_done", "rinv_ready", "prob_ready", "pt_full", "phi_done", "plo_done", "av_done"))
        ohi_done, olo_done, wo_full = sem("ohi_done"), sem("olo_done"), sem("wo_full")

        ends = {}

        def end_phase(eng):
            k = ends[eng.engine] = ends.get(eng.engine, 0) + 1
            eng.drain().then_inc(phase_done, 1)
            eng.wait_ge(phase_done, 5 * k)

        def stepper(eng, signal):
            n = [0]

            def then(ins):
                n[0] += 1
                ins.then_inc(signal, 1)
                eng.wait_ge(signal, n[0])
            return then

        vec = nc.vector
        TT, TS, STT = vec.tensor_tensor, vec.tensor_scalar, vec.scalar_tensor_tensor
        pool = nc.gpsimd
        mm = nc.tensor.matmul

        block = ctx.enter_context(nc.Block())

        @block.sync
        def _(sp):
            xv = x.rearrange("(t p) c -> p t c", p=P)
            sp.dma_start(x_tok[:, 0:TB, :], xv[:, 0:TB, :]).then_inc(x_in[0], 16)
            sp.dma_start(x_tok[:, TB:NT, :], xv[:, TB:NT, :]).then_inc(x_in[1], 16)
            sp.dma_start(cst[:, :], consts).then_inc(cst_in, 16)
            sp.dma_start(par[:, :], params).then_inc(par_in, 16)
            sp.dma_start(w_in_sb[:, :, :], w_in).then_inc(w_in_in, 16)
            sp.dma_start(w_out_sb[:, :, :], w_out).then_inc(w_out_in, 16)
            end_phase(sp)
            sp.dma_start(sel[:, :], select).then_inc(sel_in, 16)
            for i in range(FULL):
                sp.dma_start(wraw[:, i, :], w_moe[i, :, :]).then_inc(slot_in[i], 16)
            wv = w_moe.rearrange("(e i) p n -> e i p n", i=FULL)
            with sp.Fori(0, E - 1) as e:
                for i in range(FULL):
                    sp.wait_ge(wlo_done, e * FULL + (i + 1))
                    sp.dma_start(wraw[:, i, :], wv[bass.ds(e + 1, 1), i, :, :].rearrange("a p n -> (a p) n")).then_inc(slot_in[i], 16)
            for i in range(NTAIL):
                sp.wait_ge(wlo_done, (E - 1) * FULL + i + 1)
                sp.dma_start(wraw[:, i, :], w_moe_tail[i, :, :]).then_inc(slot_in[i], 16)
            end_phase(sp)
            sp.dma_start(wsg[:, :, :], w_sign).then_inc(wsg_in, 16)
            sp.dma_start(qkv_raw[:, :, :], w_qkv[0, :, :, :]).then_inc(qkv_in, 16)
            sp.dma_start(rp[:, :, :, :], rope).then_inc(rope_in, 16)
            sp.dma_start(wo_raw[:, :, :], w_o[0, :, :, :]).then_inc(wo_in, 16)
            with sp.Fori(0, KVH - 1) as g:
                sp.wait_ge(qkvlo_done, g + 1)
                sp.dma_start(qkv_raw[:, :, :], w_qkv[bass.ds(g + 1, 1), :, :, :].rearrange("a p k n -> (a p) k n")).then_inc(qkv_in, 16)
                sp.wait_ge(wolo_done, g + 1)
                sp.dma_start(wo_raw[:, :, :], w_o[bass.ds(g + 1, 1), :, :, :].rearrange("a p k n -> (a p) k n")).then_inc(wo_in, 16)
            sp.wait_ge(x_ready, 2 * NT // 2)
            sp.dma_start(out.rearrange("(t p) c -> p t c", p=P), x_tok[:, :, :]).then_inc(out_done, 16)
            sp.wait_ge(out_done, 16)

        @block.vector
        def _(dve):
            then = stepper(dve, vstep)

            def norm_stats(src, ready=None):
                for t in range(NT):
                    if ready:
                        ready(t)
                    ins = vec.bn_stats(stats[:, t, :], src[:, t, :])
                    ins.then_inc(stat_ready, 1)
                dve.wait_ge(stat_ready, NT * norms[0] + NT)
                for t in range(NT):
                    ins = vec.bn_aggr(mv[:, t, :], stats[:, t, :])
                    ins.then_inc(aggr_ready, 1)
                dve.wait_ge(aggr_ready, NT * norms[0] + NT)
                norms[0] += 1

            norms = [0]
            roots = [0]

            def rsqrt_asked(src, eps):
                TS(root_arg, src, eps, None, ALU.add).then_inc(var_ready, 1)

            def rsqrt_made(dst):
                roots[0] += 1
                dve.wait_ge(root_ready, roots[0])
                then(vec.reciprocal(dst, root))
                then(TT(sv[:, 3, :], root_arg, dst, ALU.mult))
                then(TT(sv[:, 3, :], sv[:, 3, :], dst, ALU.mult))
                then(TS(sv[:, 3, :], sv[:, 3, :], -0.5, 1.5, ALU.mult, ALU.add))
                then(TT(dst, dst, sv[:, 3, :], ALU.mult))

            def rsqrt(dst, src, eps):
                rsqrt_asked(src, eps)
                rsqrt_made(dst)

            root_arg, root = sv[:, 0, :], sv[:, 2, :]
            rstd, rrms = sv[:, 4, :], sv[:, 5, :]

            vec.memset(ones[:, :], 1.0).then_inc(ones_ready, 1)
            vec.memset(ssm[:, :, 0:TAPS - 1], 0.0).then_inc(pad_ready, 1)
            norm_stats(x_tok, lambda t: dve.wait_ge(x_in[t // TB], 16))
            rsqrt(rstd, mv[:, :, 1], 1e-5)
            then(TT(sv[:, 6, :], mv[:, :, 1], rstd, ALU.mult))
            then(TT(sv[:, 6, :], sv[:, 6, :], rstd, ALU.mult))
            for t in range(NT):
                TS(xn_tok[:, t, :], x_tok[:, t, :], mv[:, t, 0:1], rstd[:, t:t + 1], ALU.subtract, ALU.mult).then_inc(xn_ready, 1)
            rsqrt(rrms, sv[:, 6, :], 1e-6)
            dve.wait_ge(xn_ready, NT)
            for t in range(NT):
                TS(h_tok[:, t, :], xn_tok[:, t, :], rrms[:, t:t + 1], None, ALU.mult).then_inc(h_ready, 1)
            for k in range(2 * KC * BATCH):
                b, c = k // KC % BATCH, k % KC
                cs = slice(b * HALF, (b + 1) * HALF)
                dve.wait_ge(hi_done, k + 1)
                if k < KC * BATCH:
                    TT(xnT_lo[:, c, cs], bank[k][:, :], xnT_hi[:, c, cs].bitcast(F32), ALU.subtract).then_inc(lo_done, 1)
                else:
                    TT(hT_lo[:, c, cs], hT[:, c, cs], hT_hi[:, c, cs].bitcast(F32), ALU.subtract).then_inc(lo_done, 1)
            for t in range(NT):
                dve.wait_ge(dtb_full, t + 1)
                vec.tensor_copy(dtB[:, t, :], bank[t % 2][:, 0:NH + P]).then_inc(dtb_taken, 1)
            dve.wait_ge(dtb_taken, NT)
            dve.wait_ge(par_in, 16)
            v, az, z, u, d, lg = (dts[:, i, :, :] for i in range(6))
            dt, la = dts[:, 6, :, :], dts[:, 7, :, :]
            then(TT(v, dtB[:, :, 0:NH], cols("dt_bias").unsqueeze(1).to_broadcast([P, NT, NH]), ALU.add))
            then(TS(az, v, -1.0, None, ALU.mult))
            TT(az, az, v, ALU.min).then_inc(az_ready, 1)
            dve.wait_ge(z_ready, 1)
            then(TS(u, z, 1.0, None, ALU.add))
            TS(d, u, -1.0, None, ALU.add).then_inc(u_ready, 1)
            dve.wait_ge(lg_ready, 1)
            dve.wait_ge(u_ready, 1)
            then(TS(az, d, 0.0, None, ALU.is_equal))
            then(TT(d, d, az, ALU.add))
            then(TT(lg, lg, az, ALU.add))
            then(TT(lg, lg, z, ALU.mult))
            then(vec.reciprocal(u, d))
            then(TT(lg, lg, u, ALU.mult))
            then(TS(v, v, 0.0, None, ALU.max))
            then(TT(dt, v, lg, ALU.add))
            dve.wait_ge(astep, 1)
            then(TS(a_neg[:, :], a_neg[:, :], -1.0, None, ALU.mult))
            TT(la, dt, a_neg[:, :].unsqueeze(1).to_broadcast([P, NT, NH]), ALU.mult).then_inc(dt_ready, 1)
            for b in range(BATCH):
                for m in range(NCH):
                    n = b * NCH + m
                    cs = slice(b * HALF, (b + 1) * HALF)
                    dve.wait_ge(conv_start, n + 1)
                    if n == 0:
                        dve.wait_ge(pad_ready, 1)
                    for j in range(TAPS - 1):
                        ins = STT(out=xs[:, m, cs], in0=ssm[:, m, j:j + SEQ], scalar=col("conv_w", m * TAPS + j),
                                  in1=xs[:, m, cs], op0=ALU.mult, op1=ALU.add)
                        ins.then_inc(conv_done, 1)
                        dve.wait_ge(conv_done, (TAPS - 1) * n + j + 1)
            def lower_y(c):
                ts = slice(c * P, (c + 1) * P)
                dve.wait_ge(y_hi_done, c + 1)
                TT(y_lo[:, :, ts], gate[:, :, ts], y_hi[:, :, ts].bitcast(F32), ALU.subtract).then_inc(y_lo_done, 1)

            def residual(b):
                cs = slice(b * HALF, (b + 1) * HALF)
                for m in range(KC):
                    dve.wait_ge(s_full, b * KC + m + 1)
                    TT(sT[:, m, cs], bank[6 + m][:, :], xnT[:, m, cs], ALU.add).then_inc(s_part, 1)

            for c in range(NT):
                ts = slice(c * P, (c + 1) * P)
                dve.wait_ge(cb_full, c + 1)
                if c:
                    dve.wait_ge(mix_ready, c)
                TT(cbm[:, :], bank[2][:, 0:P], upto, ALU.mult).then_inc(cbm_ready, 1)
                dve.wait_ge(exps_ready, c + 1)
                dve.wait_ge(dt_ready, 1)
                if c:
                    dve.wait_ge(state_full, c)
                then(TT(w_end[:, :], dt[:, c, :], within[:, :, P - 1], ALU.mult))
                dve.wait_ge(xt_full, c + 1)
                xt = bank[3][:, :].rearrange("p (h q) -> p h q", h=NH)
                TT(x_dt[:, :, :], xt, dt[:, c, :].unsqueeze(2).to_broadcast([P, NH, P]), ALU.mult).then_inc(xdt_ready, 1)
                TT(x_end[:, :, :], xt, w_end[:, :].unsqueeze(2).to_broadcast([P, NH, P]), ALU.mult).then_inc(xend_ready, 1)
                dve.wait_ge(y_full, c + 1)
                dve.wait_ge(dx_ready, c + 1)
                yv = bank[4][:, :].rearrange("p (h q) -> p h q", h=NH)
                then(TT(dx[:, :, :], yv, dx[:, :, :], ALU.add))
                TT(gate[:, :, ts], dx[:, :, :], gate[:, :, ts], ALU.mult).then_inc(y_ready, 1)
                dve.wait_ge(state_full, c + 1)
                sv_ = bank[5][:, :].rearrange("p (h q) -> p h q", h=NH)
                if c % TB == 0:
                    vec.tensor_copy(state[:, :, :], sv_).then_inc(state_ready, 1)
                else:
                    dve.wait_ge(state_dec, c - c // TB)
                    TT(state[:, :, :], state[:, :, :], sv_, ALU.add).then_inc(state_ready, 1)
                if c:
                    lower_y(c - 1)
                if c == TB:
                    residual(0)
            lower_y(NT - 1)
            residual(1)
            end_phase(dve)

            vec.memset(zero_b[:, :], 0.0).then_inc(zero_ready, 1)
            dve.wait_ge(route_full, 1)
            then(vec.tensor_copy(route[:, :, :], bank[0][:, 0:NT * E].rearrange("p (t e) -> p t e", e=E)))
            for t in range(NT):
                vec.max(top[:, t, :], route[:, t, :]).then_inc(top_ready, 1)
            dve.wait_ge(top_ready, NT)
            for t in range(NT):
                vec.max_index(topi[:, t, :], top[:, t, :], route[:, t, :]).then_inc(topi_ready, 1)
            dve.wait_ge(topi_ready, NT)
            TT(pr[:, 0, :], top[:, :, 1], top[:, :, 0], ALU.subtract).then_inc(diff_ready, 1)
            then(vec.tensor_copy(topf[:, :, :], topi[:, :, 0:2]))
            for k in range(2):
                then(TT(onehot[:, :, k, :], expert_no.unsqueeze(1).to_broadcast([P, NT, E]),
                        topf[:, :, k].unsqueeze(2).to_broadcast([P, NT, E]), ALU.is_equal))
            dve.wait_ge(e2_ready, 1)
            then(TS(pr[:, 2, :], pr[:, 1, :], 1.0, None, ALU.add))
            then(vec.reciprocal(pr[:, 3, :], pr[:, 2, :]))
            then(TT(pr[:, 4, :], pr[:, 1, :], pr[:, 3, :], ALU.mult))
            for k in range(2):
                then(TT(onehot[:, :, k, :], onehot[:, :, k, :],
                        pr[:, 3 + k, :].unsqueeze(2).to_broadcast([P, NT, E]), ALU.mult))
            then(TT(cmb[:, :, :], onehot[:, :, 0, :], onehot[:, :, 1, :], ALU.add))
            then(vec.tensor_copy(cmb_h[:, :, :], cmb[:, :, :]))
            then(vec.tensor_copy(cmb_hl[:, :, 0:E], cmb_h[:, :, :].bitcast(F32)))
            TT(cmb_hl[:, :, E:2 * E], cmb[:, :, :], cmb_h[:, :, :].bitcast(F32), ALU.subtract).then_inc(comb_ready, 1)
            for n in range(1, 2 * NCOMB, 2):
                dve.wait_ge(spread_full, n + 1)
                vec.tensor_copy(comb[:, n // 2, HALF:T], bank[n % 4][:, :]).then_inc(spread_v, 1)

            def expert(e, chunks):
                for i in range(chunks):
                    for s in range(2):
                        u = e * (2 * FULL) + (2 * i + s)
                        dve.wait_ge(ab_full, u + 1)
                        dve.wait_ge(weighted, u + 1)
                        TT(act_h[:, s, :], act_c[:, s, :], bank[2 + s][:, :], ALU.mult).then_inc(h_made, 1)
                        dve.wait_ge(hhi_done, u + 1)
                        TT(h_lo[:, s, :], act_h[:, s, :], h_hi[:, s, :].bitcast(F32), ALU.subtract).then_inc(hlo_done, 1)

            with dve.Fori(0, E) as e:
                expert(e, FULL)
            expert(E, NTAIL)
            for n in range(KC * BATCH):
                m, s = n // 2, n % 2
                cs = slice(s * HALF, (s + 1) * HALF)
                dve.wait_ge(g_ready, n + 1)
                TT(sT[:, m, cs], sT[:, m, cs], gT[:, m, cs], ALU.mult).then_inc(sg_ready, 1)
            for n in range(NT // 2):
                dve.wait_ge(back_full, n + 1)
                xt2 = x_tok[:, 2 * n:2 * n + 2, :]
                TT(xt2, xt2, bank[n][:, :].rearrange("p (t c) -> p t c", c=C), ALU.add).then_inc(x_ready, 1)
            end_phase(dve)

            norm_stats(x_tok)
            rsqrt(rstd, mv[:, :, 1], 1e-5)
            for t in range(NT):
                TS(xn1[:, t, :], x_tok[:, t, :], mv[:, t, 0:1], rstd[:, t:t + 1], ALU.subtract, ALU.mult).then_inc(xn_ready, 1)
            for k in range(KC * BATCH):
                b, c = k // KC, k % KC
                cs = slice(b * HALF, (b + 1) * HALF)
                dve.wait_ge(hi_done, 2 * KC * BATCH + k + 1)
                TT(xnT_lo[:, c, cs], bank[k][:, :], xnT_hi[:, c, cs].bitcast(F32), ALU.subtract).then_inc(lo_done, 1)

            def gating(part):
                if part == 0:
                    dve.wait_ge(xn_ready, 2 * NT)
                    norm_stats(xn1)
                    rsqrt_asked(mv[:, :, 1], 1e-5)
                elif part == 1:
                    rsqrt_made(rrms)
                    for t in range(NT):
                        TS(xn2[:, t, :], xn1[:, t, :], mv[:, t, 0:1], rrms[:, t:t + 1], ALU.subtract, ALU.mult).then_inc(h_ready, 1)
                elif part == 2:
                    dve.wait_ge(wsg_in, 16)
                    then(vec.reduce_sum(wst[:, :, 0:1], wsg[:, :, :], axis=AX.X))
                    then(TS(wst[:, :, 1:2], wst[:, :, 0:1], 1.0 / C, None, ALU.mult))
                    for m in range(KC):
                        TS(wcen[:, m, :], wsg[:, m, :], wst[:, m, 1:2], None, ALU.subtract).then_inc(wcen_ready, 1)
                    TT(ab[:, :], cols("alpha"), cols("bias"), ALU.mult).then_inc(ab_ready, 1)

            def prep_v(g, a, t, qk_bank):
                tt = g * NT + t
                sl, hd2 = t % 2, HD // 2
                cosv = rp[:, t % TB, 0, :].unsqueeze(1).to_broadcast([P, NR, HD])
                sinv = rp[:, t % TB, 1, :].unsqueeze(1).to_broadcast([P, NR, HD])
                qk = qk_bank[:, 0:NR * HD].rearrange("p (h d) -> p h d", d=HD)
                dve.wait_ge(qk_copied, tt + 1)
                if not isinstance(tt, int) or tt > 1:
                    dve.wait_ge(qklo_done, tt - 1)
                TT(qkr[:, sl, :, :], qk, cosv, ALU.mult)
                TT(rot[:, sl, :, 0:hd2], qk[:, :, hd2:HD], sinv[:, :, 0:hd2], ALU.mult)
                TT(rot[:, sl, :, hd2:HD], qk[:, :, 0:hd2], sinv[:, :, hd2:HD], ALU.mult).then_inc(turned, 1)
                TT(v_lo[:, a, t, HD:2 * HD], qk_bank[:, NR * HD:GW], v_hi[:, a, t, HD:2 * HD].bitcast(F32),
                   ALU.subtract).then_inc(b6_free, 1)

            def attend(now, now_set, steps):
                for late, op, i, k in steps:
                    g, a = (now - 1, 1 - now_set) if late else (now, now_set)
                    q = g * PAIRS + i
                    u = q * 5 + k
                    if op == "S":
                        bk = bank[(i + k) % 2]
                        dve.wait_ge(score_full, u + 1)
                        segs = SCORES[k]
                        if k == 2:
                            vec.tensor_reduce(out=nmax[:, i % 2, :, 1:2], in_=bk[:, :].rearrange("p (h n) -> p h n", h=2),
                                              op=ALU.max, axis=AX.X, negate=True).then_inc(max_ready, 1)
                        else:
                            for h, j, at in segs:
                                ins = vec.tensor_reduce(out=nmax[:, i % 2, h, j:j + 1], in_=bk[:, at:at + (j + 1) * P],
                                                        op=ALU.max, axis=AX.X, negate=True)
                            ins.then_inc(max_ready, 1)
                    elif op == "N":
                        dve.wait_ge(exp_done, q * 5 + (HEADS_AT[k] + 2))
                        vec.reciprocal(rinv[:, i % 2, k, :], rsum[:, i % 2, k, :]).then_inc(rinv_ready, 1)
                    elif op == "T":
                        b_ = (i + k) % 4
                        dve.wait_ge(phi_done, u + 1)
                        TT(p_lo[:, b_, :], bank[2 + b_ % 2][:, :], p_hi[:, b_, :].bitcast(F32), ALU.subtract).then_inc(plo_done, 1)
                    elif op == "O":
                        b, m = i // 2, i % 2
                        dve.wait_ge(ohi_done, q + 1)
                        TT(o_lo[:, b, m, :], bank[4 + m][:, :], o_hi[:, b, m, :].bitcast(F32), ALU.subtract).then_inc(olo_done, 1)
                    elif op == "W":
                        b, m = i // KC, i % KC
                        cs = slice(b * HALF, (b + 1) * HALF)
                        dve.wait_ge(wo_full, g * (BATCH * KC) + (i + 2))
                        TT(sT[:, m, cs], sT[:, m, cs], bank[6][:, :], ALU.add).then_inc(b6_free, 1)
                    elif op == "Q":
                        prep_v(g + 1, 1 - a, i, bank[6])

            dve.wait_ge(rope_in, 16)
            for op, i, k in PREP:
                if op == "Q":
                    prep_v(0, 0, i, bank[i % 3])
                elif op == "F":
                    gating(i)
            dve.wait_ge(vpad_ready, 5)
            attend(0, 0, schedule(False, True, True, True))
            with dve.Fori(0, KVH // 2 - 1) as gp:
                for a in range(2):
                    attend(gp * 2 + (1 + a), 1 - a, schedule(True, True, True, True))
            attend(KVH - 1, 1, schedule(True, True, True, False))
            attend(KVH, 0, schedule(True, False, False, False))
            dve.wait_ge(b6_free, NT * KVH + BATCH * KC * KVH)
            for n in range(KC * BATCH):
                m, s = n // 2, n % 2
                cs = slice(s * HALF, (s + 1) * HALF)
                dve.wait_ge(g1_ready, n + 1)
                TT(sT[:, m, cs], sT[:, m, cs], g1T[:, m, cs], ALU.mult).then_inc(sg_ready, 1)
            for n in range(NT // 2):
                dve.wait_ge(back_full, NT // 2 + n + 1)
                xt2 = x_tok[:, 2 * n:2 * n + 2, :]
                TT(xt2, xt2, bank[n][:, :].rearrange("p (t c) -> p t c", c=C), ALU.add).then_inc(x_ready, 1)

        @block.scalar
        def _(act):
            actv = nc.scalar.activation

            def root(n):
                act.wait_ge(var_ready, n + 1)
                actv(sv[:, 2, :], sv[:, 0, :], ACT.Sqrt).then_inc(root_ready, 1)

            root(0)
            root(1)
            act.wait_ge(par_in, 16)
            act.wait_ge(cst_in, 16)
            for k in range(2 * KC * BATCH):
                b, c = k // KC % BATCH, k % KC
                cs = slice(b * HALF, (b + 1) * HALF)
                act.wait_ge(tr_full, k + 1)
                if k < KC * BATCH:
                    actv(xnT[:, c, cs], bank[k][:, :], ACT.Copy)
                    actv(xnT_hi[:, c, cs], bank[k][:, :], ACT.Copy).then_inc(hi_done, 1)
                else:
                    actv(hT[:, c, cs], bank[k][:, :], ACT.Copy, scale=col("norm_scale", c))
                    actv(hT_hi[:, c, cs], bank[k][:, :], ACT.Copy, scale=col("norm_scale", c)).then_inc(hi_done, 1)
            act.wait_ge(w_in_in, 16)
            actv(w_in_hi[:, :, :], w_in_sb[:, :, :], ACT.Copy).then_inc(w_in_hi_done, 1)
            actv(a_neg[:, :], cols("A_log"), ACT.Exp).then_inc(astep, 1)
            act.wait_ge(az_ready, 1)
            actv(dts[:, 2, :, :], dts[:, 1, :, :], ACT.Exp).then_inc(z_ready, 1)
            act.wait_ge(u_ready, 1)
            actv(dts[:, 5, :, :], dts[:, 3, :, :], ACT.Ln).then_inc(lg_ready, 1)
            act.wait_ge(w_out_in, 16)
            actv(w_out_hi[:, :, :], w_out_sb[:, :, :], ACT.Copy).then_inc(w_out_hi_done, 1)
            n = 0
            for b in range(BATCH):
                cs = slice(b * HALF, (b + 1) * HALF)
                for kind, m in PROJS:
                    bk = bank[2 + n % 6]
                    act.wait_ge(pr_full, n + 1)
                    if kind == "ssm":
                        if b:
                            act.wait_ge(conv_done, (TAPS - 1) * (m + 1))
                        actv(ssm[:, m, TAPS - 1:TAPS - 1 + SEQ], bk[:, :], ACT.Copy).then_inc(ssm_in, 1)
                        actv(xs[:, m, cs], bk[:, :], ACT.Identity, scale=col("conv_w", m * TAPS + TAPS - 1),
                             bias=col("conv_b", m)).then_inc(conv_start, 1)
                    elif kind == "B":
                        actv(BT[:, cs], bk[:, :], ACT.Copy).then_inc(pr_taken, 1)
                    elif kind == "C":
                        actv(CT[:, cs], bk[:, :], ACT.Copy).then_inc(pr_taken, 1)
                    else:
                        actv(gate[:, m, cs], bk[:, :], ACT.Silu).then_inc(pr_taken, 1)
                    n += 1
                for m in range(NCH):
                    act.wait_ge(conv_done, (TAPS - 1) * (b * NCH + m + 1))
                    actv(xs[:, m, cs], xs[:, m, cs], ACT.Silu).then_inc(xs_ready, 1)
            def upper_y(c):
                ts = slice(c * P, (c + 1) * P)
                act.wait_ge(y_ready, c + 1)
                actv(y_hi[:, :, ts], gate[:, :, ts], ACT.Copy).then_inc(y_hi_done, 1)

            for c in range(NT):
                act.wait_ge(decay_full, c + 1)
                if c:
                    act.wait_ge(mix_ready, c)
                    act.wait_ge(xend_ready, c)
                actv(within[:, :, :], bank[0][:, :].rearrange("p (h q) -> p h q", h=NH), ACT.Exp)
                if c:
                    act.wait_ge(cdec_ready, c)
                    if c // TB or c % TB > 1:
                        act.wait_ge(state_dec, (c - 1) - (c - 1) // TB)
                actv(since[:, :, :], bank[1][:, :].rearrange("p (h q) -> p h q", h=NH), ACT.Exp).then_inc(exps_ready, 1)
                if c:
                    upper_y(c - 1)
            upper_y(NT - 1)
            end_phase(act)

            act.wait_ge(sel_in, 16)
            actv(sel_r[:, :], sel[:, :], ACT.Copy).then_inc(sel_ready, 1)
            act.wait_ge(diff_ready, 1)
            actv(pr[:, 1, :], pr[:, 0, :], ACT.Exp).then_inc(e2_ready, 1)
            for s in range(2):
                act.wait_ge(combt_full, s + 1)
                actv(combT[:, s * HALF:(s + 1) * HALF], bank[1 + s][0:2 * E, :], ACT.Copy).then_inc(combt_ready, 1)

            def split_hi(slot, n, arrived):
                act.wait_ge(slot_in[slot], arrived)
                act.wait_ge(hslot_free, n * 2 + 2)
                actv(w_hi[:, slot, :], wraw[:, slot, :], ACT.Copy).then_inc(whi_done, 1)

            split_hi(0, 0, 16)
            for n in range(0, 2 * NCOMB, 2):
                act.wait_ge(spread_full, n + 1)
                actv(comb[:, n // 2, 0:HALF], bank[n % 4][:, :], ACT.Copy).then_inc(spread_a, 1)
            split_hi(1, 1, 16)

            def expert(e, chunks, tail_next):
                for i in range(chunks):
                    for s in range(2):
                        u = e * (2 * FULL) + (2 * i + s)
                        act.wait_ge(ab_full, u + 1)
                        actv(act_s[:, s, :], bank[s][:, :], ACT.Silu).then_inc(silu_done, 1)
                        if s == 0 and (i + 2 < chunks or tail_next):
                            j = i + 2
                            split_hi(j % FULL, e * FULL + j, (e + (1 + j // FULL)) * 16)
                        act.wait_ge(h_made, u + 1)
                        act.wait_ge(hslot_free, u + (2 * FULL - 1))
                        actv(h_hi[:, s, :], act_h[:, s, :], ACT.Copy).then_inc(hhi_done, 1)

            with act.Fori(0, E) as e:
                expert(e, FULL, True)
            expert(E, NTAIL, False)
            act.wait_ge(hslot_free, 2 * (E * FULL + NTAIL + FULL))
            for n in range(KC * BATCH):
                m, s = n // 2, n % 2
                actv(gT[:, m, s * HALF:(s + 1) * HALF], bank[4 + n][:, :], ACT.Silu).then_inc(g_ready, 1)
            end_phase(act)

            for j in (0, 2, 3):
                actv(id_b[:, j * P:(j + 1) * P], ident, ACT.Copy)
            actv(id_b[:, P:2 * P], ident, ACT.Copy, scale=0.0).then_inc(mask_ready, 1)
            actv(mask_b[:, :], after, ACT.Copy, scale=MASKED).then_inc(mask_ready, 1)
            actv(id_r[:, :], ident, ACT.Copy).then_inc(mask_ready, 1)
            root(2)
            act.wait_ge(qkv_in, 16)
            actv(qkv_hi[:, :, :], qkv_raw[:, :, :], ACT.Copy).then_inc(qkvhi_done, 1)
            for k in range(KC * BATCH):
                b, c = k // KC, k % KC
                act.wait_ge(tr_full, 2 * KC * BATCH + k + 1)
                actv(xnT_hi[:, c, b * HALF:(b + 1) * HALF], bank[k][:, :], ACT.Copy).then_inc(hi_done, 1)

            def gating(part):
                if part == 0:
                    root(3)
                elif part == 2:
                    for m in range(KC):
                        act.wait_ge(wcen_ready, m + 1)
                        actv(wsg[:, m, :], wcen[:, m, :], ACT.Sign).then_inc(wsign_ready, 1)
                elif part == 3:
                    for k in range(KC * BATCH):
                        b, c = k // KC, k % KC
                        act.wait_ge(tr_full, 3 * KC * BATCH + k + 1)
                        actv(signT[:, c, b * HALF:(b + 1) * HALF], bank[4 + k % 3][:, :], ACT.Sign, scale=col("gamma", c),
                             bias=col("beta", c)).then_inc(sign_ready, 1)
                elif part == 4:
                    act.wait_ge(wsT_full, 1)
                    actv(wsT[:, :, :], bank[4 + KC * BATCH % 3][:, :].rearrange("p (k o) -> p k o", k=KC), ACT.Copy).then_inc(wsT_ready, 1)
                elif part == 5:
                    act.wait_ge(ab_ready, 1)
                    for n in range(KC * BATCH):
                        m, s = n // 2, n % 2
                        act.wait_ge(sign_full, n + 1)
                        actv(g1T[:, m, s * HALF:(s + 1) * HALF], bank[4 + (KC * BATCH + 1 + n) % 3][:, :], ACT.Silu,
                             scale=col("alpha", m), bias=ab[:, m:m + 1]).then_inc(g1_ready, 1)

            def weights_q(g):
                act.wait_ge(qkv_in, g * 16 + 16)
                if not isinstance(g, int) or g:
                    act.wait_ge(qkv_full, g * NT)
                actv(qkv_hi[:, :, :], qkv_raw[:, :, :], ACT.Copy).then_inc(qkvhi_done, 1)

            def prep_copy(g, a, t, qk_bank):
                tt = g * NT + t
                act.wait_ge(qkv_full, tt + 1)
                if t == 0 and not (isinstance(g, int) and g <= 1):
                    act.wait_ge(av_done, (g - 1) * STEPS + (4 - STEPS // 2))
                if t == TB and not (isinstance(g, int) and g <= 1):
                    act.wait_ge(av_done, (g - 1) * STEPS + 4)
                actv(v_hi[:, a, t, HD:2 * HD], qk_bank[:, NR * HD:GW], ACT.Copy).then_inc(qk_copied, 1)

            def prep_hi(g, t):
                tt = g * NT + t
                act.wait_ge(rope_done, tt + 1)
                if not isinstance(tt, int) or tt > 1:
                    act.wait_ge(tq_full, tt * 2 - 2)
                actv(qk_hl[:, t % 2, 0:NR, 0, :], qkr[:, t % 2, :, :], ACT.Copy)
                actv(qk_hl[:, t % 2, NR, 0, :], qkr[:, t % 2, GQ, :], ACT.Copy).then_inc(qkhi_done, 1)

            def prep_take(g, a, t, k, turn_bank):
                tt = g * NT + t
                act.wait_ge(tq_full, tt * 2 + (1 + k))
                dst = qT[:, a, :, t * P:(t + 1) * P] if k == 0 else kT[:, a, :, t * P:(t + 1) * P]
                n = GQ if k == 0 else 2
                actv(dst, turn_bank[:, 0:n * P].rearrange("p (h n) -> p h n", n=P), ACT.Copy,
                     scale=1.0 if k == 0 else HD ** -0.5).then_inc(tq_taken, 1)

            def attend(now, now_set, steps):
                for late, op, i, k in steps:
                    g, a = (now - 1, 1 - now_set) if late else (now, now_set)
                    q = g * PAIRS + i
                    u = q * 5 + k
                    if op == "E":
                        bk = bank[(i + k) % 2]
                        act.wait_ge(max_ready, u + 1)
                        if k == 0 and (not isinstance(g, int) or q > 1):
                            act.wait_ge(pt_full, q * 5 - 5)
                        for h, j, at in SCORES[k]:
                            ins = actv(prob[:, i % 2, h, POFF[j]:POFF[j] + (j + 1) * P], bk[:, at:at + (j + 1) * P], ACT.Exp,
                                       bias=nmax[:, i % 2, h, j:j + 1], accum_out=rsum[:, i % 2, h, j:j + 1])
                        ins.then_inc(exp_done, 1)
                    elif op == "T":
                        b_ = (i + k) % 4
                        act.wait_ge(pt_full, u + 1)
                        act.wait_ge(av_done, u + 1)
                        actv(p_hi[:, b_, :], bank[2 + b_ % 2][:, :], ACT.Copy).then_inc(phi_done, 1)
                    elif op == "O":
                        b, m = i // 2, i % 2
                        act.wait_ge(av_done, q * 5 + 9)
                        if m == 0 and not (isinstance(g, int) and b * KC + g * (BATCH * KC) <= 1):
                            act.wait_ge(wo_full, g * (BATCH * KC) + (b * KC - 1))
                        actv(o_hi[:, b, m, :], bank[4 + m][:, :], ACT.Copy).then_inc(ohi_done, 1)
                    elif op == "VO":
                        act.wait_ge(wo_in, g * 16 + 16)
                        act.wait_ge(wo_full, g * (BATCH * KC) + 1)
                        actv(wo_hi[:, :, :], wo_raw[:, :, :], ACT.Copy).then_inc(wohi_done, 1)
                    elif op == "VQ":
                        weights_q(g + 1)
                    elif op == "Q":
                        prep_copy(g + 1, 1 - a, i, bank[6])
                    elif op == "R":
                        prep_hi(g + 1, i)
                    elif op == "X":
                        prep_take(g + 1, 1 - a, i, k, bank[7])

            act.sem_inc(exp_done, 2)
            act.wait_ge(vpad_ready, 4)
            for op, i, k in PREP:
                if op == "Q":
                    prep_copy(0, 0, i, bank[i % 3])
                elif op == "R":
                    prep_hi(0, i)
                elif op == "X":
                    prep_take(0, 0, i, k, bank[7 - 4 * k])
                elif op == "F":
                    gating(i)
            attend(0, 0, schedule(False, True, True, True))
            with act.Fori(0, KVH // 2 - 1) as gp:
                for a in range(2):
                    attend(gp * 2 + (1 + a), 1 - a, schedule(True, True, True, True))
            attend(KVH - 1, 1, schedule(True, True, True, False))
            attend(KVH, 0, schedule(True, False, False, False))

        @block.gpsimd
        def _(gp_):
            GT = pool.tensor_tensor
            gp_.wait_ge(w_in_hi_done, 1)
            GT(w_in_lo[:, :, :], w_in_sb[:, :, :], w_in_hi[:, :, :].bitcast(F32), ALU.subtract).then_inc(w_in_ready, 1)
            gp_.wait_ge(w_out_hi_done, 1)
            GT(w_out_lo[:, :, :], w_out_sb[:, :, :], w_out_hi[:, :, :].bitcast(F32), ALU.subtract).then_inc(w_out_ready, 1)
            gp_.wait_ge(dt_ready, 1)

            def decay(c):
                if c:
                    gp_.wait_ge(decay_full, c)
                GT(decay_in[:, :, :], upto.unsqueeze(1).to_broadcast([P, NH, P]),
                   dts[:, 7, c, :].unsqueeze(2).to_broadcast([P, NH, P]), ALU.mult).then_inc(decay_ready, 1)

            decay(0)
            for c in range(NT):
                b = c // TB
                ts = slice(c * P, (c + 1) * P)
                gp_.wait_ge(xs_ready, (b + 1) * NCH)
                if c:
                    gp_.wait_ge(y_ready, c)
                GT(dx[:, :, :], xs[:, :, ts], cols("D").unsqueeze(2).to_broadcast([P, NCH, P]), ALU.mult).then_inc(dx_ready, 1)
                gp_.wait_ge(exps_ready, c + 1)
                gp_.wait_ge(cbm_ready, c + 1)
                if c:
                    gp_.wait_ge(y_full, c)
                GT(mix[:, :, :], within[:, :, :], cbm[:, :].unsqueeze(1).to_broadcast([P, NH, P]), ALU.mult).then_inc(mix_ready, 1)
                if c + 1 < NT and not c % TB:
                    decay(c + 1)
                if c % TB:
                    GT(c_dec[:, :, :], since[:, :, :], CT[:, ts].unsqueeze(1).to_broadcast([P, NH, P]), ALU.mult).then_inc(cdec_ready, 1)
                    if c + 1 < NT:
                        decay(c + 1)
                    gp_.wait_ge(y_full, c + 1)
                    gp_.wait_ge(state_ready, c)
                    GT(state[:, :, :], state[:, :, :], since[:, :, P - 1].unsqueeze(2).to_broadcast([P, NH, P]), ALU.mult).then_inc(state_dec, 1)
                else:
                    gp_.sem_inc(cdec_ready, 1)
            end_phase(gp_)

            def split_lo(slot, n):
                gp_.wait_ge(whi_done, n + 1)
                GT(w_lo[:, slot, :], wraw[:, slot, :], w_hi[:, slot, :].bitcast(F32), ALU.subtract).then_inc(wlo_done, 1)

            split_lo(0, 0)
            split_lo(1, 1)
            gp_.wait_ge(spread_a, NCOMB)
            gp_.wait_ge(spread_v, NCOMB)

            def expert(e, chunks, tail_next):
                for i in range(chunks):
                    which = bass.ds(e, 1) if chunks == FULL else slice(E + i, E + i + 1)
                    for s in range(2):
                        u = e * (2 * FULL) + (2 * i + s)
                        gp_.wait_ge(silu_done, u + 1)
                        gp_.sem_inc(silu_seen, 1)
                        GT(act_c[:, s, :], act_s[:, s, :], comb[:, which, s * HALF:(s + 1) * HALF].rearrange("p a n -> p (a n)"),
                           ALU.mult).then_inc(weighted, 1)
                        if s == 0 and (i + 2 < chunks or tail_next):
                            split_lo((i + 2) % FULL, e * FULL + (i + 2))

            with gp_.Fori(0, E) as e:
                expert(e, FULL, True)
            expert(E, NTAIL, False)
            end_phase(gp_)

            pool.memset(v_hi[:, :, :, 0:HD].bitcast(F32), 0.0).then_inc(vpad_ready, 1)
            pool.memset(v_hi[:, :, :, 2 * HD:3 * HD].bitcast(F32), 0.0).then_inc(vpad_ready, 1)
            pool.memset(v_lo[:, :, :, 2 * HD:3 * HD].bitcast(F32), 0.0).then_inc(vpad_ready, 1)
            pool.memset(v_lo[:, :, :, 0:HD].bitcast(F32), 0.0).then_inc(vpad_ready, 1)
            pool.memset(sT[:, :, :], 0.0).then_inc(vpad_ready, 1)

            def weights_q(g):
                gp_.wait_ge(qkvhi_done, g + 1)
                GT(qkv_lo[:, :, :], qkv_raw[:, :, :], qkv_hi[:, :, :].bitcast(F32), ALU.subtract).then_inc(qkvlo_done, 1)

            def prep_rope(g, t):
                tt = g * NT + t
                gp_.wait_ge(turned, tt + 1)
                GT(qkr[:, t % 2, :, :], qkr[:, t % 2, :, :], rot[:, t % 2, :, :], ALU.add).then_inc(rope_done, 1)

            def prep_lo(g, t):
                tt = g * NT + t
                gp_.wait_ge(qkhi_done, tt + 1)
                GT(qk_hl[:, t % 2, 0:NR, 1, :], qkr[:, t % 2, :, :], qk_hl[:, t % 2, 0:NR, 0, :].bitcast(F32),
                   ALU.subtract).then_inc(qklo_done, 1)

            def attend(now, now_set, steps):
                for late, op, i, k in steps:
                    g, a = (now - 1, 1 - now_set) if late else (now, now_set)
                    q = g * PAIRS + i
                    if op == "N":
                        gp_.wait_ge(rinv_ready, q * 2 + (k + 1))
                        for j in range(TB):
                            seg = prob[:, i % 2, k, POFF[j]:POFF[j] + (j + 1) * P]
                            ins = GT(seg, seg, rinv[:, i % 2, k, j:j + 1].to_broadcast([P, (j + 1) * P]), ALU.mult)
                        ins.then_inc(prob_ready, 1)
                    elif op == "VO":
                        gp_.wait_ge(wohi_done, g + 1)
                        GT(wo_lo[:, :, :], wo_raw[:, :, :], wo_hi[:, :, :].bitcast(F32), ALU.subtract).then_inc(wolo_done, 1)
                    elif op == "VQ":
                        weights_q(g + 1)
                    elif op == "Q":
                        prep_rope(g + 1, i)
                    elif op == "R":
                        prep_lo(g + 1, i)

            weights_q(0)
            for op, i, k in PREP:
                if op == "Q":
                    prep_rope(0, i)
                elif op == "R":
                    prep_lo(0, i)
            attend(0, 0, schedule(False, True, True, True))
            with gp_.Fori(0, KVH // 2 - 1) as gp:
                for a in range(2):
                    attend(gp * 2 + (1 + a), 1 - a, schedule(True, True, True, True))
            attend(KVH - 1, 1, schedule(True, True, True, False))
            attend(KVH, 0, schedule(True, False, False, False))

        @block.tensor
        def _(pe):
            def tr(dst, src):
                return nc.tensor.transpose(dst, src, ident)

            def split3(dst, w_h, w_l, m_h, m_l, start, stop):
                mm(dst, w_l, m_h, start=start, stop=False)
                mm(dst, w_h, m_l, start=False, stop=False)
                return mm(dst, w_h, m_h, start=False, stop=stop)

            pe.wait_ge(cst_in, 16)
            for k in range(2 * KC * BATCH):
                b, c = k // KC % BATCH, k % KC
                src, ready = (xn_tok, xn_ready) if k < KC * BATCH else (h_tok, h_ready)
                pe.wait_ge(ready, (b + 1) * TB)
                for t in range(TB):
                    ins = tr(bank[k][:, t * P:(t + 1) * P], src[:, b * TB + t, c * P:(c + 1) * P])
                ins.then_inc(tr_full, 1)
            pe.wait_ge(lo_done, 2 * KC * BATCH)
            pe.wait_ge(w_in_in, 16)
            for t in range(NT):
                if t > 1:
                    pe.wait_ge(dtb_taken, t - 1)
                for c in range(KC):
                    ins = mm(bank[t % 2][:, 0:NH + P], hT[:, c, t * P:(t + 1) * P], w_in_sb[:, c, DT0:DT0 + NH + P],
                             start=c == 0, stop=c == KC - 1)
                ins.then_inc(dtb_full, 1)
            pe.wait_ge(w_in_ready, 1)
            n = 0
            for b in range(BATCH):
                cs = slice(b * HALF, (b + 1) * HALF)
                for kind, m in PROJS:
                    at = {"gate": m * P, "ssm": DI + m * P, "B": B0, "C": C0}[kind]
                    bk = bank[2 + n % 6]
                    if n >= 6:
                        taken = [j for j in range(n - 5)]
                        convs = sum(PROJS[j % len(PROJS)][0] == "ssm" for j in taken)
                        pe.wait_ge(conv_start, convs)
                        if len(taken) > convs:
                            pe.wait_ge(pr_taken, len(taken) - convs)
                    for c in range(KC):
                        ins = split3(bk[:, :], w_in_hi[:, c, at:at + P], w_in_lo[:, c, at:at + P],
                                     hT_hi[:, c, cs], hT_lo[:, c, cs], c == 0, c == KC - 1)
                    ins.then_inc(pr_full, 1)
                    n += 1
            def out_product(b):
                cs = slice(b * HALF, (b + 1) * HALF)
                pe.wait_ge(w_out_ready, 1)
                pe.wait_ge(y_lo_done, (b + 1) * TB)
                for m in range(KC):
                    if b:
                        pe.wait_ge(s_part, m + 1)
                    for k in range(NCH):
                        ins = split3(bank[6 + m][:, :], w_out_hi[:, k, m * P:(m + 1) * P], w_out_lo[:, k, m * P:(m + 1) * P],
                                     y_hi[:, k, cs], y_lo[:, k, cs], k == 0, k == NCH - 1)
                    ins.then_inc(s_full, 1)

            pe.wait_ge(ones_ready, 1)
            pe.wait_ge(pr_taken, BATCH * (NCH + 2))
            pe.wait_ge(conv_start, BATCH * NCH)
            for c in range(NT):
                b = c // TB
                ts = slice(c * P, (c + 1) * P)
                pe.wait_ge(decay_ready, c + 1)
                if c:
                    pe.wait_ge(exps_ready, c)
                else:
                    pe.wait_ge(dtb_taken, NT)
                dec = decay_in[:, :, :].rearrange("p h q -> p (h q)")
                mm(bank[0][:, :], after, dec, start=True, stop=True)
                mm(bank[1][:, :], ones[:, :], dec, start=True, stop=True).then_inc(decay_full, 1)
                if c:
                    pe.wait_ge(cbm_ready, c)
                mm(bank[2][:, 0:P], BT[:, ts], CT[:, ts], start=True, stop=True).then_inc(cb_full, 1)
                pe.wait_ge(xs_ready, (b + 1) * NCH)
                if c:
                    pe.wait_ge(xend_ready, c)
                for h in range(NH):
                    ins = tr(bank[3][:, h * P:(h + 1) * P], xs[:, h, ts])
                ins.then_inc(xt_full, 1)
                pe.wait_ge(mix_ready, c + 1)
                pe.wait_ge(xdt_ready, c + 1)
                if c % TB:
                    pe.wait_ge(cdec_ready, c + 1)
                if c:
                    pe.wait_ge(state_ready, c)
                    pe.wait_ge(y_ready, c)
                for h in range(NH):
                    dst = bank[4][:, h * P:(h + 1) * P]
                    ins = mm(dst, x_dt[:, h, :], mix[:, h, :], start=True, stop=c % TB == 0)
                    if c % TB:
                        ins = mm(dst, state[:, h, :], c_dec[:, h, :], start=False, stop=True)
                ins.then_inc(y_full, 1)
                pe.wait_ge(xend_ready, c + 1)
                mm(bank[5][:, :], dtB[:, c, NH:NH + P], x_end[:, :, :].rearrange("p h q -> p (h q)"),
                   start=True, stop=True).then_inc(state_full, 1)
                if c == TB:
                    out_product(0)
            out_product(1)
            end_phase(pe)

            pe.sem_inc(hslot_free, 2 * FULL)
            for t in range(NT):
                for c in range(KC):
                    ins = mm(bank[0][:, t * E:(t + 1) * E], xnT[:, c, t * P:(t + 1) * P],
                             par[:, PARAMS["gate_w"][0] + c * E:PARAMS["gate_w"][0] + (c + 1) * E], start=c == 0, stop=c == KC - 1)
            ins.then_inc(route_full, 1)
            pe.wait_ge(zero_ready, 1)
            for n in range(KC * BATCH):
                mm(bank[4 + n][:, :], zero_b[:, 0:P], zero_b[:, :], start=True, stop=False)
            pe.wait_ge(comb_ready, 1)
            for s in range(2):
                for t in range(TB):
                    ins = tr(bank[1 + s][0:2 * E, t * P:(t + 1) * P], cmb_hl[:, s * TB + t, :])
                ins.then_inc(combt_full, 1)
            pe.wait_ge(combt_ready, 2)
            pe.wait_ge(sel_ready, 1)
            for n in range(2 * NCOMB):
                k, s = n // 2, n % 2
                if n >= 4:
                    pe.wait_ge(spread_a if n % 2 == 0 else spread_v, (n - 4) // 2 + 1)
                mm(bank[n % 4][:, :], sel_r[:, k * P:(k + 1) * P], combT[:, s * HALF:(s + 1) * HALF],
                   start=True, stop=True).then_inc(spread_full, 1)
            pe.wait_ge(spread_a, NCOMB)
            pe.wait_ge(spread_v, NCOMB)

            def in_products(slot, s):
                cs = slice(s * HALF, (s + 1) * HALF)
                for bk, at in ((bank[s], 0), (bank[2 + s], FC2)):
                    for c in range(KC):
                        w = slice(at + c * P, at + (c + 1) * P)
                        ins = split3(bk[:, :], w_hi[:, slot, w], w_lo[:, slot, w], xnT_hi[:, c, cs], xnT_lo[:, c, cs],
                                     c == 0, c == KC - 1)
                ins.then_inc(ab_full, 1)

            pe.wait_ge(wlo_done, 1)
            in_products(0, 0)
            in_products(0, 1)

            def expert(e, chunks, tail_next):
                for i in range(chunks):
                    for s in range(2):
                        u = e * (2 * FULL) + (2 * i + s)
                        if i + 1 < chunks or tail_next:
                            if s == 0:
                                pe.wait_ge(wlo_done, e * FULL + (i + 2))
                            pe.wait_ge(h_made, u + 1)
                            in_products((i + 1) % FULL, s)
                        pe.wait_ge(hlo_done, u + 1)
                        last = chunks == NTAIL and i == chunks - 1
                        for m in range(KC):
                            w = slice(PJ + m * P, PJ + (m + 1) * P)
                            ins = split3(bank[4 + 2 * m + s][:, :], w_hi[:, i, w], w_lo[:, i, w], h_hi[:, s, :], h_lo[:, s, :], False, last)
                        ins.then_inc(hslot_free, 1)

            with pe.Fori(0, E) as e:
                expert(e, FULL, True)
            expert(E, NTAIL, False)
            for n in range(NT // 2):
                pe.wait_ge(sg_ready, KC * BATCH)
                for j in range(2 * KC):
                    t, m = 2 * n + j // KC, j % KC
                    ins = tr(bank[n][:, j * P:(j + 1) * P], sT[:, m, t * P:(t + 1) * P])
                ins.then_inc(back_full, 1)
            end_phase(pe)

            def turn_norm(k, src, ready, bk):
                b, c = k // KC, k % KC
                pe.wait_ge(ready, NT + (b + 1) * TB)
                for t in range(TB):
                    ins = tr(bk[:, t * P:(t + 1) * P], src[:, b * TB + t, c * P:(c + 1) * P])
                ins.then_inc(tr_full, 1)

            for k in range(KC * BATCH):
                turn_norm(k, xn1, xn_ready, bank[k])
            pe.wait_ge(lo_done, 3 * KC * BATCH)

            def gating(part):
                if part == 3:
                    for k in range(KC * BATCH):
                        if k >= 3:
                            pe.wait_ge(sign_ready, k - 2)
                        turn_norm(k, xn2, h_ready, bank[4 + k % 3])
                elif part == 4:
                    pe.wait_ge(wsign_ready, KC)
                    pe.wait_ge(sign_ready, KC * BATCH - 2)
                    for k in range(KC):
                        for m in range(KC):
                            ins = tr(bank[4 + KC * BATCH % 3][:, (k * KC + m) * P:(k * KC + m + 1) * P], wsg[:, m, k * P:(k + 1) * P])
                    ins.then_inc(wsT_full, 1)
                elif part == 5:
                    pe.wait_ge(wsT_ready, 1)
                    pe.wait_ge(sign_ready, KC * BATCH)
                    for n in range(KC * BATCH):
                        m, s = n // 2, n % 2
                        if n >= 3:
                            pe.wait_ge(g1_ready, n - 2)
                        for c in range(KC):
                            ins = mm(bank[4 + (KC * BATCH + 1 + n) % 3][:, :], wsT[:, c, m * P:(m + 1) * P],
                                     signT[:, c, s * HALF:(s + 1) * HALF], start=c == 0, stop=c == KC - 1)
                        ins.then_inc(sign_full, 1)

            def prep_qkv(g, t, event, qk_bank):
                if t == 0:
                    pe.wait_ge(qkvlo_done, g + 1)
                if not isinstance(event, int) or event > 0:
                    pe.wait_ge(b6_free, event)
                for c in range(KC):
                    ts = slice(t * P, (t + 1) * P)
                    ins = split3(qk_bank[:, 0:GW], xnT_hi[:, c, ts], xnT_lo[:, c, ts], qkv_hi[:, c, :], qkv_lo[:, c, :],
                                 c == 0, c == KC - 1)
                ins.then_inc(qkv_full, 1)

            def prep_turn(g, t, k, ahead, turn_bank):
                tt = g * NT + t
                if k == 0:
                    pe.wait_ge(qklo_done, tt + 1)
                if not isinstance(tt, int) or tt * 2 + k > ahead:
                    pe.wait_ge(tq_taken, tt * 2 + (k - ahead))
                flat = qk_hl[:, t % 2, :, :, :].rearrange("p h a d -> p (h a d)")
                for j in range(GQ if k == 0 else 2):
                    at = j * P if k == 0 else GQ * P + j * HD
                    ins = mm(turn_bank[:, j * P:(j + 1) * P], flat[:, at:at + P], id_r[:, :], start=True, stop=True)
                ins.then_inc(tq_full, 1)

            def attend(now, now_set, steps):
                per = NT + BATCH * KC
                event = NT if isinstance(now, int) and now == 0 else now * per + (NT - LATE_W)
                if isinstance(now, int) and now == KVH:
                    event = per * KVH - LATE_W
                done6 = 0
                for late, op, i, k in steps:
                    g, a = (now - 1, 1 - now_set) if late else (now, now_set)
                    q = g * PAIRS + i
                    u = q * 5 + k
                    b = i // 2
                    if op == "S":
                        if k == 0 and i % 2 == 0:
                            pe.wait_ge(tq_taken, g * (2 * NT) + (b + 1) * NT)
                        pe.wait_ge(exp_done, u + 1)
                        for h, j, at in SCORES[k]:
                            n = (j + 1) * P
                            dst = bank[(i + k) % 2][:, at:at + n]
                            qs = qT[:, a, 2 * (i % 2) + h, b * HALF + j * P:b * HALF + (j + 1) * P]
                            mm(dst, qs, kT[:, a, 0, b * HALF:b * HALF + n], start=(h, j, at) == SCORES[k][0], stop=False)
                            mm(dst, qs, kT[:, a, 1, b * HALF:b * HALF + n], start=False, stop=False)
                        lo, moved = MASKS[k]
                        mm(bank[(i + k) % 2][:, lo:HALF], mask_b[:, :], id_b[:, moved:moved + HALF - lo], start=False,
                           stop=True).then_inc(score_full, 1)
                    elif op == "T":
                        if k in (0, 2):
                            pe.wait_ge(prob_ready, q * 2 + (1 if k == 0 else 2))
                        pe.wait_ge(plo_done, u + 1)
                        for h, j, at in TURNED[k]:
                            for r in range(j, TB):
                                ins = tr(bank[2 + (i + k) % 2][:, at + (r - j) * P:at + (r - j + 1) * P],
                                         prob[:, i % 2, h, POFF[r] + j * P:POFF[r] + (j + 1) * P])
                        ins.then_inc(pt_full, 1)
                    elif op == "A":
                        pe.wait_ge(plo_done, u + 3)
                        if k == 0:
                            pe.wait_ge(olo_done, q + 1)
                        b_ = (i + k) % 4
                        for h, j, at in TURNED[k]:
                            n = (TB - j) * P
                            dst = bank[4 + i % 2][:, j * P:j * P + n]
                            vs = slice(HD, 3 * HD) if h == 0 else slice(0, 2 * HD)
                            last = k == 4 and h == 1
                            ins = split3(dst, v_hi[:, a, b * TB + j, vs], v_lo[:, a, b * TB + j, vs], p_hi[:, b_, at:at + n],
                                         p_lo[:, b_, at:at + n], k == 0, last)
                        ins.then_inc(av_done, 1)
                    elif op == "W":
                        m = i % KC
                        b = i // KC
                        pe.wait_ge(wolo_done, g + 1)
                        pe.wait_ge(olo_done, g * PAIRS + (2 * b + 4))
                        pe.wait_ge(b6_free, event + done6)
                        done6 += 1
                        for c in range(2):
                            ins = split3(bank[6][:, :], wo_hi[:, c, m * P:(m + 1) * P], wo_lo[:, c, m * P:(m + 1) * P],
                                         o_hi[:, b, c, :], o_lo[:, b, c, :], c == 0, c == 1)
                        ins.then_inc(wo_full, 1)
                    elif op == "Q":
                        prep_qkv(g + 1, i, event + done6, bank[6])
                        done6 += 1
                    elif op == "X":
                        prep_turn(g + 1, i, k, 0, bank[7])

            pe.sem_inc(plo_done, 2)
            pe.sem_inc(olo_done, 2)
            pe.sem_inc(av_done, 4)
            pe.sem_inc(wo_full, 1)
            pe.wait_ge(mask_ready, 3)
            for op, i, k in PREP:
                if op == "Q":
                    prep_qkv(0, i, i - 2, bank[i % 3])
                elif op == "X":
                    prep_turn(0, i, k, 1, bank[7 - 4 * k])
                elif op == "F":
                    gating(i)
            pe.wait_ge(g1_ready, KC * BATCH)
            pe.wait_ge(b6_free, NT)
            pe.wait_ge(tq_taken, TAKEN_EARLY)
            attend(0, 0, schedule(False, True, True, True))
            with pe.Fori(0, KVH // 2 - 1) as gp:
                for a in range(2):
                    attend(gp * 2 + (1 + a), 1 - a, schedule(True, True, True, True))
            attend(KVH - 1, 1, schedule(True, True, True, False))
            attend(KVH, 0, schedule(True, False, False, False))
            for n in range(NT // 2):
                pe.wait_ge(sg_ready, 2 * KC * BATCH)
                for j in range(2 * KC):
                    t, m = 2 * n + j // KC, j % KC
                    ins = tr(bank[n][:, j * P:(j + 1) * P], sT[:, m, t * P:(t + 1) * P])
                ins.then_inc(back_full, 1)


def _constants():
    import numpy as np
    p = np.arange(P)
    ident = np.eye(P)
    upto = p[:, None] <= p[None, :]
    after = p[:, None] > p[None, :]
    number = np.broadcast_to(np.arange(E), (P, E))
    consts = np.concatenate([ident, upto, after, number], 1).astype(np.float32)
    select = np.zeros((2, E, NCOMB, P), np.float32)
    for k in range(E):
        select[:, k, k, :] = 1
    for j in range(NTAIL):
        for r in range(P // TAIL):
            select[:, j * (P // TAIL) + r, E + j, r * TAIL:(r + 1) * TAIL] = 1
    freq = (1.0 / np.float32(10000.0) ** (np.arange(0, HD, 2, dtype=np.float32) / np.float32(HD))).astype(np.float32)
    angle = np.arange(SEQ, dtype=np.float32)[:, None] * freq[None, :]
    cos, sin = np.cos(angle), np.sin(angle)
    rope = np.stack([np.concatenate([cos, cos], 1), np.concatenate([-sin, sin], 1)], 1)
    rope = rope.reshape(TB, P, 2, HD).transpose(1, 0, 2, 3)
    return consts, select.reshape(2 * E, NCOMB * P), np.ascontiguousarray(rope, np.float32)


def kernel(**inputs):
    import numpy as np
    import concourse.bacc as bacc
    from concourse.bass_utils import run_bass_kernel_spmd

    a = {k: np.asarray(v) for k, v in inputs.items()}

    def by_column(v):
        return v.reshape(-1, P).T

    def rows(v):
        return np.broadcast_to(v, (P, v.shape[0]))

    consts, select, rope = _constants()
    params = np.concatenate([
        by_column(a["L0_attn_norm_scale"]),
        a["L0_attn_conv_weight"].reshape(TAPS, NCH, P).transpose(2, 1, 0).reshape(P, NCH * TAPS),
        by_column(a["L0_attn_conv_bias"]), by_column(a["L0_attn_D"]),
        rows(a["L0_attn_dt_bias"]), rows(a["L0_attn_A_log"]),
        by_column(a["L1_ffn_gamma"]), by_column(a["L1_ffn_beta"]), by_column(a["L1_ffn_bias"]), by_column(a["L1_ffn_alpha"]),
        a["L0_ffn_gate_w"].reshape(E, KC, P).transpose(2, 1, 0).reshape(P, KC * E)], 1)
    fc = [a[f"L0_ffn_fc{i}_w"].reshape(E, I, KC, P) for i in (1, 2)]
    pj = a["L0_ffn_proj_w"].transpose(0, 2, 1)

    def chunks(f, n):
        return f.reshape(n, P, KC, P).transpose(0, 3, 2, 1).reshape(n, P, C)

    cut = FULL * P
    w_moe = np.concatenate([chunks(f[:, :cut], E * FULL) for f in fc] + [pj[:, :cut].reshape(E * FULL, P, C)], 2)
    w_tail = np.concatenate([chunks(f[:, cut:], NTAIL) for f in fc] + [pj[:, cut:].reshape(NTAIL, P, C)], 2)
    wq = a["L1_attn_Wq"].reshape(KVH, GQ * HD, KC, P)
    wk, wv = (a[f"L1_attn_{n}"].reshape(KVH, HD, KC, P) for n in ("Wk", "Wv"))
    w_qkv = np.concatenate([wq, wk, wv], 1).transpose(0, 3, 2, 1)
    w_o = a["L1_attn_Wo"].reshape(C, KVH, 2, P).transpose(1, 3, 2, 0)
    sent = {
        "x": a["L0_attn_x"].reshape(T, C), "params": params, "consts": consts, "select": select, "rope": rope,
        "w_in": a["L0_attn_in_proj_w"].reshape(KC, P, PROJ).transpose(1, 0, 2),
        "w_out": a["L0_attn_out_proj_w"].reshape(NCH, P, C).transpose(1, 0, 2),
        "w_moe": w_moe, "w_moe_tail": w_tail, "w_qkv": w_qkv, "w_o": w_o,
        "w_sign": a["L1_ffn_weight"].reshape(KC, P, C).transpose(1, 0, 2),
    }
    sent = {f"in_{k}": np.ascontiguousarray(v) for k, v in sent.items()}
    nc = bacc.Bacc("TRN2", target_bir_lowering=False, num_devices=1)
    args = [nc.dram_tensor(k, v.shape, mybir.dt.from_np(v.dtype), kind="ExternalInput").ap() for k, v in sent.items()]
    args.append(nc.dram_tensor("out_x", (T, C), F32, kind="ExternalOutput").ap())
    layered_kernel(nc, *args)
    r = run_bass_kernel_spmd(nc, [sent], core_ids=[0])
    return r.results[0]["out_x"].reshape(BATCH, SEQ, C)
```

```python
import concourse.bass as bass
from concourse import mybir
from contextlib import ExitStack

F32 = mybir.dt.float32
F32R = mybir.dt.float32r
BF16 = mybir.dt.bfloat16
U32 = mybir.dt.uint32

P = 128
BATCH, SEQ, C = 2, 512, 256
T = BATCH * SEQ
NT = T // P
TB = SEQ // P
KC = C // P
HALF = SEQ
DI, NH = 512, 4
NCH = DI // P
PROJ = 2 * DI + NH + 2 * P
DT0 = 2 * DI
B0, C0 = DT0 + NH, DT0 + NH + P
TAPS = 4
E, I = 8, 704
FULL = I // P
TAIL = I - FULL * P
NTAIL = E * TAIL // P
WM = 3 * C
FC2, PJ = C, 2 * C
H, KVH, HD = 32, 8, 64
GQ = H // KVH
GW = GQ * HD + 2 * HD
NR = GQ + 1
PAIRS = BATCH * GQ // 2
NCOL = P * TB * (TB + 1) // 2
PARAMS = {}
_at = 0
for _n, _k in (("norm_scale", KC), ("conv_w", NCH * TAPS), ("conv_b", NCH), ("D", NCH), ("dt_bias", NH),
               ("A_log", NH), ("gamma", KC), ("beta", KC), ("bias", KC), ("alpha", KC), ("gate_w", KC * E)):
    PARAMS[_n] = (_at, _k)
    _at += _k
NPARAM = _at
NCONST = 3 * P + E
NCOMB = E + NTAIL
MASKED = -1e30
PROJS = [("ssm", m) for m in range(NCH)] + [("B", 0), ("C", 0)] + [("gate", m) for m in range(NCH)]
POFF = [P * j * (j + 1) // 2 for j in range(TB)]
SCORES = [[(0, 3, 0)], [(0, 2, 0), (0, 0, 3 * P)], [(0, 1, 0), (1, 1, 2 * P)], [(1, 3, 0)], [(1, 2, 0), (1, 0, 3 * P)]]
MASKS = [(3 * P, 3 * P), (2 * P, 2 * P), (P, 0), (3 * P, 3 * P), (2 * P, 2 * P)]
HEADS_AT = (3, 5)
TURNED = [[(0, 0, 0)], [(0, 1, 0), (0, 3, 3 * P)], [(1, 0, 0)], [(1, 1, 0), (1, 3, 3 * P)], [(0, 2, 0), (1, 2, 2 * P)]]
STEPS = 5 * PAIRS
LAG = 6
TO_V = 2


def schedule(last, this, prep_last, prep):
    ready = [(0, 1, "VQ", 0, 0)]
    for t in range(NT):
        n = 2 * t + STEPS - 2 * NT + 1
        ready += [(n, 8, "Q", t, 0), (n + 2, 8.2, "R", t, 0), (n + 5, 6.5, "X", t, 0), (n + 6, 6.5, "X", t, 1)]
    own = [(13, 0, "VO", 0, 0)]
    for r in range(PAIRS):
        for k in range(5):
            n = 5 * r + k
            own += [(n, 2, "S", r, k), (n, 4, "E", r, k), (n + LAG, 3, "T", r, k), (n + LAG + TO_V, 5, "A", r, k)]
        for h in range(2):
            own += [(5 * r + HEADS_AT[h], 5, "N", r, h)]
        own += [(5 * r + 4 + LAG + TO_V + 1, 1, "O", r, 0)]
    for b in range(BATCH):
        for m in range(KC):
            own += [(5 * (2 * b + 1) + 4 + LAG + TO_V + 3 + 2 * m, 8.5, "W", b * KC + m, 0)]
    picked = [(n - late * STEPS, p, late, op, i, k)
              for at, late, wanted in ((own, True, last), (ready, True, prep_last), (own, False, this), (ready, False, prep))
              for n, p, op, i, k in at if wanted and (n >= STEPS) == late]
    return [z[2:] for z in sorted(picked, key=lambda z: z[:2])]


GATING_PARTS = 6
PREP = []
for _late, _op, _i, _k in schedule(False, False, False, True):
    PREP += [(_op, _i, _k)] + ([("F", _i, 0)] if _op == "Q" and _i < GATING_PARTS else [])
TAKEN_EARLY = sum(z[0] == "X" for z in PREP)
LATE_W = sum(z[1] == "W" for z in schedule(True, False, False, False))


def layered_kernel(nc, x, params, consts, select, rope, w_in, w_out, w_moe, w_moe_tail, w_qkv, w_o, w_sign, out):
    ALU = mybir.AluOpType
    ACT = mybir.ActivationFunctionType
    AX = mybir.AxisListType
    ctx = ExitStack()
    with ctx:
        def sem(name):
            return ctx.enter_context(nc.semaphore(name))

        def sb(name, shape, dt=F32, scope=ctx):
            return scope.enter_context(nc.sbuf_tensor(name, shape, dt))

        bank = [ctx.enter_context(nc.psum_tensor(f"bank{i}", [P, HALF], F32)) for i in range(8)]

        cst = sb("cst", [P, NCONST])
        ident, upto, after = cst[:, 0:P], cst[:, P:2 * P], cst[:, 2 * P:3 * P]
        expert_no = cst[:, 3 * P:3 * P + E]
        ones = sb("ones", [P, P])
        par = sb("par", [P, NPARAM])
        x_tok = sb("x_tok", [P, NT, C])
        xnT = sb("xnT", [P, KC, T])
        xnT_hi = sb("xnT_hi", [P, KC, T], F32R)
        xnT_lo = sb("xnT_lo", [P, KC, T], F32R)
        sT = sb("sT", [P, KC, T])
        stats = sb("stats", [P, NT, 6])
        mv = sb("mv", [P, NT, 2])
        sv = sb("sv", [P, 10, NT])

        def col(name, i=0):
            return par[:, PARAMS[name][0] + i:PARAMS[name][0] + i + 1]

        def cols(name):
            return par[:, PARAMS[name][0]:PARAMS[name][0] + PARAMS[name][1]]

        s0 = ExitStack()
        sel = sb("sel", [2 * E, NCOMB * P], F32, s0)
        sel_r = sb("sel_r", [2 * E, NCOMB * P], F32R, s0)
        route = sb("route", [P, NT, E], F32, s0)
        top = sb("top", [P, NT, E], F32, s0)
        topi = sb("topi", [P, NT, E], U32, s0)
        topf = sb("topf", [P, NT, 2], F32, s0)
        pr = sb("pr", [P, 6, NT], F32, s0)
        onehot = sb("onehot", [P, NT, 2, E], F32, s0)
        cmb = sb("cmb", [P, NT, E], F32, s0)
        cmb_hl = sb("cmb_hl", [P, NT, 2 * E], F32, s0)
        cmb_h = sb("cmb_h", [P, NT, E], F32R, s0)
        combT = sb("combT", [2 * E, T], F32R, s0)

        s1 = ExitStack()
        w_out_sb = sb("w_out_sb", [P, NCH, C], F32, s1)
        w_out_hi = sb("w_out_hi", [P, NCH, C], F32R, s1)
        w_out_lo = sb("w_out_lo", [P, NCH, C], F32R, s1)
        xs = sb("xs", [P, NCH, T], F32, s1)
        norm_tok = xs[:, :, :].rearrange("p a (b c) -> p (a b) c", c=C)
        xn_tok, h_tok = norm_tok[:, 0:NT, :], norm_tok[:, NT:2 * NT, :]
        hT = sT
        y_hi = sb("y_hi", [P, NCH, T], F32R, s1)
        y_lo = sb("y_lo", [P, NCH, T], F32R, s1)
        hT_hi, hT_lo = y_hi[:, 0:KC, :], y_lo[:, 0:KC, :]
        ssm = sb("ssm", [P, NCH, TAPS - 1 + SEQ], F32, s1)
        gate = sb("gate", [P, NCH, T], F32, s1)
        BT = sb("BT", [P, T], F32, s1)
        CT = sb("CT", [P, T], F32, s1)
        dtB = sb("dtB", [P, NT, NH + P], F32, s1)
        dts = sb("dts", [P, 8, NT, NH], F32, s1)
        a_neg = sb("a_neg", [P, NH], F32, s1)
        decay_in = sb("decay_in", [P, 2, NH, P], F32, s1)
        w_end = sb("w_end", [P, 2, NH], F32, s1)
        dx = sb("dx", [P, 2, NCH, P], F32, s1)
        state = sb("state", [P, NH, P], F32, s1)
        s1_in = ExitStack()
        w_in_sb = sb("w_in_sb", [P, KC, PROJ], F32, s1_in)
        w_in_hi = sb("w_in_hi", [P, KC, PROJ], F32R, s1_in)
        w_in_lo = sb("w_in_lo", [P, KC, PROJ], F32R, s1_in)
        s1_in.close()
        s1_scan = ExitStack()
        within = sb("within", [P, 2, NH, P], F32, s1_scan)
        since = sb("since", [P, 2, NH, P], F32, s1_scan)
        cbm = sb("cbm", [P, 2, P], F32, s1_scan)
        mix = sb("mix", [P, 2, NH, P], F32, s1_scan)
        c_dec = sb("c_dec", [P, 2, NH, P], F32, s1_scan)
        x_dt = sb("x_dt", [P, 2, NH, P], F32, s1_scan)
        x_end = sb("x_end", [P, 2, NH, P], F32, s1_scan)
        s1_scan.close()
        s1.close()

        s2 = ExitStack()
        wraw = sb("wraw", [P, FULL, WM], F32, s2)
        w_hi = sb("w_hi", [P, FULL, WM], F32R, s2)
        w_lo = sb("w_lo", [P, FULL, WM], F32R, s2)
        comb = sb("comb", [P, NCOMB, T], F32, s2)
        zero_b = sb("zero_b", [P, HALF], BF16, s2)
        act_s = sb("act_s", [P, 2, HALF], F32, s2)
        act_c = sb("act_c", [P, 2, HALF], F32, s2)
        act_h = sb("act_h", [P, 2, HALF], F32, s2)
        h_hi = sb("h_hi", [P, 2, HALF], F32R, s2)
        h_lo = sb("h_lo", [P, 2, HALF], F32R, s2)
        gT = sb("gT", [P, KC, T], F32, s2)
        s2.close()
        s0.close()

        s3 = ExitStack()
        prob = sb("prob", [P, 2, 2, NCOL], F32, s3)
        before = prob[:, :, :, :].rearrange("p s h n -> p (s h n)")
        xn1 = before[:, 0:NT * C].rearrange("p (t c) -> p t c", c=C)
        xn2 = before[:, NT * C:2 * NT * C].rearrange("p (t c) -> p t c", c=C)
        wsg = before[:, 2 * NT * C:2 * NT * C + KC * C].rearrange("p (k c) -> p k c", c=C)
        wcen = before[:, 2 * NT * C + KC * C:2 * NT * C + 2 * KC * C].rearrange("p (k c) -> p k c", c=C)
        signT = sb("signT", [P, KC, T], BF16, s3)
        g1T = xnT
        wst = sb("wst", [P, KC, 4], F32, s3)
        wsT = sb("wsT", [P, KC, C], BF16, s3)
        ab = sb("ab", [P, KC], F32, s3)
        rp = sb("rp", [P, TB, 2, HD], F32, s3)
        id_b = sb("id_b", [P, 4 * P], BF16, s3)
        mask_b = sb("mask_b", [P, P], BF16, s3)
        qkv_raw = sb("qkv_raw", [P, KC, GW], F32, s3)
        qkv_hi = sb("qkv_hi", [P, KC, GW], F32R, s3)
        qkv_lo = sb("qkv_lo", [P, KC, GW], F32R, s3)
        wo_raw = sb("wo_raw", [P, 2, C], F32, s3)
        wo_hi = sb("wo_hi", [P, 2, C], F32R, s3)
        wo_lo = sb("wo_lo", [P, 2, C], F32R, s3)
        id_r = sb("id_r", [P, P], F32R, s3)
        rot = sb("rot", [P, 2, NR, HD], F32, s3)
        qkr = sb("qkr", [P, 2, NR, HD], F32, s3)
        qk_hl = sb("qk_hl", [P, 2, NR + 1, 2, HD], F32R, s3)
        qT = sb("qT", [P, 2, GQ, T], F32R, s3)
        kT = sb("kT", [P, 2, 2, T], F32R, s3)
        v_hi = sb("v_hi", [P, 2, NT, 3 * HD], F32R, s3)
        v_lo = sb("v_lo", [P, 2, NT, 3 * HD], F32R, s3)
        nmax = sb("nmax", [P, 2, 2, TB], F32, s3)
        rsum = sb("rsum", [P, 2, 2, TB], F32, s3)
        rinv = sb("rinv", [P, 2, 2, TB], F32, s3)
        p_hi = sb("p_hi", [P, 4, HALF], F32R, s3)
        p_lo = sb("p_lo", [P, 4, HALF], F32R, s3)
        o_hi = sb("o_hi", [P, 2, 2, HALF], F32R, s3)
        o_lo = sb("o_lo", [P, 2, 2, HALF], F32R, s3)
        s3.close()

        def sems(names):
            return (sem(n) for n in names.split())

        x_in = [sem(f"x_in{b}") for b in range(BATCH)]
        par_in, cst_in, w_in_in, w_out_in, sel_in, wsg_in, rope_in, qkv_in, wo_in, out_done = sems(
            "par_in cst_in w_in_in w_out_in sel_in wsg_in rope_in qkv_in wo_in out_done")
        slot_in = [sem(f"slot_in{i}") for i in range(FULL)]
        phase_done = sem("phase_done")
        vstep = sem("vstep")
        var_ready, root_ready, stat_ready, aggr_ready, xn_ready, h_ready, tr_full, hi_done, lo_done, ones_ready, pad_ready = sems(
            "var_ready root_ready stat_ready aggr_ready xn_ready h_ready tr_full hi_done lo_done ones_ready pad_ready")
        w_in_hi_done, w_in_ready, w_out_hi_done, w_out_ready, dtb_full, dtb_taken, pr_full, pr_taken = sems(
            "w_in_hi_done w_in_ready w_out_hi_done w_out_ready dtb_full dtb_taken pr_full pr_taken")
        a_ready, az_ready, z_ready, u_ready, lg_ready, dt_ready, ssm_in, conv_start, conv_done, xs_ready = sems(
            "a_ready az_ready z_ready u_ready lg_ready dt_ready ssm_in conv_start conv_done xs_ready")
        decay_ready, decay_full, exps_ready, cb_full, cbm_ready, xt_full, xdt_ready, xend_ready, mix_ready, cdec_ready = sems(
            "decay_ready decay_full exps_ready cb_full cbm_ready xt_full xdt_ready xend_ready mix_ready cdec_ready")
        y_full, state_full, state_ready, dx_ready, y_ready, y_hi_done, y_lo_done, s_full, s_part = sems(
            "y_full state_full state_ready dx_ready y_ready y_hi_done y_lo_done s_full s_part")
        route_full, route_taken, top_ready, topi_ready, diff_ready, e2_ready, comb_ready, combt_full, combt_ready = sems(
            "route_full route_taken top_ready topi_ready diff_ready e2_ready comb_ready combt_full combt_ready")
        sel_ready, zero_ready, spread_full, spread_a, spread_v = sems("sel_ready zero_ready spread_full spread_a spread_v")
        whi_done, wlo_done, ab_full, silu_done, silu_seen, weighted, h_made, hhi_done, hlo_done, hslot_free = sems(
            "whi_done wlo_done ab_full silu_done silu_seen weighted h_made hhi_done hlo_done hslot_free")
        g_ready, sg_ready, back_full, x_ready = sems("g_ready sg_ready back_full x_ready")
        wcen_ready, wsign_ready, wsT_full, wsT_ready, sign_ready, sign_full, ab_ready, g1_ready, mask_ready, vpad_ready = sems(
            "wcen_ready wsign_ready wsT_full wsT_ready sign_ready sign_full ab_ready g1_ready mask_ready vpad_ready")
        qkvhi_done, qkvlo_done, wohi_done, wolo_done, qkv_full, v_hi_done, b6_free, turned, rope_done = sems(
            "qkvhi_done qkvlo_done wohi_done wolo_done qkv_full v_hi_done b6_free turned rope_done")
        qkhi_done, qklo_done, tq_full, tq_taken = sems("qkhi_done qklo_done tq_full tq_taken")
        score_full, max_ready, exp_done, rinv_ready, prob_ready, pt_full, phi_done, plo_done, av_done = sems(
            "score_full max_ready exp_done rinv_ready prob_ready pt_full phi_done plo_done av_done")
        ohi_done, olo_done, wo_full = sems("ohi_done olo_done wo_full")

        ends = {}

        def end_phase(eng):
            k = ends[eng.engine] = ends.get(eng.engine, 0) + 1
            eng.drain().then_inc(phase_done, 1)
            eng.wait_ge(phase_done, 5 * k)

        def stepper(eng, signal):
            n = [0]

            def then(ins):
                n[0] += 1
                ins.then_inc(signal, 1)
                eng.wait_ge(signal, n[0])
            return then

        vec = nc.vector
        TT, TS, STT = vec.tensor_tensor, vec.tensor_scalar, vec.scalar_tensor_tensor
        pool = nc.gpsimd
        mm = nc.tensor.matmul

        block = ctx.enter_context(nc.Block())

        def carried(c):
            return c - c // TB

        @block.sync
        def _(sp):
            xv = x.rearrange("(t p) c -> p t c", p=P)
            sp.dma_start(x_tok[:, 0:TB, :], xv[:, 0:TB, :]).then_inc(x_in[0], 16)
            sp.dma_start(x_tok[:, TB:NT, :], xv[:, TB:NT, :]).then_inc(x_in[1], 16)
            sp.dma_start(cst[:, :], consts).then_inc(cst_in, 16)
            sp.dma_start(par[:, :], params).then_inc(par_in, 16)
            sp.dma_start(w_in_sb[:, :, :], w_in).then_inc(w_in_in, 16)
            sp.dma_start(w_out_sb[:, :, :], w_out).then_inc(w_out_in, 16)
            sp.dma_start(sel[:, :], select).then_inc(sel_in, 16)
            end_phase(sp)
            for i in range(FULL):
                sp.dma_start(wraw[:, i, :], w_moe[i, :, :]).then_inc(slot_in[i], 16)
            wv = w_moe.rearrange("(e i) p n -> e i p n", i=FULL)
            with sp.Fori(0, E - 1) as e:
                for i in range(FULL):
                    sp.wait_ge(wlo_done, e * FULL + (i + 1))
                    sp.dma_start(wraw[:, i, :], wv[bass.ds(e + 1, 1), i, :, :].rearrange("a p n -> (a p) n")).then_inc(slot_in[i], 16)
            for i in range(NTAIL):
                sp.wait_ge(wlo_done, (E - 1) * FULL + i + 1)
                sp.dma_start(wraw[:, i, :], w_moe_tail[i, :, :]).then_inc(slot_in[i], 16)
            end_phase(sp)
            sp.dma_start(wsg[:, :, :], w_sign).then_inc(wsg_in, 16)
            sp.dma_start(qkv_raw[:, :, :], w_qkv[0, :, :, :]).then_inc(qkv_in, 16)
            sp.dma_start(rp[:, :, :, :], rope).then_inc(rope_in, 16)
            sp.dma_start(wo_raw[:, :, :], w_o[0, :, :, :]).then_inc(wo_in, 16)
            with sp.Fori(0, KVH - 1) as g:
                sp.wait_ge(qkvlo_done, g + 1)
                sp.dma_start(qkv_raw[:, :, :], w_qkv[bass.ds(g + 1, 1), :, :, :].rearrange("a p k n -> (a p) k n")).then_inc(qkv_in, 16)
                sp.wait_ge(wolo_done, g + 1)
                sp.dma_start(wo_raw[:, :, :], w_o[bass.ds(g + 1, 1), :, :, :].rearrange("a p k n -> (a p) k n")).then_inc(wo_in, 16)
            for b in range(BATCH):
                sp.wait_ge(x_ready, NT // 2 + (b + 1) * TB // 2)
                ts = slice(b * TB, (b + 1) * TB)
                sp.dma_start(out.rearrange("(t p) c -> p t c", p=P)[:, ts, :], x_tok[:, ts, :]).then_inc(out_done, 16)
            sp.wait_ge(out_done, BATCH * 16)

        @block.vector
        def _(dve):
            then = stepper(dve, vstep)

            def norm_stats(src, ready=None):
                for t in range(NT):
                    if ready:
                        ready(t)
                    ins = vec.bn_stats(stats[:, t, :], src[:, t, :])
                    ins.then_inc(stat_ready, 1)
                dve.wait_ge(stat_ready, NT * norms[0] + NT)
                for t in range(NT):
                    ins = vec.bn_aggr(mv[:, t, :], stats[:, t, :])
                    ins.then_inc(aggr_ready, 1)
                dve.wait_ge(aggr_ready, NT * norms[0] + NT)
                norms[0] += 1

            norms = [0]
            roots = [0]

            def rsqrt_asked(src, eps):
                TS(root_arg, src, eps, None, ALU.add).then_inc(var_ready, 1)

            def rsqrt_made(dst):
                roots[0] += 1
                dve.wait_ge(root_ready, roots[0])
                then(vec.reciprocal(dst, root))
                then(TT(sv[:, 3, :], root_arg, dst, ALU.mult))
                then(TT(sv[:, 3, :], sv[:, 3, :], dst, ALU.mult))
                then(TS(sv[:, 3, :], sv[:, 3, :], -0.5, 1.5, ALU.mult, ALU.add))
                then(TT(dst, dst, sv[:, 3, :], ALU.mult))

            def rsqrt(dst, src, eps):
                rsqrt_asked(src, eps)
                rsqrt_made(dst)

            root_arg, root = sv[:, 0, :], sv[:, 2, :]
            rstd, rrms = sv[:, 4, :], sv[:, 5, :]

            vec.memset(ones[:, :], 1.0).then_inc(ones_ready, 1)
            vec.memset(ssm[:, :, 0:TAPS - 1], 0.0).then_inc(pad_ready, 1)
            norm_stats(x_tok, lambda t: dve.wait_ge(x_in[t // TB], 16))
            rsqrt(rstd, mv[:, :, 1], 1e-5)
            then(TT(sv[:, 6, :], mv[:, :, 1], rstd, ALU.mult))
            then(TT(sv[:, 6, :], sv[:, 6, :], rstd, ALU.mult))
            rsqrt(rrms, sv[:, 6, :], 1e-6)
            then(TT(sv[:, 7, :], rstd, rrms, ALU.mult))
            for src, scale, ready in ((h_tok, sv[:, 7, :], h_ready), (xn_tok, rstd, xn_ready)):
                for t in range(NT):
                    TS(src[:, t, :], x_tok[:, t, :], mv[:, t, 0:1], scale[:, t:t + 1], ALU.subtract, ALU.mult).then_inc(ready, 1)
            for k in range(KC * BATCH):
                b, c = k // KC, k % KC
                cs = slice(b * HALF, (b + 1) * HALF)
                dve.wait_ge(hi_done, k + 1)
                TT(hT_lo[:, c, cs], hT[:, c, cs], hT_hi[:, c, cs].bitcast(F32), ALU.subtract).then_inc(lo_done, 1)
            for t in range(NT):
                dve.wait_ge(dtb_full, t + 1)
                vec.tensor_copy(dtB[:, t, :], bank[t % 2][:, 0:NH + P]).then_inc(dtb_taken, 1)
            dve.wait_ge(dtb_taken, NT)
            dve.wait_ge(par_in, 16)
            v, az, z, u, d, lg = (dts[:, i, :, :] for i in range(6))
            dt, la = dts[:, 6, :, :], dts[:, 7, :, :]
            then(TT(v, dtB[:, :, 0:NH], cols("dt_bias").unsqueeze(1).to_broadcast([P, NT, NH]), ALU.add))
            then(TS(az, v, -1.0, None, ALU.mult))
            TT(az, az, v, ALU.min).then_inc(az_ready, 1)
            dve.wait_ge(z_ready, 1)
            then(TS(u, z, 1.0, None, ALU.add))
            TS(d, u, -1.0, None, ALU.add).then_inc(u_ready, 1)
            dve.wait_ge(lg_ready, 1)
            dve.wait_ge(u_ready, 1)
            then(TS(az, d, 0.0, None, ALU.is_equal))
            then(TT(d, d, az, ALU.add))
            then(TT(lg, lg, az, ALU.add))
            then(TT(lg, lg, z, ALU.mult))
            then(vec.reciprocal(u, d))
            then(TT(lg, lg, u, ALU.mult))
            then(TS(v, v, 0.0, None, ALU.max))
            then(TT(dt, v, lg, ALU.add))
            dve.wait_ge(a_ready, 1)
            then(TS(a_neg[:, :], a_neg[:, :], -1.0, None, ALU.mult))
            TT(la, dt, a_neg[:, :].unsqueeze(1).to_broadcast([P, NT, NH]), ALU.mult).then_inc(dt_ready, 1)
            def choose_experts():
                dve.wait_ge(route_full, 1)
                vec.tensor_copy(route[:, :, :], bank[1][:, 0:NT * E].rearrange("p (t e) -> p t e", e=E)).then_inc(route_taken, 1)
                dve.wait_ge(route_taken, 1)
                for t in range(NT):
                    vec.max(top[:, t, :], route[:, t, :]).then_inc(top_ready, 1)
                dve.wait_ge(top_ready, NT)
                for t in range(NT):
                    vec.max_index(topi[:, t, :], top[:, t, :], route[:, t, :]).then_inc(topi_ready, 1)
                dve.wait_ge(topi_ready, NT)
                TT(pr[:, 0, :], top[:, :, 1], top[:, :, 0], ALU.subtract).then_inc(diff_ready, 1)
                then(vec.tensor_copy(topf[:, :, :], topi[:, :, 0:2]))
                for k in range(2):
                    then(TT(onehot[:, :, k, :], expert_no.unsqueeze(1).to_broadcast([P, NT, E]),
                            topf[:, :, k].unsqueeze(2).to_broadcast([P, NT, E]), ALU.is_equal))

            def weigh_experts():
                dve.wait_ge(e2_ready, 1)
                then(TS(pr[:, 2, :], pr[:, 1, :], 1.0, None, ALU.add))
                then(vec.reciprocal(pr[:, 3, :], pr[:, 2, :]))
                then(TT(pr[:, 4, :], pr[:, 1, :], pr[:, 3, :], ALU.mult))
                for k in range(2):
                    then(TT(onehot[:, :, k, :], onehot[:, :, k, :],
                            pr[:, 3 + k, :].unsqueeze(2).to_broadcast([P, NT, E]), ALU.mult))
                then(TT(cmb[:, :, :], onehot[:, :, 0, :], onehot[:, :, 1, :], ALU.add))
                then(vec.tensor_copy(cmb_h[:, :, :], cmb[:, :, :]))
                then(vec.tensor_copy(cmb_hl[:, :, 0:E], cmb_h[:, :, :].bitcast(F32)))
                TT(cmb_hl[:, :, E:2 * E], cmb[:, :, :], cmb_h[:, :, :].bitcast(F32), ALU.subtract).then_inc(comb_ready, 1)

            for b in range(BATCH):
                if b:
                    choose_experts()
                for m in range(NCH):
                    n = b * NCH + m
                    cs = slice(b * HALF, (b + 1) * HALF)
                    dve.wait_ge(conv_start, n + 1)
                    if n == 0:
                        dve.wait_ge(pad_ready, 1)
                    for j in range(TAPS - 1):
                        ins = STT(out=xs[:, m, cs], in0=ssm[:, m, j:j + SEQ], scalar=col("conv_w", m * TAPS + j),
                                  in1=xs[:, m, cs], op0=ALU.mult, op1=ALU.add)
                        ins.then_inc(conv_done, 1)
                        dve.wait_ge(conv_done, (TAPS - 1) * n + j + 1)
            for k in range(KC * BATCH):
                b, c = k // KC, k % KC
                cs = slice(b * HALF, (b + 1) * HALF)
                dve.wait_ge(hi_done, KC * BATCH + k + 1)
                TT(xnT_lo[:, c, cs], xnT[:, c, cs], xnT_hi[:, c, cs].bitcast(F32), ALU.subtract).then_inc(lo_done, 1)

            def lower_y(c):
                ts = slice(c * P, (c + 1) * P)
                dve.wait_ge(y_hi_done, c + 1)
                TT(y_lo[:, :, ts], gate[:, :, ts], y_hi[:, :, ts].bitcast(F32), ALU.subtract).then_inc(y_lo_done, 1)

            def residual(b):
                cs = slice(b * HALF, (b + 1) * HALF)
                for m in range(KC):
                    dve.wait_ge(s_full, b * KC + m + 1)
                    TT(sT[:, m, cs], bank[6 * (1 - b) + m][:, :], xnT[:, m, cs], ALU.add).then_inc(s_part, 1)

            def scan_front(c):
                dve.wait_ge(cb_full, c + 1)
                if c > 1:
                    dve.wait_ge(mix_ready, c - 1)
                TT(cbm[:, c % 2, :], bank[2][:, 0:P], upto, ALU.mult).then_inc(cbm_ready, 1)
                dve.wait_ge(exps_ready, c + 1)
                dve.wait_ge(dt_ready, 1)
                if c > 1:
                    dve.wait_ge(state_full, c - 1)
                then(TT(w_end[:, c % 2, :], dt[:, c, :], within[:, c % 2, :, P - 1], ALU.mult))
                dve.wait_ge(xt_full, c + 1)
                xt = bank[3][:, :].rearrange("p (h q) -> p h q", h=NH)
                TT(x_dt[:, c % 2, :, :], xt, dt[:, c, :].unsqueeze(2).to_broadcast([P, NH, P]), ALU.mult).then_inc(xdt_ready, 1)
                TT(x_end[:, c % 2, :, :], xt, w_end[:, c % 2, :].unsqueeze(2).to_broadcast([P, NH, P]), ALU.mult).then_inc(xend_ready, 1)

            def scan_back(c):
                ts = slice(c * P, (c + 1) * P)
                yv, added = (bank[i][:, :].rearrange("p (h q) -> p h q", h=NH) for i in (4, 5))
                dve.wait_ge(y_full, c + 1)
                if c % TB:
                    then(TT(state[:, :, :], state[:, :, :], since[:, c % 2, :, P - 1].unsqueeze(2).to_broadcast([P, NH, P]), ALU.mult))
                dve.wait_ge(state_full, c + 1)
                if c % TB:
                    TT(state[:, :, :], state[:, :, :], added, ALU.add).then_inc(state_ready, 1)
                else:
                    vec.tensor_copy(state[:, :, :], added).then_inc(state_ready, 1)
                dve.wait_ge(dx_ready, c + 1)
                then(TT(dx[:, c % 2, :, :], yv, dx[:, c % 2, :, :], ALU.add))
                TT(gate[:, :, ts], dx[:, c % 2, :, :], gate[:, :, ts], ALU.mult).then_inc(y_ready, 1)

            for c in range(NT + 1):
                if c < NT:
                    scan_front(c)
                if c > 0:
                    scan_back(c - 1)
                if c > 1:
                    lower_y(c - 2)
                if c == 1:
                    weigh_experts()
            lower_y(NT - 1)
            residual(0)
            residual(1)
            end_phase(dve)

            vec.memset(zero_b[:, :], 0.0).then_inc(zero_ready, 1)
            for n in range(1, 2 * NCOMB, 2):
                dve.wait_ge(spread_full, n + 1)
                vec.tensor_copy(comb[:, n // 2, HALF:T], bank[n % 4][:, :]).then_inc(spread_v, 1)

            def expert(e, chunks):
                for i in range(chunks):
                    for s in range(2):
                        u = e * (2 * FULL) + (2 * i + s)
                        dve.wait_ge(ab_full, u + 1)
                        dve.wait_ge(weighted, u + 1)
                        TT(act_h[:, s, :], act_c[:, s, :], bank[2 + s][:, :], ALU.mult).then_inc(h_made, 1)
                        dve.wait_ge(hhi_done, u + 1)
                        TT(h_lo[:, s, :], act_h[:, s, :], h_hi[:, s, :].bitcast(F32), ALU.subtract).then_inc(hlo_done, 1)

            with dve.Fori(0, E) as e:
                expert(e, FULL)
            expert(E, NTAIL)
            for n in range(KC * BATCH):
                s, m = n // KC, n % KC
                cs = slice(s * HALF, (s + 1) * HALF)
                dve.wait_ge(g_ready, n + 1)
                TT(sT[:, m, cs], sT[:, m, cs], gT[:, m, cs], ALU.mult).then_inc(sg_ready, 1)
            for n in range(NT // 2):
                dve.wait_ge(back_full, n + 1)
                xt2 = x_tok[:, 2 * n:2 * n + 2, :]
                TT(xt2, xt2, bank[n][:, :].rearrange("p (t c) -> p t c", c=C), ALU.add).then_inc(x_ready, 1)
            end_phase(dve)

            norm_stats(x_tok)
            rsqrt(rstd, mv[:, :, 1], 1e-5)
            for t in range(NT):
                TS(xn1[:, t, :], x_tok[:, t, :], mv[:, t, 0:1], rstd[:, t:t + 1], ALU.subtract, ALU.mult).then_inc(xn_ready, 1)
            for k in range(KC * BATCH):
                b, c = k // KC, k % KC
                cs = slice(b * HALF, (b + 1) * HALF)
                dve.wait_ge(hi_done, 2 * KC * BATCH + k + 1)
                TT(xnT_lo[:, c, cs], bank[k][:, :], xnT_hi[:, c, cs].bitcast(F32), ALU.subtract).then_inc(lo_done, 1)

            def gating(part):
                if part == 0:
                    dve.wait_ge(xn_ready, 2 * NT)
                    norm_stats(xn1)
                    rsqrt_asked(mv[:, :, 1], 1e-5)
                elif part == 1:
                    rsqrt_made(rrms)
                    for t in range(NT):
                        TS(xn2[:, t, :], xn1[:, t, :], mv[:, t, 0:1], rrms[:, t:t + 1], ALU.subtract, ALU.mult).then_inc(h_ready, 1)
                elif part == 2:
                    dve.wait_ge(wsg_in, 16)
                    then(vec.reduce_sum(wst[:, :, 0:1], wsg[:, :, :], axis=AX.X))
                    then(TS(wst[:, :, 1:2], wst[:, :, 0:1], 1.0 / C, None, ALU.mult))
                    for m in range(KC):
                        TS(wcen[:, m, :], wsg[:, m, :], wst[:, m, 1:2], None, ALU.subtract).then_inc(wcen_ready, 1)
                    TT(ab[:, :], cols("alpha"), cols("bias"), ALU.mult).then_inc(ab_ready, 1)

            def prep_v(g, a, t, qk_bank):
                tt = g * NT + t
                sl, hd2 = t % 2, HD // 2
                cosv = rp[:, t % TB, 0, :].unsqueeze(1).to_broadcast([P, NR, HD])
                sinv = rp[:, t % TB, 1, :].unsqueeze(1).to_broadcast([P, NR, HD])
                qk = qk_bank[:, 0:NR * HD].rearrange("p (h d) -> p h d", d=HD)
                dve.wait_ge(v_hi_done, tt + 1)
                if not isinstance(tt, int) or tt > 1:
                    dve.wait_ge(qklo_done, tt - 1)
                TT(qkr[:, sl, :, :], qk, cosv, ALU.mult)
                TT(rot[:, sl, :, 0:hd2], qk[:, :, hd2:HD], sinv[:, :, 0:hd2], ALU.mult)
                TT(rot[:, sl, :, hd2:HD], qk[:, :, 0:hd2], sinv[:, :, hd2:HD], ALU.mult).then_inc(turned, 1)
                TT(v_lo[:, a, t, HD:2 * HD], qk_bank[:, NR * HD:GW], v_hi[:, a, t, HD:2 * HD].bitcast(F32),
                   ALU.subtract).then_inc(b6_free, 1)

            def attend(now, now_set, steps):
                for late, op, i, k in steps:
                    g, a = (now - 1, 1 - now_set) if late else (now, now_set)
                    q = g * PAIRS + i
                    u = q * 5 + k
                    if op == "S":
                        bk = bank[(i + k) % 2]
                        dve.wait_ge(score_full, u + 1)
                        segs = SCORES[k]
                        if k == 2:
                            vec.tensor_reduce(out=nmax[:, i % 2, :, 1:2], in_=bk[:, :].rearrange("p (h n) -> p h n", h=2),
                                              op=ALU.max, axis=AX.X, negate=True).then_inc(max_ready, 1)
                        else:
                            for h, j, at in segs:
                                ins = vec.tensor_reduce(out=nmax[:, i % 2, h, j:j + 1], in_=bk[:, at:at + (j + 1) * P],
                                                        op=ALU.max, axis=AX.X, negate=True)
                            ins.then_inc(max_ready, 1)
                    elif op == "N":
                        dve.wait_ge(exp_done, q * 5 + (HEADS_AT[k] + 2))
                        vec.reciprocal(rinv[:, i % 2, k, :], rsum[:, i % 2, k, :]).then_inc(rinv_ready, 1)
                    elif op == "T":
                        b_ = (i + k) % 4
                        dve.wait_ge(phi_done, u + 1)
                        TT(p_lo[:, b_, :], bank[2 + b_ % 2][:, :], p_hi[:, b_, :].bitcast(F32), ALU.subtract).then_inc(plo_done, 1)
                    elif op == "O":
                        b, m = i // 2, i % 2
                        dve.wait_ge(ohi_done, q + 1)
                        TT(o_lo[:, b, m, :], bank[4 + m][:, :], o_hi[:, b, m, :].bitcast(F32), ALU.subtract).then_inc(olo_done, 1)
                    elif op == "W":
                        b, m = i // KC, i % KC
                        cs = slice(b * HALF, (b + 1) * HALF)
                        dve.wait_ge(wo_full, g * (BATCH * KC) + (i + 2))
                        TT(sT[:, m, cs], sT[:, m, cs], bank[6][:, :], ALU.add).then_inc(b6_free, 1)
                    elif op == "Q":
                        prep_v(g + 1, 1 - a, i, bank[6])

            dve.wait_ge(rope_in, 16)
            for op, i, k in PREP:
                if op == "Q":
                    prep_v(0, 0, i, bank[i % 3])
                elif op == "F":
                    gating(i)
            dve.wait_ge(vpad_ready, 5)
            attend(0, 0, schedule(False, True, True, True))
            with dve.Fori(0, KVH // 2 - 1) as gp:
                for a in range(2):
                    attend(gp * 2 + (1 + a), 1 - a, schedule(True, True, True, True))
            attend(KVH - 1, 1, schedule(True, True, True, False))
            attend(KVH, 0, schedule(True, False, False, False))
            dve.wait_ge(b6_free, NT * KVH + BATCH * KC * KVH)
            for n in range(KC * BATCH):
                s, m = n // KC, n % KC
                cs = slice(s * HALF, (s + 1) * HALF)
                dve.wait_ge(g1_ready, KC * BATCH)
                TT(sT[:, m, cs], sT[:, m, cs], g1T[:, m, cs], ALU.mult).then_inc(sg_ready, 1)
            for n in range(NT // 2):
                dve.wait_ge(back_full, NT // 2 + n + 1)
                xt2 = x_tok[:, 2 * n:2 * n + 2, :]
                TT(xt2, xt2, bank[n][:, :].rearrange("p (t c) -> p t c", c=C), ALU.add).then_inc(x_ready, 1)

        @block.scalar
        def _(act):
            actv = nc.scalar.activation

            def root(n):
                act.wait_ge(var_ready, n + 1)
                actv(sv[:, 2, :], sv[:, 0, :], ACT.Sqrt).then_inc(root_ready, 1)

            root(0)
            root(1)
            act.wait_ge(w_in_in, 16)
            actv(w_in_hi[:, :, :], w_in_sb[:, :, :], ACT.Copy).then_inc(w_in_hi_done, 1)
            act.wait_ge(par_in, 16)
            act.wait_ge(cst_in, 16)
            for k in range(2 * KC * BATCH):
                b, c = k // KC % BATCH, k % KC
                cs = slice(b * HALF, (b + 1) * HALF)
                act.wait_ge(tr_full, k + 1)
                if k < KC * BATCH:
                    actv(hT[:, c, cs], bank[k][:, :], ACT.Copy, scale=col("norm_scale", c))
                    actv(hT_hi[:, c, cs], bank[k][:, :], ACT.Copy, scale=col("norm_scale", c)).then_inc(hi_done, 1)
                else:
                    actv(xnT[:, c, cs], bank[k][:, :], ACT.Copy)
                    actv(xnT_hi[:, c, cs], bank[k][:, :], ACT.Copy).then_inc(hi_done, 1)
            actv(a_neg[:, :], cols("A_log"), ACT.Exp).then_inc(a_ready, 1)
            act.wait_ge(az_ready, 1)
            actv(dts[:, 2, :, :], dts[:, 1, :, :], ACT.Exp).then_inc(z_ready, 1)
            act.wait_ge(u_ready, 1)
            actv(dts[:, 5, :, :], dts[:, 3, :, :], ACT.Ln).then_inc(lg_ready, 1)
            act.wait_ge(w_out_in, 16)
            actv(w_out_hi[:, :, :], w_out_sb[:, :, :], ACT.Copy).then_inc(w_out_hi_done, 1)
            n = 0
            for b in range(BATCH):
                cs = slice(b * HALF, (b + 1) * HALF)
                for kind, m in PROJS:
                    bk = bank[2 + n % 6]
                    act.wait_ge(pr_full, n + 1)
                    if kind == "ssm":
                        if b:
                            act.wait_ge(conv_done, (TAPS - 1) * (m + 1))
                        actv(ssm[:, m, TAPS - 1:TAPS - 1 + SEQ], bk[:, :], ACT.Copy).then_inc(ssm_in, 1)
                    elif kind == "B":
                        actv(BT[:, cs], bk[:, :], ACT.Copy).then_inc(pr_taken, 1)
                    elif kind == "C":
                        actv(CT[:, cs], bk[:, :], ACT.Copy).then_inc(pr_taken, 1)
                    else:
                        actv(gate[:, m, cs], bk[:, :], ACT.Silu).then_inc(pr_taken, 1)
                    n += 1
                for m in range(NCH):
                    act.wait_ge(conv_done, (TAPS - 1) * (b * NCH + m + 1))
                    actv(xs[:, m, cs], xs[:, m, cs], ACT.Silu).then_inc(xs_ready, 1)
            def upper_y(c):
                ts = slice(c * P, (c + 1) * P)
                act.wait_ge(y_ready, c + 1)
                actv(y_hi[:, :, ts], gate[:, :, ts], ACT.Copy).then_inc(y_hi_done, 1)

            act.wait_ge(diff_ready, 1)
            actv(pr[:, 1, :], pr[:, 0, :], ACT.Exp).then_inc(e2_ready, 1)
            for c in range(NT + 1):
                if c == 2:
                    act.wait_ge(sel_in, 16)
                    actv(sel_r[:, :], sel[:, :], ACT.Copy).then_inc(sel_ready, 1)
                if c == TB:
                    for s in range(2):
                        act.wait_ge(combt_full, s + 1)
                        actv(combT[:, s * HALF:(s + 1) * HALF], bank[6 + s][0:2 * E, :], ACT.Copy).then_inc(combt_ready, 1)
                if c < NT:
                    act.wait_ge(decay_full, c + 1)
                    if c > 1:
                        act.wait_ge(mix_ready, c - 1)
                        if carried(c - 2):
                            act.wait_ge(cdec_ready, carried(c - 2))
                        act.wait_ge(xend_ready, c - 1)
                        act.wait_ge(state_ready, c - 1)
                    actv(within[:, c % 2, :, :], bank[0][:, :].rearrange("p (h q) -> p h q", h=NH), ACT.Exp)
                    actv(since[:, c % 2, :, :], bank[1][:, :].rearrange("p (h q) -> p h q", h=NH), ACT.Exp).then_inc(exps_ready, 1)
                    act.wait_ge(xs_ready, (c // TB + 1) * NCH)
                    if c > 1:
                        act.wait_ge(y_ready, c - 1)
                    for h in range(NCH):
                        ins = actv(dx[:, c % 2, h, :], xs[:, h, c * P:(c + 1) * P], ACT.Copy, scale=col("D", h))
                    ins.then_inc(dx_ready, 1)
                if c > 1:
                    upper_y(c - 2)
            upper_y(NT - 1)
            end_phase(act)

            def split_hi(slot, n, arrived):
                act.wait_ge(slot_in[slot], arrived)
                act.wait_ge(hslot_free, n * 2 + 2)
                actv(w_hi[:, slot, :], wraw[:, slot, :], ACT.Copy).then_inc(whi_done, 1)

            for n in range(0, 2 * NCOMB, 2):
                if n == 6:
                    split_hi(0, 0, 16)
                act.wait_ge(spread_full, n + 1)
                actv(comb[:, n // 2, 0:HALF], bank[n % 4][:, :], ACT.Copy).then_inc(spread_a, 1)
            split_hi(1, 1, 16)

            def expert(e, chunks, tail_next):
                for i in range(chunks):
                    for s in range(2):
                        u = e * (2 * FULL) + (2 * i + s)
                        act.wait_ge(ab_full, u + 1)
                        actv(act_s[:, s, :], bank[s][:, :], ACT.Silu).then_inc(silu_done, 1)
                        if s == 0 and (i + 2 < chunks or tail_next):
                            j = i + 2
                            split_hi(j % FULL, e * FULL + j, (e + (1 + j // FULL)) * 16)
                        act.wait_ge(h_made, u + 1)
                        act.wait_ge(hslot_free, u + (2 * FULL - 1))
                        actv(h_hi[:, s, :], act_h[:, s, :], ACT.Copy).then_inc(hhi_done, 1)

            with act.Fori(0, E) as e:
                expert(e, FULL, True)
            expert(E, NTAIL, False)
            act.wait_ge(hslot_free, 2 * (E * FULL + NTAIL + FULL))
            for n in range(KC * BATCH):
                s, m = n // KC, n % KC
                actv(gT[:, m, s * HALF:(s + 1) * HALF], bank[4 + 2 * m + s][:, :], ACT.Silu).then_inc(g_ready, 1)
            end_phase(act)

            for j in (0, 2, 3):
                actv(id_b[:, j * P:(j + 1) * P], ident, ACT.Copy)
            actv(id_b[:, P:2 * P], ident, ACT.Copy, scale=0.0).then_inc(mask_ready, 1)
            actv(mask_b[:, :], after, ACT.Copy, scale=MASKED).then_inc(mask_ready, 1)
            actv(id_r[:, :], ident, ACT.Copy).then_inc(mask_ready, 1)
            root(2)
            act.wait_ge(qkv_in, 16)
            actv(qkv_hi[:, :, :], qkv_raw[:, :, :], ACT.Copy).then_inc(qkvhi_done, 1)
            for k in range(KC * BATCH):
                b, c = k // KC, k % KC
                act.wait_ge(tr_full, 2 * KC * BATCH + k + 1)
                actv(xnT_hi[:, c, b * HALF:(b + 1) * HALF], bank[k][:, :], ACT.Copy).then_inc(hi_done, 1)

            def gating(part):
                if part == 0:
                    root(3)
                elif part == 2:
                    for m in range(KC):
                        act.wait_ge(wcen_ready, m + 1)
                        actv(wsg[:, m, :], wcen[:, m, :], ACT.Sign).then_inc(wsign_ready, 1)
                elif part == 3:
                    for k in range(KC * BATCH):
                        b, c = k // KC, k % KC
                        act.wait_ge(tr_full, 3 * KC * BATCH + k + 1)
                        actv(signT[:, c, b * HALF:(b + 1) * HALF], bank[4 + k % 3][:, :], ACT.Sign, scale=col("gamma", c),
                             bias=col("beta", c)).then_inc(sign_ready, 1)
                elif part == 4:
                    act.wait_ge(wsT_full, 1)
                    actv(wsT[:, :, :], bank[4 + KC * BATCH % 3][:, :].rearrange("p (k o) -> p k o", k=KC), ACT.Copy).then_inc(wsT_ready, 1)
                elif part == 5:
                    act.wait_ge(ab_ready, 1)
                    for n in range(KC * BATCH):
                        m, s = n // 2, n % 2
                        act.wait_ge(sign_full, n + 1)
                        actv(g1T[:, m, s * HALF:(s + 1) * HALF], bank[4 + (KC * BATCH + 1 + n) % 3][:, :], ACT.Silu,
                             scale=col("alpha", m), bias=ab[:, m:m + 1]).then_inc(g1_ready, 1)

            def weights_q(g):
                act.wait_ge(qkv_in, g * 16 + 16)
                if not isinstance(g, int) or g:
                    act.wait_ge(qkv_full, g * NT)
                actv(qkv_hi[:, :, :], qkv_raw[:, :, :], ACT.Copy).then_inc(qkvhi_done, 1)

            def prep_copy(g, a, t, qk_bank):
                tt = g * NT + t
                act.wait_ge(qkv_full, tt + 1)
                if t == 0 and not (isinstance(g, int) and g <= 1):
                    act.wait_ge(av_done, (g - 1) * STEPS + (4 - STEPS // 2))
                if t == TB and not (isinstance(g, int) and g <= 1):
                    act.wait_ge(av_done, (g - 1) * STEPS + 4)
                actv(v_hi[:, a, t, HD:2 * HD], qk_bank[:, NR * HD:GW], ACT.Copy).then_inc(v_hi_done, 1)

            def prep_hi(g, t):
                tt = g * NT + t
                act.wait_ge(rope_done, tt + 1)
                if not isinstance(tt, int) or tt > 1:
                    act.wait_ge(tq_full, tt * 2 - 2)
                actv(qk_hl[:, t % 2, 0:NR, 0, :], qkr[:, t % 2, :, :], ACT.Copy)
                actv(qk_hl[:, t % 2, NR, 0, :], qkr[:, t % 2, GQ, :], ACT.Copy).then_inc(qkhi_done, 1)

            def prep_take(g, a, t, k, turn_bank):
                tt = g * NT + t
                act.wait_ge(tq_full, tt * 2 + (1 + k))
                dst = qT[:, a, :, t * P:(t + 1) * P] if k == 0 else kT[:, a, :, t * P:(t + 1) * P]
                n = GQ if k == 0 else 2
                actv(dst, turn_bank[:, 0:n * P].rearrange("p (h n) -> p h n", n=P), ACT.Copy,
                     scale=1.0 if k == 0 else HD ** -0.5).then_inc(tq_taken, 1)

            def attend(now, now_set, steps):
                for late, op, i, k in steps:
                    g, a = (now - 1, 1 - now_set) if late else (now, now_set)
                    q = g * PAIRS + i
                    u = q * 5 + k
                    if op == "E":
                        bk = bank[(i + k) % 2]
                        act.wait_ge(max_ready, u + 1)
                        if k == 0 and (not isinstance(g, int) or q > 1):
                            act.wait_ge(pt_full, q * 5 - 5)
                        for h, j, at in SCORES[k]:
                            ins = actv(prob[:, i % 2, h, POFF[j]:POFF[j] + (j + 1) * P], bk[:, at:at + (j + 1) * P], ACT.Exp,
                                       bias=nmax[:, i % 2, h, j:j + 1], accum_out=rsum[:, i % 2, h, j:j + 1])
                        ins.then_inc(exp_done, 1)
                    elif op == "T":
                        b_ = (i + k) % 4
                        act.wait_ge(pt_full, u + 1)
                        act.wait_ge(av_done, u + 1)
                        actv(p_hi[:, b_, :], bank[2 + b_ % 2][:, :], ACT.Copy).then_inc(phi_done, 1)
                    elif op == "O":
                        b, m = i // 2, i % 2
                        act.wait_ge(av_done, q * 5 + 9)
                        if m == 0 and not (isinstance(g, int) and b * KC + g * (BATCH * KC) <= 1):
                            act.wait_ge(wo_full, g * (BATCH * KC) + (b * KC - 1))
                        actv(o_hi[:, b, m, :], bank[4 + m][:, :], ACT.Copy).then_inc(ohi_done, 1)
                    elif op == "VO":
                        act.wait_ge(wo_in, g * 16 + 16)
                        act.wait_ge(wo_full, g * (BATCH * KC) + 1)
                        actv(wo_hi[:, :, :], wo_raw[:, :, :], ACT.Copy).then_inc(wohi_done, 1)
                    elif op == "VQ":
                        weights_q(g + 1)
                    elif op == "Q":
                        prep_copy(g + 1, 1 - a, i, bank[6])
                    elif op == "R":
                        prep_hi(g + 1, i)
                    elif op == "X":
                        prep_take(g + 1, 1 - a, i, k, bank[7])

            act.sem_inc(exp_done, 2)
            act.wait_ge(vpad_ready, 4)
            for op, i, k in PREP:
                if op == "Q":
                    prep_copy(0, 0, i, bank[i % 3])
                elif op == "R":
                    prep_hi(0, i)
                elif op == "X":
                    prep_take(0, 0, i, k, bank[7 - 4 * k])
                elif op == "F":
                    gating(i)
            attend(0, 0, schedule(False, True, True, True))
            with act.Fori(0, KVH // 2 - 1) as gp:
                for a in range(2):
                    attend(gp * 2 + (1 + a), 1 - a, schedule(True, True, True, True))
            attend(KVH - 1, 1, schedule(True, True, True, False))
            attend(KVH, 0, schedule(True, False, False, False))

        @block.gpsimd
        def _(gp_):
            GT = pool.tensor_tensor
            gp_.wait_ge(w_in_hi_done, 1)
            GT(w_in_lo[:, :, :], w_in_sb[:, :, :], w_in_hi[:, :, :].bitcast(F32), ALU.subtract).then_inc(w_in_ready, 1)
            gp_.wait_ge(w_out_hi_done, 1)
            GT(w_out_lo[:, :, :], w_out_sb[:, :, :], w_out_hi[:, :, :].bitcast(F32), ALU.subtract).then_inc(w_out_ready, 1)
            def first_tap(b):
                for m in range(NCH):
                    gp_.wait_ge(ssm_in, b * NCH + m + 1)
                    pool.tensor_scalar(xs[:, m, b * HALF:(b + 1) * HALF], ssm[:, m, TAPS - 1:TAPS - 1 + SEQ],
                                       col("conv_w", m * TAPS + TAPS - 1), col("conv_b", m), ALU.mult, ALU.add).then_inc(conv_start, 1)

            for b in range(BATCH):
                first_tap(b)
            gp_.wait_ge(dt_ready, 1)

            def decay(c):
                if c > 1:
                    gp_.wait_ge(decay_full, c - 1)
                GT(decay_in[:, c % 2, :, :], upto.unsqueeze(1).to_broadcast([P, NH, P]),
                   dts[:, 7, c, :].unsqueeze(2).to_broadcast([P, NH, P]), ALU.mult).then_inc(decay_ready, 1)

            decay(0)
            for c in range(NT):
                ts = slice(c * P, (c + 1) * P)
                if c + 1 < NT:
                    decay(c + 1)
                gp_.wait_ge(exps_ready, c + 1)
                gp_.wait_ge(cbm_ready, c + 1)
                if c > 1:
                    gp_.wait_ge(y_full, c - 1)
                GT(mix[:, c % 2, :, :], within[:, c % 2, :, :], cbm[:, c % 2, :].unsqueeze(1).to_broadcast([P, NH, P]),
                   ALU.mult).then_inc(mix_ready, 1)
                if c % TB:
                    GT(c_dec[:, c % 2, :, :], since[:, c % 2, :, :], CT[:, ts].unsqueeze(1).to_broadcast([P, NH, P]),
                       ALU.mult).then_inc(cdec_ready, 1)
            end_phase(gp_)

            def split_lo(slot, n):
                gp_.wait_ge(whi_done, n + 1)
                GT(w_lo[:, slot, :], wraw[:, slot, :], w_hi[:, slot, :].bitcast(F32), ALU.subtract).then_inc(wlo_done, 1)

            split_lo(0, 0)
            split_lo(1, 1)
            gp_.wait_ge(spread_a, NCOMB)
            gp_.wait_ge(spread_v, NCOMB)

            def expert(e, chunks, tail_next):
                for i in range(chunks):
                    which = bass.ds(e, 1) if chunks == FULL else slice(E + i, E + i + 1)
                    for s in range(2):
                        u = e * (2 * FULL) + (2 * i + s)
                        gp_.wait_ge(silu_done, u + 1)
                        gp_.sem_inc(silu_seen, 1)
                        GT(act_c[:, s, :], act_s[:, s, :], comb[:, which, s * HALF:(s + 1) * HALF].rearrange("p a n -> p (a n)"),
                           ALU.mult).then_inc(weighted, 1)
                        if s == 0 and (i + 2 < chunks or tail_next):
                            split_lo((i + 2) % FULL, e * FULL + (i + 2))

            with gp_.Fori(0, E) as e:
                expert(e, FULL, True)
            expert(E, NTAIL, False)
            end_phase(gp_)

            pool.memset(v_hi[:, :, :, 0:HD].bitcast(F32), 0.0).then_inc(vpad_ready, 1)
            pool.memset(v_hi[:, :, :, 2 * HD:3 * HD].bitcast(F32), 0.0).then_inc(vpad_ready, 1)
            pool.memset(v_lo[:, :, :, 2 * HD:3 * HD].bitcast(F32), 0.0).then_inc(vpad_ready, 1)
            pool.memset(v_lo[:, :, :, 0:HD].bitcast(F32), 0.0).then_inc(vpad_ready, 1)
            pool.memset(sT[:, :, :], 0.0).then_inc(vpad_ready, 1)

            def weights_q(g):
                gp_.wait_ge(qkvhi_done, g + 1)
                GT(qkv_lo[:, :, :], qkv_raw[:, :, :], qkv_hi[:, :, :].bitcast(F32), ALU.subtract).then_inc(qkvlo_done, 1)

            def prep_rope(g, t):
                tt = g * NT + t
                gp_.wait_ge(turned, tt + 1)
                GT(qkr[:, t % 2, :, :], qkr[:, t % 2, :, :], rot[:, t % 2, :, :], ALU.add).then_inc(rope_done, 1)

            def prep_lo(g, t):
                tt = g * NT + t
                gp_.wait_ge(qkhi_done, tt + 1)
                GT(qk_hl[:, t % 2, 0:NR, 1, :], qkr[:, t % 2, :, :], qk_hl[:, t % 2, 0:NR, 0, :].bitcast(F32),
                   ALU.subtract).then_inc(qklo_done, 1)

            def attend(now, now_set, steps):
                for late, op, i, k in steps:
                    g, a = (now - 1, 1 - now_set) if late else (now, now_set)
                    q = g * PAIRS + i
                    if op == "N":
                        gp_.wait_ge(rinv_ready, q * 2 + (k + 1))
                        for j in range(TB):
                            seg = prob[:, i % 2, k, POFF[j]:POFF[j] + (j + 1) * P]
                            ins = GT(seg, seg, rinv[:, i % 2, k, j:j + 1].to_broadcast([P, (j + 1) * P]), ALU.mult)
                        ins.then_inc(prob_ready, 1)
                    elif op == "VO":
                        gp_.wait_ge(wohi_done, g + 1)
                        GT(wo_lo[:, :, :], wo_raw[:, :, :], wo_hi[:, :, :].bitcast(F32), ALU.subtract).then_inc(wolo_done, 1)
                    elif op == "VQ":
                        weights_q(g + 1)
                    elif op == "Q":
                        prep_rope(g + 1, i)
                    elif op == "R":
                        prep_lo(g + 1, i)

            weights_q(0)
            for op, i, k in PREP:
                if op == "Q":
                    prep_rope(0, i)
                elif op == "R":
                    prep_lo(0, i)
            attend(0, 0, schedule(False, True, True, True))
            with gp_.Fori(0, KVH // 2 - 1) as gp:
                for a in range(2):
                    attend(gp * 2 + (1 + a), 1 - a, schedule(True, True, True, True))
            attend(KVH - 1, 1, schedule(True, True, True, False))
            attend(KVH, 0, schedule(True, False, False, False))

        @block.tensor
        def _(pe):
            def tr(dst, src):
                return nc.tensor.transpose(dst, src, ident)

            def split3(dst, w_h, w_l, m_h, m_l, start, stop):
                mm(dst, w_l, m_h, start=start, stop=False)
                mm(dst, w_h, m_l, start=False, stop=False)
                return mm(dst, w_h, m_h, start=False, stop=stop)

            pe.wait_ge(cst_in, 16)
            for k in range(2 * KC * BATCH):
                b, c = k // KC % BATCH, k % KC
                src, ready = (h_tok, h_ready) if k < KC * BATCH else (xn_tok, xn_ready)
                pe.wait_ge(ready, (b + 1) * TB)
                for t in range(TB):
                    ins = tr(bank[k][:, t * P:(t + 1) * P], src[:, b * TB + t, c * P:(c + 1) * P])
                ins.then_inc(tr_full, 1)
            pe.wait_ge(hi_done, KC * BATCH)
            pe.wait_ge(w_in_in, 16)
            for t in range(NT):
                if t > 1:
                    pe.wait_ge(dtb_taken, t - 1)
                for c in range(KC):
                    ins = mm(bank[t % 2][:, 0:NH + P], hT[:, c, t * P:(t + 1) * P], w_in_sb[:, c, DT0:DT0 + NH + P],
                             start=c == 0, stop=c == KC - 1)
                ins.then_inc(dtb_full, 1)
            pe.wait_ge(w_in_ready, 1)
            pe.wait_ge(lo_done, KC * BATCH)
            pe.wait_ge(hi_done, 2 * KC * BATCH)
            n = 0
            for b in range(BATCH):
                cs = slice(b * HALF, (b + 1) * HALF)
                for kind, m in PROJS:
                    at = {"gate": m * P, "ssm": DI + m * P, "B": B0, "C": C0}[kind]
                    bk = bank[2 + n % 6]
                    if n >= 6:
                        taken = [j for j in range(n - 5)]
                        convs = sum(PROJS[j % len(PROJS)][0] == "ssm" for j in taken)
                        pe.wait_ge(ssm_in, convs)
                        if len(taken) > convs:
                            pe.wait_ge(pr_taken, len(taken) - convs)
                    for c in range(KC):
                        ins = split3(bk[:, :], w_in_hi[:, c, at:at + P], w_in_lo[:, c, at:at + P],
                                     hT_hi[:, c, cs], hT_lo[:, c, cs], c == 0, c == KC - 1)
                    ins.then_inc(pr_full, 1)
                    n += 1
                if b == 0:
                    pe.wait_ge(dtb_taken, NT)
                    for t in range(NT):
                        for c in range(KC):
                            ins = mm(bank[1][:, t * E:(t + 1) * E], xnT[:, c, t * P:(t + 1) * P],
                                     par[:, PARAMS["gate_w"][0] + c * E:PARAMS["gate_w"][0] + (c + 1) * E], start=c == 0, stop=c == KC - 1)
                    ins.then_inc(route_full, 1)
            def out_product(b):
                cs = slice(b * HALF, (b + 1) * HALF)
                pe.wait_ge(w_out_ready, 1)
                pe.wait_ge(y_lo_done, (b + 1) * TB)
                for m in range(KC):
                    for k in range(NCH):
                        ins = split3(bank[6 * (1 - b) + m][:, :], w_out_hi[:, k, m * P:(m + 1) * P], w_out_lo[:, k, m * P:(m + 1) * P],
                                     y_hi[:, k, cs], y_lo[:, k, cs], k == 0, k == NCH - 1)
                    ins.then_inc(s_full, 1)

            pe.wait_ge(ones_ready, 1)
            pe.wait_ge(pr_taken, BATCH * (NCH + 2))
            pe.wait_ge(ssm_in, BATCH * NCH)
            def scan_front(c):
                ts = slice(c * P, (c + 1) * P)
                pe.wait_ge(decay_ready, c + 1)
                if c:
                    pe.wait_ge(exps_ready, c)
                else:
                    pe.wait_ge(route_taken, 1)
                dec = decay_in[:, c % 2, :, :].rearrange("p h q -> p (h q)")
                mm(bank[0][:, :], after, dec, start=True, stop=True)
                mm(bank[1][:, :], ones[:, :], dec, start=True, stop=True).then_inc(decay_full, 1)
                if c:
                    pe.wait_ge(cbm_ready, c)
                mm(bank[2][:, 0:P], BT[:, ts], CT[:, ts], start=True, stop=True).then_inc(cb_full, 1)
                pe.wait_ge(xs_ready, (c // TB + 1) * NCH)
                if c:
                    pe.wait_ge(xend_ready, c)
                for h in range(NH):
                    ins = tr(bank[3][:, h * P:(h + 1) * P], xs[:, h, ts])
                ins.then_inc(xt_full, 1)

            def scan_back(c):
                pe.wait_ge(mix_ready, c + 1)
                pe.wait_ge(xdt_ready, c + 1)
                if c % TB:
                    pe.wait_ge(cdec_ready, carried(c))
                if c:
                    pe.wait_ge(state_ready, c)
                    pe.wait_ge(y_ready, c)
                for h in range(NH):
                    dst = bank[4][:, h * P:(h + 1) * P]
                    ins = mm(dst, x_dt[:, c % 2, h, :], mix[:, c % 2, h, :], start=True, stop=c % TB == 0)
                    if c % TB:
                        ins = mm(dst, state[:, h, :], c_dec[:, c % 2, h, :], start=False, stop=True)
                ins.then_inc(y_full, 1)
                pe.wait_ge(xend_ready, c + 1)
                mm(bank[5][:, :], dtB[:, c, NH:NH + P], x_end[:, c % 2, :, :].rearrange("p h q -> p (h q)"),
                   start=True, stop=True).then_inc(state_full, 1)

            for c in range(NT + 1):
                if c < NT:
                    scan_front(c)
                if c > 0:
                    scan_back(c - 1)
                if c == 3:
                    pe.wait_ge(comb_ready, 1)
                    for s in range(2):
                        for t in range(TB):
                            ins = tr(bank[6 + s][0:2 * E, t * P:(t + 1) * P], cmb_hl[:, s * TB + t, :])
                        ins.then_inc(combt_full, 1)
            pe.wait_ge(combt_ready, 2)
            out_product(0)
            out_product(1)
            end_phase(pe)

            pe.sem_inc(hslot_free, 2 * FULL)
            pe.wait_ge(zero_ready, 1)
            for n in range(KC * BATCH):
                mm(bank[4 + n][:, :], zero_b[:, 0:P], zero_b[:, :], start=True, stop=False)
            for n in range(2 * NCOMB):
                k, s = n // 2, n % 2
                if n >= 4:
                    pe.wait_ge(spread_a if n % 2 == 0 else spread_v, (n - 4) // 2 + 1)
                mm(bank[n % 4][:, :], sel_r[:, k * P:(k + 1) * P], combT[:, s * HALF:(s + 1) * HALF],
                   start=True, stop=True).then_inc(spread_full, 1)
            pe.wait_ge(spread_a, NCOMB)
            pe.wait_ge(spread_v, NCOMB)

            def in_products(slot, s):
                cs = slice(s * HALF, (s + 1) * HALF)
                for bk, at in ((bank[s], 0), (bank[2 + s], FC2)):
                    for c in range(KC):
                        w = slice(at + c * P, at + (c + 1) * P)
                        ins = split3(bk[:, :], w_hi[:, slot, w], w_lo[:, slot, w], xnT_hi[:, c, cs], xnT_lo[:, c, cs],
                                     c == 0, c == KC - 1)
                ins.then_inc(ab_full, 1)

            pe.wait_ge(wlo_done, 1)
            in_products(0, 0)
            in_products(0, 1)

            def expert(e, chunks, tail_next):
                for i in range(chunks):
                    for s in range(2):
                        u = e * (2 * FULL) + (2 * i + s)
                        if i + 1 < chunks or tail_next:
                            if s == 0:
                                pe.wait_ge(wlo_done, e * FULL + (i + 2))
                            pe.wait_ge(h_made, u + 1)
                            in_products((i + 1) % FULL, s)
                        pe.wait_ge(hlo_done, u + 1)
                        last = chunks == NTAIL and i == chunks - 1
                        for m in range(KC):
                            w = slice(PJ + m * P, PJ + (m + 1) * P)
                            ins = split3(bank[4 + 2 * m + s][:, :], w_hi[:, i, w], w_lo[:, i, w], h_hi[:, s, :], h_lo[:, s, :], False, last)
                        ins.then_inc(hslot_free, 1)

            with pe.Fori(0, E) as e:
                expert(e, FULL, True)
            expert(E, NTAIL, False)
            for n in range(NT // 2):
                pe.wait_ge(sg_ready, KC * (n // (TB // 2) + 1))
                for j in range(2 * KC):
                    t, m = 2 * n + j // KC, j % KC
                    ins = tr(bank[n][:, j * P:(j + 1) * P], sT[:, m, t * P:(t + 1) * P])
                ins.then_inc(back_full, 1)
            end_phase(pe)

            def turn_norm(k, src, ready, bk):
                b, c = k // KC, k % KC
                pe.wait_ge(ready, NT + (b + 1) * TB)
                for t in range(TB):
                    ins = tr(bk[:, t * P:(t + 1) * P], src[:, b * TB + t, c * P:(c + 1) * P])
                ins.then_inc(tr_full, 1)

            for k in range(KC * BATCH):
                turn_norm(k, xn1, xn_ready, bank[k])
            pe.wait_ge(lo_done, 3 * KC * BATCH)

            def gating(part):
                if part == 3:
                    for k in range(KC * BATCH):
                        if k >= 3:
                            pe.wait_ge(sign_ready, k - 2)
                        turn_norm(k, xn2, h_ready, bank[4 + k % 3])
                elif part == 4:
                    pe.wait_ge(wsign_ready, KC)
                    pe.wait_ge(sign_ready, KC * BATCH - 2)
                    for k in range(KC):
                        for m in range(KC):
                            ins = tr(bank[4 + KC * BATCH % 3][:, (k * KC + m) * P:(k * KC + m + 1) * P], wsg[:, m, k * P:(k + 1) * P])
                    ins.then_inc(wsT_full, 1)
                elif part == 5:
                    pe.wait_ge(wsT_ready, 1)
                    pe.wait_ge(sign_ready, KC * BATCH)
                    for n in range(KC * BATCH):
                        m, s = n // 2, n % 2
                        if n >= 3:
                            pe.wait_ge(g1_ready, n - 2)
                        for c in range(KC):
                            ins = mm(bank[4 + (KC * BATCH + 1 + n) % 3][:, :], wsT[:, c, m * P:(m + 1) * P],
                                     signT[:, c, s * HALF:(s + 1) * HALF], start=c == 0, stop=c == KC - 1)
                        ins.then_inc(sign_full, 1)

            def prep_qkv(g, t, event, qk_bank):
                if t == 0:
                    pe.wait_ge(qkvlo_done, g + 1)
                if not isinstance(event, int) or event > 0:
                    pe.wait_ge(b6_free, event)
                for c in range(KC):
                    ts = slice(t * P, (t + 1) * P)
                    ins = split3(qk_bank[:, 0:GW], xnT_hi[:, c, ts], xnT_lo[:, c, ts], qkv_hi[:, c, :], qkv_lo[:, c, :],
                                 c == 0, c == KC - 1)
                ins.then_inc(qkv_full, 1)

            def prep_turn(g, t, k, ahead, turn_bank):
                tt = g * NT + t
                if k == 0:
                    pe.wait_ge(qklo_done, tt + 1)
                if not isinstance(tt, int) or tt * 2 + k > ahead:
                    pe.wait_ge(tq_taken, tt * 2 + (k - ahead))
                flat = qk_hl[:, t % 2, :, :, :].rearrange("p h a d -> p (h a d)")
                for j in range(GQ if k == 0 else 2):
                    at = j * P if k == 0 else GQ * P + j * HD
                    ins = mm(turn_bank[:, j * P:(j + 1) * P], flat[:, at:at + P], id_r[:, :], start=True, stop=True)
                ins.then_inc(tq_full, 1)

            def attend(now, now_set, steps):
                per = NT + BATCH * KC
                event = NT if isinstance(now, int) and now == 0 else now * per + (NT - LATE_W)
                if isinstance(now, int) and now == KVH:
                    event = per * KVH - LATE_W
                done6 = 0
                for late, op, i, k in steps:
                    g, a = (now - 1, 1 - now_set) if late else (now, now_set)
                    q = g * PAIRS + i
                    u = q * 5 + k
                    b = i // 2
                    if op == "S":
                        if k == 0 and i % 2 == 0:
                            pe.wait_ge(tq_taken, g * (2 * NT) + (b + 1) * NT)
                        pe.wait_ge(exp_done, u + 1)
                        for h, j, at in SCORES[k]:
                            n = (j + 1) * P
                            dst = bank[(i + k) % 2][:, at:at + n]
                            qs = qT[:, a, 2 * (i % 2) + h, b * HALF + j * P:b * HALF + (j + 1) * P]
                            mm(dst, qs, kT[:, a, 0, b * HALF:b * HALF + n], start=(h, j, at) == SCORES[k][0], stop=False)
                            mm(dst, qs, kT[:, a, 1, b * HALF:b * HALF + n], start=False, stop=False)
                        lo, moved = MASKS[k]
                        mm(bank[(i + k) % 2][:, lo:HALF], mask_b[:, :], id_b[:, moved:moved + HALF - lo], start=False,
                           stop=True).then_inc(score_full, 1)
                    elif op == "T":
                        if k in (0, 2):
                            pe.wait_ge(prob_ready, q * 2 + (1 if k == 0 else 2))
                        pe.wait_ge(plo_done, u + 1)
                        for h, j, at in TURNED[k]:
                            for r in range(j, TB):
                                ins = tr(bank[2 + (i + k) % 2][:, at + (r - j) * P:at + (r - j + 1) * P],
                                         prob[:, i % 2, h, POFF[r] + j * P:POFF[r] + (j + 1) * P])
                        ins.then_inc(pt_full, 1)
                    elif op == "A":
                        pe.wait_ge(plo_done, u + 3)
                        if k == 0:
                            pe.wait_ge(olo_done, q + 1)
                        b_ = (i + k) % 4
                        for h, j, at in TURNED[k]:
                            n = (TB - j) * P
                            dst = bank[4 + i % 2][:, j * P:j * P + n]
                            vs = slice(HD, 3 * HD) if h == 0 else slice(0, 2 * HD)
                            last = k == 4 and h == 1
                            ins = split3(dst, v_hi[:, a, b * TB + j, vs], v_lo[:, a, b * TB + j, vs], p_hi[:, b_, at:at + n],
                                         p_lo[:, b_, at:at + n], k == 0, last)
                        ins.then_inc(av_done, 1)
                    elif op == "W":
                        m = i % KC
                        b = i // KC
                        pe.wait_ge(wolo_done, g + 1)
                        pe.wait_ge(olo_done, g * PAIRS + (2 * b + 4))
                        pe.wait_ge(b6_free, event + done6)
                        done6 += 1
                        for c in range(2):
                            ins = split3(bank[6][:, :], wo_hi[:, c, m * P:(m + 1) * P], wo_lo[:, c, m * P:(m + 1) * P],
                                         o_hi[:, b, c, :], o_lo[:, b, c, :], c == 0, c == 1)
                        ins.then_inc(wo_full, 1)
                    elif op == "Q":
                        prep_qkv(g + 1, i, event + done6, bank[6])
                        done6 += 1
                    elif op == "X":
                        prep_turn(g + 1, i, k, 0, bank[7])

            pe.sem_inc(plo_done, 2)
            pe.sem_inc(olo_done, 2)
            pe.sem_inc(av_done, 4)
            pe.sem_inc(wo_full, 1)
            pe.wait_ge(mask_ready, 3)
            for op, i, k in PREP:
                if op == "Q":
                    prep_qkv(0, i, i - 2, bank[i % 3])
                elif op == "X":
                    prep_turn(0, i, k, 1, bank[7 - 4 * k])
                elif op == "F":
                    gating(i)
            pe.wait_ge(g1_ready, KC * BATCH)
            pe.wait_ge(b6_free, NT)
            pe.wait_ge(tq_taken, TAKEN_EARLY)
            attend(0, 0, schedule(False, True, True, True))
            with pe.Fori(0, KVH // 2 - 1) as gp:
                for a in range(2):
                    attend(gp * 2 + (1 + a), 1 - a, schedule(True, True, True, True))
            attend(KVH - 1, 1, schedule(True, True, True, False))
            attend(KVH, 0, schedule(True, False, False, False))
            for n in range(NT // 2):
                pe.wait_ge(sg_ready, KC * BATCH + KC * (n // (TB // 2) + 1))
                for j in range(2 * KC):
                    t, m = 2 * n + j // KC, j % KC
                    ins = tr(bank[n][:, j * P:(j + 1) * P], sT[:, m, t * P:(t + 1) * P])
                ins.then_inc(back_full, 1)


def _constants():
    import numpy as np
    p = np.arange(P)
    ident = np.eye(P)
    upto = p[:, None] <= p[None, :]
    after = p[:, None] > p[None, :]
    number = np.broadcast_to(np.arange(E), (P, E))
    consts = np.concatenate([ident, upto, after, number], 1).astype(np.float32)
    select = np.zeros((2, E, NCOMB, P), np.float32)
    for k in range(E):
        select[:, k, k, :] = 1
    for j in range(NTAIL):
        for r in range(P // TAIL):
            select[:, j * (P // TAIL) + r, E + j, r * TAIL:(r + 1) * TAIL] = 1
    freq = (1.0 / np.float32(10000.0) ** (np.arange(0, HD, 2, dtype=np.float32) / np.float32(HD))).astype(np.float32)
    angle = np.arange(SEQ, dtype=np.float32)[:, None] * freq[None, :]
    cos, sin = np.cos(angle), np.sin(angle)
    rope = np.stack([np.concatenate([cos, cos], 1), np.concatenate([-sin, sin], 1)], 1)
    rope = rope.reshape(TB, P, 2, HD).transpose(1, 0, 2, 3)
    return consts, select.reshape(2 * E, NCOMB * P), np.ascontiguousarray(rope, np.float32)


def kernel(**inputs):
    import numpy as np
    import concourse.bacc as bacc
    from concourse.bass_utils import run_bass_kernel_spmd

    a = {k: np.asarray(v) for k, v in inputs.items()}

    def by_column(v):
        return v.reshape(-1, P).T

    def rows(v):
        return np.broadcast_to(v, (P, v.shape[0]))

    consts, select, rope = _constants()
    params = np.concatenate([
        by_column(a["L0_attn_norm_scale"]),
        a["L0_attn_conv_weight"].reshape(TAPS, NCH, P).transpose(2, 1, 0).reshape(P, NCH * TAPS),
        by_column(a["L0_attn_conv_bias"]), by_column(a["L0_attn_D"]),
        rows(a["L0_attn_dt_bias"]), rows(a["L0_attn_A_log"]),
        by_column(a["L1_ffn_gamma"]), by_column(a["L1_ffn_beta"]), by_column(a["L1_ffn_bias"]), by_column(a["L1_ffn_alpha"]),
        a["L0_ffn_gate_w"].reshape(E, KC, P).transpose(2, 1, 0).reshape(P, KC * E)], 1)
    fc = [a[f"L0_ffn_fc{i}_w"].reshape(E, I, KC, P) for i in (1, 2)]
    pj = a["L0_ffn_proj_w"].transpose(0, 2, 1)

    def chunks(f, n):
        return f.reshape(n, P, KC, P).transpose(0, 3, 2, 1).reshape(n, P, C)

    cut = FULL * P
    w_moe = np.concatenate([chunks(f[:, :cut], E * FULL) for f in fc] + [pj[:, :cut].reshape(E * FULL, P, C)], 2)
    w_tail = np.concatenate([chunks(f[:, cut:], NTAIL) for f in fc] + [pj[:, cut:].reshape(NTAIL, P, C)], 2)
    wq = a["L1_attn_Wq"].reshape(KVH, GQ * HD, KC, P)
    wk, wv = (a[f"L1_attn_{n}"].reshape(KVH, HD, KC, P) for n in ("Wk", "Wv"))
    w_qkv = np.concatenate([wq, wk, wv], 1).transpose(0, 3, 2, 1)
    w_o = a["L1_attn_Wo"].reshape(C, KVH, 2, P).transpose(1, 3, 2, 0)
    sent = {
        "x": a["L0_attn_x"].reshape(T, C), "params": params, "consts": consts, "select": select, "rope": rope,
        "w_in": a["L0_attn_in_proj_w"].reshape(KC, P, PROJ).transpose(1, 0, 2),
        "w_out": a["L0_attn_out_proj_w"].reshape(NCH, P, C).transpose(1, 0, 2),
        "w_moe": w_moe, "w_moe_tail": w_tail, "w_qkv": w_qkv, "w_o": w_o,
        "w_sign": a["L1_ffn_weight"].reshape(KC, P, C).transpose(1, 0, 2),
    }
    sent = {f"in_{k}": np.ascontiguousarray(v) for k, v in sent.items()}
    nc = bacc.Bacc("TRN2", target_bir_lowering=False, num_devices=1)
    args = [nc.dram_tensor(k, v.shape, mybir.dt.from_np(v.dtype), kind="ExternalInput").ap() for k, v in sent.items()]
    args.append(nc.dram_tensor("out_x", (T, C), F32, kind="ExternalOutput").ap())
    layered_kernel(nc, *args)
    r = run_bass_kernel_spmd(nc, [sent], core_ids=[0])
    return r.results[0]["out_x"].reshape(BATCH, SEQ, C)
```
